# Optimizing a Trainium2 kernel written in Bass

```python
import numpy as np
import jax
import jax.numpy as jnp

def _softmax(x, axis=-1):
    return jax.nn.softmax(x, axis=axis)

def _gelu(x):
    return jax.nn.gelu(x, approximate=True)

def _silu(x):
    return jax.nn.silu(x)

def _sigmoid(x):
    return jax.nn.sigmoid(x)

def _layernorm(x, axis=-1, eps=1e-05):
    m = jnp.mean(x, axis=axis, keepdims=True)
    v = jnp.var(x, axis=axis, keepdims=True)
    return (x - m) / jnp.sqrt(v + eps)

def _scatter_add(tgt, idx, src, axis=0):
    return tgt.at[idx].add(src)

def _segment_sum(src, seg, n):
    return jax.ops.segment_sum(src, seg, n)
kernel_name = 'mk_seq_postln_d2_jaxref_r8_5378cc'

def setup_inputs(seed: int=0):
    np.random.seed(seed)
    _w = jnp.asarray

    def _L0_attn_setup():
        import jax, jax.numpy as jnp
        import numpy as np
        B, L = (2, 128)
        D_MODEL, D_CKV, D_CQ = (128, 32, 64)
        N_HEAD, D_HEAD, D_ROPE = (8, 64, 32)
        N_IDX_HEAD = 4
        K_TS, LW = (96, 64)
        ROPE_BASE = 10000.0

        def _pope(x, angles):
            cos, sin = (jnp.cos(angles), jnp.sin(angles))
            mu1, mu2 = jnp.split(jax.nn.softplus(x), 2, axis=-1)
            return jnp.concatenate([mu1 * cos - mu2 * sin, mu1 * sin + mu2 * cos], axis=-1)

        def _forward(x, W_dkv, W_uk, W_uv, W_dq, W_uq, W_qr, W_kr, W_out, idx_wq, idx_wk, idx_w, raw_delta):
            B_, L_, _ = x.shape
            c_kv = x @ W_dkv
            q_i = (x @ idx_wq).reshape(B_, L_, N_IDX_HEAD, D_HEAD)
            k_i = x @ idx_wk
            s_i = jax.nn.relu(jnp.einsum('bthd,bsd->bths', q_i, k_i))
            I = jnp.einsum('bths,h->bts', s_i, idx_w)
            qpos = jnp.arange(L_)[:, None]
            kpos = jnp.arange(L_)[None, :]
            local = (kpos >= qpos - LW + 1) & (kpos <= qpos)
            causal = kpos > qpos
            I = jnp.where(local[None], jnp.inf, I)
            I = jnp.where(causal[None], -jnp.inf, I)
            kk = min(K_TS, L_)
            _, idx = jax.lax.top_k(I, kk)
            bi = jnp.arange(B_)[:, None, None]
            key_c = (c_kv @ W_uk)[bi, idx].reshape(B_, L_, kk, N_HEAD, D_HEAD)
            value = (c_kv @ W_uv)[bi, idx].reshape(B_, L_, kk, N_HEAD, D_HEAD)
            c_q = x @ W_dq
            query_c = (c_q @ W_uq).reshape(B_, L_, N_HEAD, D_HEAD)
            half = D_ROPE // 2
            theta = 1.0 / ROPE_BASE ** (2.0 * jnp.arange(half, dtype=jnp.float32) / D_ROPE)
            delta = -2.0 * jnp.pi * jax.nn.sigmoid(raw_delta)
            angles_q = jnp.arange(L_, dtype=jnp.float32)[:, None] * theta[None, :] + delta
            query_r = _pope((c_q @ W_qr).reshape(B_, L_, N_HEAD, D_ROPE), angles_q[None, :, None, :])
            kr_sel = (x @ W_kr)[bi, idx]
            angles_k = jnp.arange(kk, dtype=jnp.float32)[:, None] * theta[None, :] + delta
            key_r = _pope(kr_sel, angles_k[None, None, :, :])
            scale = (D_HEAD + D_ROPE) ** (-0.5)
            q_c = query_c.transpose(0, 2, 1, 3)
            q_r = query_r.transpose(0, 2, 1, 3)
            k_c = key_c.transpose(0, 3, 1, 2, 4)
            v = value.transpose(0, 3, 1, 2, 4)
            scores = (jnp.einsum('bhld,bhlkd->bhlk', q_c, k_c) + jnp.einsum('bhld,blkd->bhlk', q_r, key_r)) * scale
            attn = jax.nn.softmax(scores.astype(jnp.float32), axis=-1).astype(v.dtype)
            out = jnp.einsum('bhlk,bhlkd->bhld', attn, v)
            out = out.transpose(0, 2, 1, 3).reshape(B_, L_, N_HEAD * D_HEAD)
            return out @ W_out
        key = jax.random.key(seed)
        ks = jax.random.split(key, 14)

        def w(k, shape, fan_in):
            return jax.random.normal(k, shape, dtype=jnp.float32) * fan_in ** (-0.5)
        return {'x': jax.random.normal(ks[0], (B, L, D_MODEL), dtype=jnp.float32), 'W_dkv': w(ks[1], (D_MODEL, D_CKV), D_MODEL), 'W_uk': w(ks[2], (D_CKV, N_HEAD * D_HEAD), D_CKV), 'W_uv': w(ks[3], (D_CKV, N_HEAD * D_HEAD), D_CKV), 'W_dq': w(ks[4], (D_MODEL, D_CQ), D_MODEL), 'W_uq': w(ks[5], (D_CQ, N_HEAD * D_HEAD), D_CQ), 'W_qr': w(ks[6], (D_CQ, N_HEAD * D_ROPE), D_CQ), 'W_kr': w(ks[7], (D_MODEL, D_ROPE), D_MODEL), 'W_out': w(ks[8], (N_HEAD * D_HEAD, D_MODEL), N_HEAD * D_HEAD), 'idx_wq': w(ks[9], (D_MODEL, N_IDX_HEAD * D_HEAD), D_MODEL), 'idx_wk': w(ks[10], (D_MODEL, D_HEAD), D_MODEL), 'idx_w': jnp.ones((N_IDX_HEAD,), dtype=jnp.float32), 'raw_delta': jax.random.normal(ks[11], (D_ROPE // 2,), dtype=jnp.float32) * 0.1}
    _L0_attn_in = _L0_attn_setup()

    def _L0_ffn_setup():
        import jax, jax.numpy as jnp
        import numpy as np
        B, T, C = (4, 256, 128)
        E = 8
        K = 2
        H = 176
        HS = 176 * 2
        key = jax.random.key(seed)
        k = jax.random.split(key, 8)
        s = 0.02
        return {'x': jax.random.normal(k[0], (B, T, C), jnp.float32), 'Wg': jax.random.normal(k[1], (C, E), jnp.float32) * s, 'W1': jax.random.normal(k[2], (E, C, H), jnp.float32) * s, 'W2': jax.random.normal(k[3], (E, C, H), jnp.float32) * s, 'W3': jax.random.normal(k[4], (E, H, C), jnp.float32) * s, 'Ws1': jax.random.normal(k[5], (C, HS), jnp.float32) * s, 'Ws2': jax.random.normal(k[6], (C, HS), jnp.float32) * s, 'Ws3': jax.random.normal(k[7], (HS, C), jnp.float32) * s}
    _L0_ffn_in = _L0_ffn_setup()

    def _L1_attn_setup():
        import jax, jax.numpy as jnp
        import numpy as np
        D = 128
        H = 16
        KVH = 4
        HD = D // H
        LAT = 32
        WIN = 32
        B, S = (1, 256)
        BASE_G, BASE_L = (1000000.0, 10000.0)
        EPS = 1e-06

        def rmsnorm(x, w):
            return x * jax.lax.rsqrt(jnp.mean(x * x, axis=-1, keepdims=True) + EPS) * w

        def qk_norm(x):
            return x * jax.lax.rsqrt(jnp.mean(x * x, axis=-1, keepdims=True) + EPS)

        def rope(x, base):
            s, hd = (x.shape[-2], x.shape[-1])
            inv_freq = 1.0 / base ** (jnp.arange(0, hd, 2, dtype=jnp.float32) / hd)
            freqs = jnp.arange(s, dtype=jnp.float32)[:, None] * inv_freq[None, :]
            cos, sin = (jnp.cos(freqs), jnp.sin(freqs))
            xe, xo = (x[..., ::2], x[..., 1::2])
            out = jnp.stack([xe * cos - xo * sin, xe * sin + xo * cos], axis=-1)
            return out.reshape(x.shape)

        def split_heads(x, n_heads):
            b, s, _ = x.shape
            return x.reshape(b, s, n_heads, HD).transpose(0, 2, 1, 3)

        def repeat_kv(x):
            return jnp.repeat(x, H // KVH, axis=1)

        def sdpa(q, k, v, mask):
            scores = jnp.einsum('bhqd,bhkd->bhqk', q, k) / np.sqrt(HD).astype(np.float32)
            scores = jnp.where(mask, scores, jnp.float32(-1e+30))
            probs = jax.nn.softmax(scores, axis=-1)
            return jnp.einsum('bhqk,bhkd->bhqd', probs, v)

        def merge_heads(x):
            b, h, s, hd = x.shape
            return x.transpose(0, 2, 1, 3).reshape(b, s, h * hd)

        def global_latent_attn(x, wq, w_kv_down, w_k_up, w_v_up, wo):
            q = split_heads(x @ wq, H)
            latent = x @ w_kv_down
            k = split_heads(latent @ w_k_up, KVH)
            v = split_heads(latent @ w_v_up, KVH)
            q, k = (rope(q, BASE_G), rope(k, BASE_G))
            q, k = (qk_norm(q), qk_norm(k))
            k, v = (repeat_kv(k), repeat_kv(v))
            i = jnp.arange(x.shape[1])
            causal = i[:, None] >= i[None, :]
            return merge_heads(sdpa(q, k, v, causal)) @ wo

        def local_gqa_attn(x, wq, wk, wv, wo):
            q = split_heads(x @ wq, H)
            k = split_heads(x @ wk, KVH)
            v = split_heads(x @ wv, KVH)
            q, k = (rope(q, BASE_L), rope(k, BASE_L))
            q, k = (qk_norm(q), qk_norm(k))
            k, v = (repeat_kv(k), repeat_kv(v))
            i = jnp.arange(x.shape[1])
            diff = i[:, None] - i[None, :]
            mask = (diff >= 0) & (diff < WIN)
            return merge_heads(sdpa(q, k, v, mask)) @ wo
        key = jax.random.key(seed)
        ks = jax.random.split(key, 12)
        std = 0.02
        return {'hidden': jax.random.normal(ks[0], (B, S, D), dtype=jnp.float32), 'norm1_w': jnp.ones((D,), jnp.float32), 'norm2_w': jnp.ones((D,), jnp.float32), 'g_wq': jax.random.normal(ks[1], (D, H * HD), jnp.float32) * std, 'g_kv_down': jax.random.normal(ks[2], (D, LAT), jnp.float32) * std, 'g_k_up': jax.random.normal(ks[3], (LAT, KVH * HD), jnp.float32) * std, 'g_v_up': jax.random.normal(ks[4], (LAT, KVH * HD), jnp.float32) * std, 'g_wo': jax.random.normal(ks[5], (D, D), jnp.float32) * std, 'l_wq': jax.random.normal(ks[6], (D, H * HD), jnp.float32) * std, 'l_wk': jax.random.normal(ks[7], (D, KVH * HD), jnp.float32) * std, 'l_wv': jax.random.normal(ks[8], (D, KVH * HD), jnp.float32) * std, 'l_wo': jax.random.normal(ks[9], (D, D), jnp.float32) * std}
    _L1_attn_in = _L1_attn_setup()

    def _L1_ffn_setup():
        import jax, jax.numpy as jnp
        import numpy as np
        B, S, D, E = (4, 512, 128, 8)
        key = jax.random.key(seed)
        ks = jax.random.split(key, 6)
        scale = 1.0 / np.sqrt(D)
        return {'tokens': jax.random.normal(ks[0], (B, S, D), dtype=jnp.float32), 'gate_w': jax.random.normal(ks[1], (D, E), dtype=jnp.float32) * scale, 'w0': jax.random.normal(ks[2], (D, D), dtype=jnp.float32) * scale, 'b0': jax.random.normal(ks[3], (D,), dtype=jnp.float32) * 0.01, 'w1': jax.random.normal(ks[4], (D, D), dtype=jnp.float32) * scale, 'b1': jax.random.normal(ks[5], (D,), dtype=jnp.float32) * 0.01}
    _L1_ffn_in = _L1_ffn_setup()
    _d = {'L0_attn_x': _L0_attn_in['x'], 'L0_attn_W_dkv': _L0_attn_in['W_dkv'], 'L0_attn_W_uk': _L0_attn_in['W_uk'], 'L0_attn_W_uv': _L0_attn_in['W_uv'], 'L0_attn_W_dq': _L0_attn_in['W_dq'], 'L0_attn_W_uq': _L0_attn_in['W_uq'], 'L0_attn_W_qr': _L0_attn_in['W_qr'], 'L0_attn_W_kr': _L0_attn_in['W_kr'], 'L0_attn_W_out': _L0_attn_in['W_out'], 'L0_attn_idx_wq': _L0_attn_in['idx_wq'], 'L0_attn_idx_wk': _L0_attn_in['idx_wk'], 'L0_attn_idx_w': _L0_attn_in['idx_w'], 'L0_attn_raw_delta': _L0_attn_in['raw_delta'], 'L0_ffn_Wg': _L0_ffn_in['Wg'], 'L0_ffn_W1': _L0_ffn_in['W1'], 'L0_ffn_W2': _L0_ffn_in['W2'], 'L0_ffn_W3': _L0_ffn_in['W3'], 'L0_ffn_Ws1': _L0_ffn_in['Ws1'], 'L0_ffn_Ws2': _L0_ffn_in['Ws2'], 'L0_ffn_Ws3': _L0_ffn_in['Ws3'], 'L1_attn_norm1_w': _L1_attn_in['norm1_w'], 'L1_attn_norm2_w': _L1_attn_in['norm2_w'], 'L1_attn_g_wq': _L1_attn_in['g_wq'], 'L1_attn_g_kv_down': _L1_attn_in['g_kv_down'], 'L1_attn_g_k_up': _L1_attn_in['g_k_up'], 'L1_attn_g_v_up': _L1_attn_in['g_v_up'], 'L1_attn_g_wo': _L1_attn_in['g_wo'], 'L1_attn_l_wq': _L1_attn_in['l_wq'], 'L1_attn_l_wk': _L1_attn_in['l_wk'], 'L1_attn_l_wv': _L1_attn_in['l_wv'], 'L1_attn_l_wo': _L1_attn_in['l_wo'], 'L1_ffn_gate_w': _L1_ffn_in['gate_w'], 'L1_ffn_w0': _L1_ffn_in['w0'], 'L1_ffn_b0': _L1_ffn_in['b0'], 'L1_ffn_w1': _L1_ffn_in['w1'], 'L1_ffn_b1': _L1_ffn_in['b1']}
    _x0 = _d['L0_attn_x']
    _d['L0_attn_x'] = jax.random.normal(jax.random.fold_in(jax.random.key(seed), 1), (8, 256, 128), dtype=_x0.dtype)
    del _x0
    return _d

def reference(L0_attn_x, L0_attn_W_dkv, L0_attn_W_uk, L0_attn_W_uv, L0_attn_W_dq, L0_attn_W_uq, L0_attn_W_qr, L0_attn_W_kr, L0_attn_W_out, L0_attn_idx_wq, L0_attn_idx_wk, L0_attn_idx_w, L0_attn_raw_delta, L0_ffn_Wg, L0_ffn_W1, L0_ffn_W2, L0_ffn_W3, L0_ffn_Ws1, L0_ffn_Ws2, L0_ffn_Ws3, L1_attn_norm1_w, L1_attn_norm2_w, L1_attn_g_wq, L1_attn_g_kv_down, L1_attn_g_k_up, L1_attn_g_v_up, L1_attn_g_wo, L1_attn_l_wq, L1_attn_l_wk, L1_attn_l_wv, L1_attn_l_wo, L1_ffn_gate_w, L1_ffn_w0, L1_ffn_b0, L1_ffn_w1, L1_ffn_b1):

    def _L0_attn_ref(x, W_dkv, W_uk, W_uv, W_dq, W_uq, W_qr, W_kr, W_out, idx_wq, idx_wk, idx_w, raw_delta):
        import jax, jax.numpy as jnp
        import numpy as np
        B, L = (2, 128)
        D_MODEL, D_CKV, D_CQ = (128, 32, 64)
        N_HEAD, D_HEAD, D_ROPE = (8, 64, 32)
        N_IDX_HEAD = 4
        K_TS, LW = (96, 64)
        ROPE_BASE = 10000.0

        def _pope(x, angles):
            cos, sin = (jnp.cos(angles), jnp.sin(angles))
            mu1, mu2 = jnp.split(jax.nn.softplus(x), 2, axis=-1)
            return jnp.concatenate([mu1 * cos - mu2 * sin, mu1 * sin + mu2 * cos], axis=-1)

        def _forward(x, W_dkv, W_uk, W_uv, W_dq, W_uq, W_qr, W_kr, W_out, idx_wq, idx_wk, idx_w, raw_delta):
            B_, L_, _ = x.shape
            c_kv = x @ W_dkv
            q_i = (x @ idx_wq).reshape(B_, L_, N_IDX_HEAD, D_HEAD)
            k_i = x @ idx_wk
            s_i = jax.nn.relu(jnp.einsum('bthd,bsd->bths', q_i, k_i))
            I = jnp.einsum('bths,h->bts', s_i, idx_w)
            qpos = jnp.arange(L_)[:, None]
            kpos = jnp.arange(L_)[None, :]
            local = (kpos >= qpos - LW + 1) & (kpos <= qpos)
            causal = kpos > qpos
            I = jnp.where(local[None], jnp.inf, I)
            I = jnp.where(causal[None], -jnp.inf, I)
            kk = min(K_TS, L_)
            _, idx = jax.lax.top_k(I, kk)
            bi = jnp.arange(B_)[:, None, None]
            key_c = (c_kv @ W_uk)[bi, idx].reshape(B_, L_, kk, N_HEAD, D_HEAD)
            value = (c_kv @ W_uv)[bi, idx].reshape(B_, L_, kk, N_HEAD, D_HEAD)
            c_q = x @ W_dq
            query_c = (c_q @ W_uq).reshape(B_, L_, N_HEAD, D_HEAD)
            half = D_ROPE // 2
            theta = 1.0 / ROPE_BASE ** (2.0 * jnp.arange(half, dtype=jnp.float32) / D_ROPE)
            delta = -2.0 * jnp.pi * jax.nn.sigmoid(raw_delta)
            angles_q = jnp.arange(L_, dtype=jnp.float32)[:, None] * theta[None, :] + delta
            query_r = _pope((c_q @ W_qr).reshape(B_, L_, N_HEAD, D_ROPE), angles_q[None, :, None, :])
            kr_sel = (x @ W_kr)[bi, idx]
            angles_k = jnp.arange(kk, dtype=jnp.float32)[:, None] * theta[None, :] + delta
            key_r = _pope(kr_sel, angles_k[None, None, :, :])
            scale = (D_HEAD + D_ROPE) ** (-0.5)
            q_c = query_c.transpose(0, 2, 1, 3)
            q_r = query_r.transpose(0, 2, 1, 3)
            k_c = key_c.transpose(0, 3, 1, 2, 4)
            v = value.transpose(0, 3, 1, 2, 4)
            scores = (jnp.einsum('bhld,bhlkd->bhlk', q_c, k_c) + jnp.einsum('bhld,blkd->bhlk', q_r, key_r)) * scale
            attn = jax.nn.softmax(scores.astype(jnp.float32), axis=-1).astype(v.dtype)
            out = jnp.einsum('bhlk,bhlkd->bhld', attn, v)
            out = out.transpose(0, 2, 1, 3).reshape(B_, L_, N_HEAD * D_HEAD)
            return out @ W_out
        return _forward(x, W_dkv, W_uk, W_uv, W_dq, W_uq, W_qr, W_kr, W_out, idx_wq, idx_wk, idx_w, raw_delta)

    def _L0_ffn_ref(x, Wg, W1, W2, W3, Ws1, Ws2, Ws3):
        import jax, jax.numpy as jnp
        import numpy as np
        B, T, C = (4, 256, 128)
        E = 8
        K = 2
        H = 176
        HS = 176 * 2
        b, t, c = x.shape
        xf = x.reshape(-1, c)
        n = xf.shape[0]
        router = xf @ Wg
        top_logits, idx = jax.lax.top_k(router, K)
        probs = jax.nn.softmax(top_logits.astype(jnp.float32), axis=-1).astype(x.dtype)
        w = jnp.zeros((n, E), x.dtype).at[jnp.arange(n)[:, None], idx].add(probs)
        h = jax.nn.silu(jnp.einsum('tc,ech->eth', xf, W1)) * jnp.einsum('tc,ech->eth', xf, W2)
        y = jnp.einsum('eth,ehc,te->tc', h, W3, w)
        y = y.reshape(b, t, c)
        hs = jax.nn.silu(xf @ Ws1) * (xf @ Ws2)
        y = y + (hs @ Ws3).reshape(b, t, c)
        return y

    def _L1_attn_ref(hidden, norm1_w, norm2_w, g_wq, g_kv_down, g_k_up, g_v_up, g_wo, l_wq, l_wk, l_wv, l_wo):
        import jax, jax.numpy as jnp
        import numpy as np
        D = 128
        H = 16
        KVH = 4
        HD = D // H
        LAT = 32
        WIN = 32
        B, S = (1, 256)
        BASE_G, BASE_L = (1000000.0, 10000.0)
        EPS = 1e-06

        def rmsnorm(x, w):
            return x * jax.lax.rsqrt(jnp.mean(x * x, axis=-1, keepdims=True) + EPS) * w

        def qk_norm(x):
            return x * jax.lax.rsqrt(jnp.mean(x * x, axis=-1, keepdims=True) + EPS)

        def rope(x, base):
            s, hd = (x.shape[-2], x.shape[-1])
            inv_freq = 1.0 / base ** (jnp.arange(0, hd, 2, dtype=jnp.float32) / hd)
            freqs = jnp.arange(s, dtype=jnp.float32)[:, None] * inv_freq[None, :]
            cos, sin = (jnp.cos(freqs), jnp.sin(freqs))
            xe, xo = (x[..., ::2], x[..., 1::2])
            out = jnp.stack([xe * cos - xo * sin, xe * sin + xo * cos], axis=-1)
            return out.reshape(x.shape)

        def split_heads(x, n_heads):
            b, s, _ = x.shape
            return x.reshape(b, s, n_heads, HD).transpose(0, 2, 1, 3)

        def repeat_kv(x):
            return jnp.repeat(x, H // KVH, axis=1)

        def sdpa(q, k, v, mask):
            scores = jnp.einsum('bhqd,bhkd->bhqk', q, k) / np.sqrt(HD).astype(np.float32)
            scores = jnp.where(mask, scores, jnp.float32(-1e+30))
            probs = jax.nn.softmax(scores, axis=-1)
            return jnp.einsum('bhqk,bhkd->bhqd', probs, v)

        def merge_heads(x):
            b, h, s, hd = x.shape
            return x.transpose(0, 2, 1, 3).reshape(b, s, h * hd)

        def global_latent_attn(x, wq, w_kv_down, w_k_up, w_v_up, wo):
            q = split_heads(x @ wq, H)
            latent = x @ w_kv_down
            k = split_heads(latent @ w_k_up, KVH)
            v = split_heads(latent @ w_v_up, KVH)
            q, k = (rope(q, BASE_G), rope(k, BASE_G))
            q, k = (qk_norm(q), qk_norm(k))
            k, v = (repeat_kv(k), repeat_kv(v))
            i = jnp.arange(x.shape[1])
            causal = i[:, None] >= i[None, :]
            return merge_heads(sdpa(q, k, v, causal)) @ wo

        def local_gqa_attn(x, wq, wk, wv, wo):
            q = split_heads(x @ wq, H)
            k = split_heads(x @ wk, KVH)
            v = split_heads(x @ wv, KVH)
            q, k = (rope(q, BASE_L), rope(k, BASE_L))
            q, k = (qk_norm(q), qk_norm(k))
            k, v = (repeat_kv(k), repeat_kv(v))
            i = jnp.arange(x.shape[1])
            diff = i[:, None] - i[None, :]
            mask = (diff >= 0) & (diff < WIN)
            return merge_heads(sdpa(q, k, v, mask)) @ wo
        x = hidden
        x = x + global_latent_attn(rmsnorm(x, norm1_w), g_wq, g_kv_down, g_k_up, g_v_up, g_wo)
        x = x + local_gqa_attn(rmsnorm(x, norm2_w), l_wq, l_wk, l_wv, l_wo)
        return x

    def _L1_ffn_ref(tokens, gate_w, w0, b0, w1, b1):
        import jax, jax.numpy as jnp
        import numpy as np
        B, S, D, E = (4, 512, 128, 8)
        b, s, d = tokens.shape
        logits = jnp.einsum('bsd,de->bse', tokens, gate_w)
        weights = jax.nn.softmax(logits, axis=-1)
        topk_w, topk_idx = jax.lax.top_k(weights, 2)
        x = tokens.reshape(b * s, d)
        fw = topk_w.reshape(b * s, 2)
        fidx = topk_idx.reshape(b * s, 2)
        e0 = jax.nn.silu(x @ w0.T + b0)
        e1 = jax.nn.silu(x @ w1.T + b1)
        m0 = (fidx[:, 0:1] == 0).astype(x.dtype)
        m1 = (fidx[:, 1:2] == 1).astype(x.dtype)
        out = e0 * fw[:, 0:1] * m0 + e1 * fw[:, 1:2] * m1
        return out.reshape(b, s, d)
    x = L0_attn_x
    x = _layernorm(x + _L0_attn_ref(x, L0_attn_W_dkv, L0_attn_W_uk, L0_attn_W_uv, L0_attn_W_dq, L0_attn_W_uq, L0_attn_W_qr, L0_attn_W_kr, L0_attn_W_out, L0_attn_idx_wq, L0_attn_idx_wk, L0_attn_idx_w, L0_attn_raw_delta), axis=-1)
    x = _layernorm(x + _L0_ffn_ref(x, L0_ffn_Wg, L0_ffn_W1, L0_ffn_W2, L0_ffn_W3, L0_ffn_Ws1, L0_ffn_Ws2, L0_ffn_Ws3), axis=-1)
    x = _layernorm(x + _L1_attn_ref(x, L1_attn_norm1_w, L1_attn_norm2_w, L1_attn_g_wq, L1_attn_g_kv_down, L1_attn_g_k_up, L1_attn_g_v_up, L1_attn_g_wo, L1_attn_l_wq, L1_attn_l_wk, L1_attn_l_wv, L1_attn_l_wo), axis=-1)
    x = _layernorm(x + _L1_ffn_ref(x, L1_ffn_gate_w, L1_ffn_w0, L1_ffn_b0, L1_ffn_w1, L1_ffn_b1), axis=-1)
    return x

_drawn_inputs = setup_inputs


def setup_inputs(seed=0):
    import zlib

    import numpy as np

    out = dict(_drawn_inputs(seed))
    spreads = {'L0_attn_idx_w': (1.0, 0.2), 'L1_attn_norm1_w': (1.0, 0.6), 'L1_attn_norm2_w': (1.0, 0.6)}
    factors = {'L0_attn_raw_delta': 64.0,
     'L0_ffn_Wg': 6.431,
     'L0_ffn_W1': 6.554,
     'L0_ffn_W2': 6.363,
     'L0_ffn_W3': 7.326,
     'L0_ffn_Ws1': 3.962,
     'L0_ffn_Ws2': 4.284,
     'L0_ffn_Ws3': 3.973,
     'L1_attn_g_wq': 8.0,
     'L1_attn_g_kv_down': 8.0,
     'L1_attn_g_k_up': 8.0,
     'L1_attn_g_v_up': 8.0,
     'L1_attn_g_wo': 8.0,
     'L1_attn_l_wq': 6.219,
     'L1_attn_l_wk': 6.398,
     'L1_attn_l_wv': 4.421,
     'L1_attn_l_wo': 4.603,
     'L1_ffn_b0': 51.035,
     'L1_ffn_b1': 64.0}
    for name, (base, spread) in spreads.items():
        noise = np.random.default_rng([zlib.crc32(name.encode()), seed]).standard_normal(out[name].shape)
        drawn = base * np.exp(spread * noise) if base else spread * noise
        out[name] = jnp.asarray(drawn.astype(out[name].dtype))
    for name, factor in factors.items():
        out[name] = (out[name] * factor).astype(out[name].dtype)
    return out
```

```python
import numpy as np
import concourse.bass as bass
from concourse import mybir
from concourse.alu_op_type import AluOpType as ALU
from contextlib import ExitStack

NB, S, D = 8, 256, 128
P = 128
NT = S // P
H0, DH0, LAT, CQ, ROPE = 8, 64, 32, 64, 32
NI, DI = 4, 64
TOPK, WIN0 = 96, 64
NR = TOPK - WIN0
FE = 2 * ROPE + LAT
UQ = 16
NU = S // UQ
AW = WIN0 + UQ
BW = 4 * NR
J0, J1 = TOPK, S - WIN0
E, HE, HS, BLK = 8, 176, 352, 88
NBLK = (E * HE + HS) // BLK
H1, KV, HD, WIN1 = 16, 4, 8, 32
GH = H1 // KV
NQK = (H1 + KV) * HD
NPJ = 2 * NQK + KV * HD
FAR, GONE = -1e30, -3e38
FN = ROPE + LAT
ANG = 2 * S + NR


def constants():
    p = np.arange(P)
    cols = {}
    cols["ident"] = np.eye(P)
    quad, qi = p // 32, p % 4
    dq = 4 * quad + qi
    jj = np.arange(AW)
    own = np.where(np.arange(BW)[None] // NR == qi[:, None], 0.0, FAR)
    first = np.where(np.broadcast_to(jj[None] < WIN0, (P, AW)), 0.0, FAR)
    later = np.where((jj[None] >= 1 + dq[:, None]) & (jj[None] <= WIN0 + dq[:, None]), 0.0, FAR)
    cols["mask_first"] = np.concatenate([first, own], 1)
    cols["mask_later"] = np.concatenate([later, own], 1)
    for t, n in ((0, J0), (1, J1)):
        q, j = (t * P + p)[:, None], np.arange(n)[None]
        m = np.where(j > np.maximum(q, WIN0 - 1), FAR * (1 + j / 256.0), GONE)
        cols[f"mask_rank{t}"] = np.where(j <= q - WIN0, 0.0, m)
    cols["iota"] = np.stack([p, p + P], 1)
    cols["causal"] = (p[None] >= p[:, None]) * 1.0
    diff = p[None] - p[:, None]
    cols["local"] = ((diff >= 0) & (diff < WIN1)) * 1.0
    cols["seam"] = np.where(p[:, None] >= P - WIN1, (p[:, None] - (P - WIN1)) > np.arange(WIN1)[None], 0) * 1.0
    cols["headsel"] = (p[:, None] // HD % GH == np.arange(GH)[None]) * 1.0
    cols["before"] = np.tile((np.arange(E)[None] < np.arange(E)[:, None]).reshape(1, -1), (P, 1)) * 1.0
    cols["power"] = np.full((P, 2 * (H1 + KV)), -0.5)
    pos = np.arange(S).reshape(NT, P).T
    for name, base in (("g", 1e6), ("l", 1e4)):
        f = (1.0 / np.float32(base) ** (np.arange(0, HD, 2, dtype=np.float32) / HD)).astype(np.float32)
        a = (pos[:, :, None].astype(np.float32) * f).astype(np.float64)
        c, s = np.cos(a), np.sin(a)
        cols[f"cos_{name}"] = np.stack([c, c], -1).reshape(P, -1)
        cols[f"sin_{name}"] = np.stack([-s, s], -1).reshape(P, -1)
    half = ROPE // 2
    theta = (1.0 / np.float32(10000.0) ** (2.0 * np.arange(half, dtype=np.float32) / ROPE)).astype(np.float32)
    q = np.arange(S)
    near = np.where(q < WIN0, q, 2 * q - (WIN0 - 1))
    at = np.concatenate([near, q, np.arange(WIN0, TOPK)]).astype(np.float32)
    a = (theta[:, None] * at[None]).astype(np.float64)
    a = np.concatenate([a, a])
    sign = np.where(np.arange(ROPE) < half, -1.0, 1.0)[:, None]
    u = np.concatenate([np.cos(a), sign * np.sin(a)])
    v = np.concatenate([-np.sin(a), sign * np.cos(a)])
    where, at = {}, 0
    for k, c in cols.items():
        where[k] = (at, at + c.shape[1])
        at += c.shape[1]
    return np.concatenate(list(cols.values()), 1).astype(np.float32), where, np.stack([u, v]).astype(np.float32)


def layers(nc, x, consts, w, out, where, stop=4):
    F, BF, U32 = mybir.dt.float32, mybir.dt.bfloat16, mybir.dt.uint32
    ACT, AX = mybir.ActivationFunctionType, mybir.AxisListType
    ctx = ExitStack()
    with ctx:
        def sb(name, shape, dt=F):
            return ctx.enter_context(nc.sbuf_tensor(name, shape, dt))

        def sem(name):
            return ctx.enter_context(nc.semaphore(name))

        cst = sb("cst", [P, consts.shape[1]])

        def c(name, rows=P):
            return cst[0:rows, where[name][0]:where[name][1]]

        ident = c("ident")
        x_next = sb("x_next", [P, NT, D])
        hid = sb("hid", [P, NBLK, S])
        spare = hid[:].rearrange("p b s -> p (b s)")
        spare_at = [0]

        def early(rows, a, b):
            lo = spare_at[0]
            spare_at[0] += a * b
            return spare[0:rows, lo:lo + a * b].rearrange("p (a b) -> p a b", a=a)

        w_dqT = sb("w_dqT", [CQ, D])
        w_uqT = early(DH0, H0, CQ)
        w_ukT = early(DH0, H0, LAT)
        w_uvT = early(DH0, H0, LAT)
        w_out = early(DH0, H0, D)
        w_up3 = early(CQ, H0, FN)
        turn_u = early(2 * ROPE, 1, ANG)[:, 0, :]
        turn_v = early(2 * ROPE, 1, ANG)[:, 0, :]
        w_key = sb("w_key", [D, 2 * ROPE + LAT])
        idx_wq = sb("idx_wq", [D, NI * DI])
        idx_wk = sb("idx_wk", [D, 2 * DI])
        idx_w = sb("idx_w", [P, NI])
        raw_delta = sb("raw_delta", [2 * ROPE, 1])
        wg = sb("wg", [D, E])
        w1 = sb("w1", [D, NBLK, BLK])
        w2 = sb("w2", [D, NBLK, BLK])
        w3 = sb("w3", [BLK, NBLK, D])
        norm_w = sb("norm_w", [D, 2])
        wpj = sb("wpj", [D, 2, NPJ])
        kv_downT = sb("kv_downT", [LAT, D])
        kv_up = sb("kv_up", [LAT, 3 * KV * HD])
        wo = sb("wo", [D, 2, D])
        gate_w = sb("gate_w", [D, E])
        w01 = sb("w01", [D, 2 * D])
        b01 = sb("b01", [1, 2 * D])
        wq3 = sb("wq3", [D, H0, FN])
        wvo = sb("wvo", [LAT, H0, D])
        turn = sb("turn", [2 * ROPE, ANG])
        rank_turn = sb("rank_turn", [FE, NR])
        turns_t = sb("turns_t", [P, 2, NT, 2 * ROPE])
        dlt = sb("dlt", [2 * ROPE, 6])
        ones_row = sb("ones_row", [1, P])
        xa = sb("xa", [P, NT, D])
        xaT = sb("xaT", [D, S])
        idxT = sb("idxT", [P, 3, S])
        relu_i = sb("relu_i", [P, 2, 2, J1])
        rank_in = sb("rank_in", [P, NT, J1])
        top = sb("top", [P, NR])
        idx_u = sb("idx_u", [P, NT, NR], U32)
        idx_b = sb("idx_b", [P, NT, NR], BF)
        idx_rows = sb("idx_rows", [P, NT, P * NR], BF)
        hot_low = sb("hot_low", [P, P * NR], BF)
        k_low = sb("k_low", [P, NT, 2 * ROPE])
        k_exp = sb("k_exp", [P, NT, 2 * ROPE])
        k_log = sb("k_log", [P, NT, 2 * ROPE])
        k_feat = sb("k_feat", [P, NT, FE])
        k_mul = sb("k_mul", [P, NT, 2 * ROPE])
        k_rot = sb("k_rot", [P, NT, FN])
        k_rest = sb("k_rest", [P, 2, NT, FE])
        k_split = sb("k_split", [P, 3, NT, FE], BF)
        keysT = sb("keysT", [FN, S])
        q_low = sb("q_low", [P, NT, H0, ROPE])
        q_turn = sb("q_turn", [P, 2, NT, H0, ROPE])
        q_near_t = sb("q_near_t", [P, NT, H0, FN])
        q_far_t = sb("q_far_t", [P, NT, H0, FE])
        q_near = sb("q_near", [FN, NU, P])
        q_far = sb("q_far", [FE, NU, P])
        lat_win = sb("lat_win", [AW, NU, LAT])
        got = sb("got", [FE, 2, 4, BW])
        sc = sb("sc", [P, AW + BW])
        top_s = sb("top_s", [P, 1])
        neg_top = sb("neg_top", [P, 1])
        probs = sb("probs", [P, AW + BW])
        total = sb("total", [P, 1])
        inv_total = sb("inv_total", [P, 1])
        probsT = sb("probsT", [P, 3, P])
        headsT = sb("headsT", [LAT, H0, S])
        pre = sb("pre", [P, NT, D])
        st6 = sb("st6", [P, NT, 6])
        mv = sb("mv", [P, NT, 2])
        var_e = sb("var_e", [P, NT])
        rstd = sb("rstd", [P, NT])
        x1 = sb("x1", [P, NT, D])
        xbT = sb("xbT", [D, S])
        lg = sb("lg", [P, NT, E])
        gt = sb("gt", [P, NT, E, E])
        eq = sb("eq", [P, NT, E, E])
        rank = sb("rank", [P, 4, NT, E])
        small = sb("small", [P, 8, NT])
        egate = sb("egate", [P, 3, NT, E])
        th = sb("th", [BLK, 2, 2, S])
        preb = sb("preb", [P, NT, D])
        x2 = sb("x2", [P, NT, D])
        sqx = sb("sqx", [P, D])
        ssx = sb("ssx", [P, NT])
        msx = sb("msx", [P, NT])
        rsx = sb("rsx", [P, NT])
        pj = sb("pj", [P, NT, NPJ])
        ssh = sb("ssh", [P, NT, H1 + KV])
        rsh = sb("rsh", [P, NT, H1 + KV])
        ro = sb("ro", [P, 2, NT, NQK])
        qn = sb("qn", [P, NT, H1 * HD])
        kn = sb("kn", [P, NT, KV, GH, HD])
        qT = sb("qT", [P, S])
        kbig = sb("kbig", [P, GH, S])
        v1 = sb("v1", [P, NT, KV, HD + 1])
        pr0 = sb("pr0", [P, 2, GH, S])
        pr1 = sb("pr1", [P, 2, GH, P])
        prs = sb("prs", [P, H1, WIN1])
        inv_l = sb("inv_l", [P, NT, H1])
        att = sb("att", [P, NT, D])
        attT = sb("attT", [D, S])
        x3 = sb("x3", [P, 2, NT, D])
        e01 = sb("e01", [P, 1, NT, 2 * D])
        fin = sb("fin", [P, NT, D])

        pa = ctx.enter_context(nc.psum_tensor("pa", [P, 4, 512], F))
        pb = ctx.enter_context(nc.psum_tensor("pb", [P, 4, 512], F))

        idx_dram = nc.dram_tensor("idx_dram", [NT, P * NR], BF, kind="Internal").ap()

        class Signal:
            def __init__(self, name, per_run):
                self.sem, self.n = sem(name), per_run

            def at(self, r, k=None):
                return r * self.n + (self.n if k is None else k)

        loaded = sem("loaded")
        derived_pe = sem("derived_pe")
        derived_act = sem("derived_act")
        derived_dve = sem("derived_dve")
        N = {}

        def signal(name, n):
            N[name] = Signal(name, n)
            return N[name]

        fin_free = sem("fin_free")
        x_free = sem("x_free")
        x_ok = signal("x_ok", 16)
        x_in = signal("x_in", 1)
        xaT_ps = signal("xaT_ps", 1)
        xaT_ok = signal("xaT_ok", 1)
        idx_ps = signal("idx_ps", 1)
        idxT_ok = signal("idxT_ok", 1)
        is_ps = signal("is_ps", 2)
        relu_ok = signal("relu_ok", 2)
        rin_ok = signal("rin_ok", 2)
        ib_ok = signal("ib_ok", 1)
        iw_ok = signal("iw_ok", 16)
        ir_ok = signal("ir_ok", 32)
        hot_ok = signal("hot_ok", 2)
        key_ps = signal("key_ps", 1)
        klow_ok = signal("klow_ok", 1)
        klog_ok = signal("klog_ok", 1)
        klat_ok = signal("klat_ok", 1)
        krot_ok = signal("krot_ok", 1)
        ksplit_ok = signal("ksplit_ok", 1)
        keyT_ps = signal("keyT_ps", 1)
        keysT_ok = signal("keysT_ok", 1)
        q_ps = signal("q_ps", 1)
        qlow_ok = signal("qlow_ok", 1)
        qlog_ok = signal("qlog_ok", 1)
        qT0_ps = signal("qT0_ps", 8)
        qT0_ok = signal("qT0_ok", 8)
        qf_ok = signal("qf_ok", 1)
        win_ps = signal("win_ps", 1)
        win_ok = signal("win_ok", 1)
        got_ps = signal("got_ps", NU)
        got_ok = signal("got_ok", NU)
        sc_ps = signal("sc_ps", NU)
        sc_ok = signal("sc_ok", NU)
        pr_e = signal("pr_e", NU)
        pr_ok = signal("pr_ok", NU)
        pt_ps = signal("pt_ps", NU)
        pt_ok = signal("pt_ok", NU)
        o_ps = signal("o_ps", NU)
        o_ok = signal("o_ok", 4)
        y_ps = signal("y_ps", 1)
        a_var = signal("a_var", 1)
        a_rstd = signal("a_rstd", 1)
        x1_ok = signal("x1_ok", 1)
        r_ps = signal("r_ps", 1)
        xbT_ok = signal("xbT_ok", 1)
        lg_ps = signal("lg_ps", 1)
        sh_ok = signal("sh_ok", 1)
        eg_ok = signal("eg_ok", 1)
        up_ps = signal("up_ps", NBLK // 2)
        th_ok = signal("th_ok", NBLK // 2)
        hid_ok = signal("hid_ok", NBLK // 2)
        dn_ps = signal("dn_ps", 5)
        dn_ok = signal("dn_ok", 5)
        b_var = signal("b_var", 1)
        b_rstd = signal("b_rstd", 1)
        x2_ok = signal("x2_ok", 1)
        tx_ps = signal("tx_ps", 2)
        tx_ok = signal("tx_ok", 2)
        ms_ok = signal("ms_ok", 2)
        rs_ok = signal("rs_ok", 2)
        pj_ps = signal("pj_ps", 2)
        pj_ok = signal("pj_ok", 2)
        mh_ok = signal("mh_ok", 2)
        rh_ok = signal("rh_ok", 2)
        qk_ok = signal("qk_ok", 2)
        qkT_ps = signal("qkT_ps", 2)
        qT_ok = signal("qT_ok", 2)
        kb_ok = signal("kb_ok", 2)
        s_ps = signal("s_ps", 2 * KV)
        e_ok = signal("e_ok", 2 * KV)
        m_ok = signal("m_ok", 2 * KV)
        seam_ps = signal("seam_ps", 1)
        seam_e = signal("seam_e", 1)
        seam_ok = signal("seam_ok", 1)
        pv_ps = signal("pv_ps", 2 * KV)
        att_ok = signal("att_ok", 2)
        aT_ps = signal("aT_ps", 2)
        aT_ok = signal("aT_ok", 2)
        wo_ps = signal("wo_ps", 2)
        x3_ok = signal("x3_ok", 2)
        c_var = signal("c_var", 1)
        c_rstd = signal("c_rstd", 1)
        x4_ok = signal("x4_ok", 1)
        t4_ps = signal("t4_ps", 1)
        t4_ok = signal("t4_ok", 1)
        f_ps = signal("f_ps", 1)
        fth_ok = signal("fth_ok", 1)
        fsh_ok = signal("fsh_ok", 1)
        feg_ok = signal("feg_ok", 1)
        d_var = signal("d_var", 1)
        d_rstd = signal("d_rstd", 1)
        fin_ok = signal("fin_ok", 1)
        out_ok = signal("out_ok", 16)
        chain_a = signal("chain_a", CHAIN_A)
        chain_b = signal("chain_b", CHAIN_B)
        act_a = signal("act_a", 2)
        pool_b = signal("pool_b", 4)
        ready = sem("ready")

        def bc(ap, shape):
            return ap.to_broadcast(shape) if False else ap.broadcast_to(shape)

        xv = x.rearrange("b (t p) d -> b p t d", p=P)
        ov = out.rearrange("b (t p) d -> b p t d", p=P)
        loads = []

        def plan(dst, src):
            loads.append((dst, src))

        plan(cst[:], consts)
        plan(turn_u, w["turns"][0])
        plan(turn_v, w["turns"][1])
        plan(w_dqT[:], w["w_dqT"])
        plan(w_uqT, w["w_uqT"])
        plan(w_ukT, w["w_ukT"])
        plan(w_uvT, w["w_uvT"])
        plan(w_out, w["w_out"])
        plan(w_up3, w["w_up3"])
        plan(w_key[:], w["w_key"])
        plan(idx_wq[:], w["idx_wq"])
        plan(idx_wk[:, 0:DI], w["idx_wk"])
        plan(idx_wk[:, DI:2 * DI], w["idx_wk"])
        plan(idx_w[:], w["idx_w"].rearrange("(a n) -> a n", a=1).broadcast_to([P, NI]))
        for k in range(4):
            plan(raw_delta[16 * k:16 * k + 16, :], w["raw_delta"].rearrange("(n a) -> n a", a=1))
        plan(wg[:], w["wg"])
        plan(w1[:], w["w1"])
        plan(w2[:], w["w2"])
        plan(w3[:], w["w3"])
        plan(norm_w[:], w["norm_w"])
        plan(wpj[:], w["wpj"])
        plan(kv_downT[:], w["kv_downT"])
        plan(kv_up[:], w["kv_up"])
        plan(wo[:], w["wo"])
        plan(gate_w[:], w["gate_w"])
        plan(w01[:], w["w01"])
        plan(b01[:], w["b01"])
        ALL = 16 * len(loads)

        passed = sem("passed")

        def plain(eng):
            eng.sem_inc(passed, 1)

        def ws(u):
            return max(0, UQ * u - WIN0)

        nc.disable_value_cache = True
        block = ctx.enter_context(nc.Block())

        @block.sync
        def _(sp):
            for dst, src in loads:
                sp.dma_start(dst, src).then_inc(loaded, 16)
            with nc.sync.Fori(0, NB) as r:
                sp.wait_ge(x_free, r + 1)
                sp.dma_start(x_next[:], xv[bass.ds(r, 1)].rearrange("a p t d -> (a p) t d")).then_inc(x_ok.sem, 16)
                sp.wait_ge(ib_ok.sem, ib_ok.at(r))
                sp.dma_start(idx_dram.rearrange("t (p n) -> p t n", p=P), idx_b[:]).then_inc(iw_ok.sem, 16)
                sp.wait_ge(iw_ok.sem, iw_ok.at(r))
                sp.dma_start(idx_rows[0:J0, 0, :], idx_dram[0:1, :].broadcast_to([J0, P * NR])).then_inc(ir_ok.sem, 16)
                sp.dma_start(idx_rows[:, 1, :], idx_dram[1:2, :].broadcast_to([P, P * NR])).then_inc(ir_ok.sem, 16)
            sp.wait_ge(out_ok.sem, 16 * NB)

        @block.gpsimd
        def _(pool):
            pool.wait_ge(loaded, ALL)

            def rsqrt(dst, src, n):
                return nc.gpsimd.tensor_tensor(dst, src, c("power")[:, 0:n], ALU.pow)

            def attention0(r):
                pool.wait_ge(x_ok.sem, x_ok.at(r))
                plain(pool)
                nc.gpsimd.tensor_copy(xa[:], x_next[:]).then_inc(x_in.sem, 1)
                pool.wait_ge(x_in.sem, x_in.at(r))
                pool.sem_inc(x_free, 1)
                pool.wait_ge(a_var.sem, a_var.at(r))
                rsqrt(rstd[:], var_e[:], NT).then_inc(a_rstd.sem, 1)

            def rest(r):
                pool.wait_ge(b_var.sem, b_var.at(r))
                rsqrt(rstd[:], var_e[:], NT).then_inc(b_rstd.sem, 1)
                for a in range(2):
                    pool.wait_ge(ms_ok.sem, ms_ok.at(r, a + 1))
                    rsqrt(rsx[:], msx[:], NT).then_inc(rs_ok.sem, 1)
                    pool.wait_ge(mh_ok.sem, mh_ok.at(r, a + 1))
                    rsqrt(rsh[:].rearrange("p t h -> p (t h)"), sq_ms(), NT * (H1 + KV)).then_inc(rh_ok.sem, 1)
                    mask = c("causal") if a == 0 else c("local")
                    if a == 1:
                        pool.wait_ge(seam_e.sem, seam_e.at(r))
                        nc.gpsimd.tensor_tensor(prs[P - WIN1:P], prs[P - WIN1:P],
                                                c("seam")[P - WIN1:P, None, :].broadcast_to([WIN1, H1, WIN1]),
                                                ALU.mult).then_inc(seam_ok.sem, 1)
                        pool.wait_ge(seam_ok.sem, seam_ok.at(r))
                    for g in range(KV):
                        pool.wait_ge(e_ok.sem, e_ok.at(r, a * KV + g + 1))
                        m = mask[:, None, :].broadcast_to([P, GH, P])
                        nc.gpsimd.tensor_tensor(pr0[:, g % 2, :, 0:P], pr0[:, g % 2, :, 0:P], m, ALU.mult)
                        nc.gpsimd.tensor_tensor(pr1[:, g % 2], pr1[:, g % 2], m, ALU.mult).then_inc(m_ok.sem, 1)
                pool.wait_ge(c_var.sem, c_var.at(r))
                rsqrt(rstd[:], var_e[:], NT).then_inc(c_rstd.sem, 1)
                pool.wait_ge(d_var.sem, d_var.at(r))
                rsqrt(rstd[:], var_e[:], NT).then_inc(d_rstd.sem, 1)
                pool.wait_ge(fin_ok.sem, fin_ok.at(r))
                plain(pool)
                pool.dma_start(ov[bass.ds(r, 1)].rearrange("a p t d -> (a p) t d"), fin[:]).then_inc(out_ok.sem, 16)
                pool.wait_ge(out_ok.sem, out_ok.at(r))
                pool.sem_inc(fin_free, 1)

            def sq_ms():
                return ssh[:].rearrange("p t h -> p (t h)")

            pool.sem_inc(x_free, 1)
            pool.sem_inc(fin_free, 1)
            with nc.gpsimd.Fori(0, NB) as r:
                attention0(r)
                rest(r)

        @block.tensor
        def _(pe):
            pe.wait_ge(loaded, ALL)
            for h in range(H0):
                last = nc.tensor.matmul(pa[0:CQ, 0, h * LAT:(h + 1) * LAT], w_uqT[:, h, :], w_ukT[:, h, :],
                                        start=True, stop=True)
            for h in range(H0):
                last = nc.tensor.matmul(pa[0:LAT, 2 + h // 4, (h % 4) * D:(h % 4 + 1) * D], w_uvT[:, h, :],
                                        w_out[:, h, :], start=True, stop=True)
            last = nc.tensor.matmul(pb[:, 0, 0:3 * KV * HD], kv_downT[:], kv_up[:], start=True, stop=True)
            last.then_inc(derived_pe, 1)
            pe.wait_ge(derived_dve, 1)
            nc.tensor.matmul(pb[:, 1, :], w_dqT[:], w_up3.rearrange("q h f -> q (h f)"), start=True, stop=True)
            for t in range(2 * NT):
                last = nc.tensor.transpose(pb[:, 3, t * 2 * ROPE:(t + 1) * 2 * ROPE], turn[:, t * P:(t + 1) * P],
                                           ident[0:2 * ROPE, 0:2 * ROPE])
            last.then_inc(derived_pe, 1)
            pe.wait_ge(derived_dve, 2)

            def tiles_T(dst, src):
                for t in range(NT):
                    last = nc.tensor.transpose(dst[:, t * P:(t + 1) * P], src[:, t, :], ident)
                return last

            def a_front(r):
                pe.wait_ge(x_in.sem, x_in.at(r))
                tiles_T(pa[:, 0, 0:S], xa).then_inc(xaT_ps.sem, 1)
                pe.wait_ge(xaT_ok.sem, xaT_ok.at(r))
                pj3 = pa[:, 1:3, :].rearrange("p b n -> p (b n)")
                nc.tensor.matmul(pj3[:, 0:S], idx_wk[:], xaT[:], start=True, stop=True)
                for k in range(2):
                    last = nc.tensor.matmul(pj3[:, (k + 1) * S:(k + 2) * S], idx_wq[:, k * P:(k + 1) * P], xaT[:],
                                            start=True, stop=True)
                last.then_inc(idx_ps.sem, 1)
                for t in range(NT):
                    last = nc.tensor.matmul(pa[:, 3, t * FE:(t + 1) * FE], xaT[:, t * P:(t + 1) * P], w_key[:],
                                            start=True, stop=True)
                last.then_inc(key_ps.sem, 1)
                pe.wait_ge(idxT_ok.sem, idxT_ok.at(r))
                pe.wait_ge(klow_ok.sem, klow_ok.at(r))
                pe.wait_ge(klat_ok.sem, klat_ok.at(r))
                pe.wait_ge(krot_ok.sem, krot_ok.at(r))
                for t, n in ((0, J0), (1, J1)):
                    for half in range(2):
                        for k in range(2):
                            lo = DI * half
                            last = nc.tensor.matmul(pa[:, 2 * t + half, k * S:k * S + n],
                                                    idxT[lo:lo + DI, 1 + k, t * P:(t + 1) * P],
                                                    idxT[lo:lo + DI, 0, 0:n], start=True, stop=True)
                    last.then_inc(is_ps.sem, 1)
                pe.wait_ge(relu_ok.sem, relu_ok.at(r))
                plain(pe)
                for t in range(NT):
                    last = nc.tensor.transpose(pa[0:FN, 0, t * P:(t + 1) * P], k_rot[:, t, :], ident)
                last.then_inc(keyT_ps.sem, 1)
                pe.wait_ge(keysT_ok.sem, keysT_ok.at(r))
                plain(pe)
                for u in range(NU):
                    last = nc.tensor.transpose(pa[0:AW, 1, u * LAT:(u + 1) * LAT], keysT[ROPE:FN, ws(u):ws(u) + AW],
                                               ident[ROPE:FN, ROPE:FN])
                last.then_inc(win_ps.sem, 1)
                pe.wait_ge(win_ok.sem, win_ok.at(r))
                for t in range(NT):
                    last = nc.tensor.matmul(pa[:, t, :], xaT[:, t * P:(t + 1) * P], wq3[:].rearrange("d h f -> d (h f)"),
                                            start=True, stop=True)
                last.then_inc(q_ps.sem, 1)
                pe.wait_ge(qf_ok.sem, qf_ok.at(r))
                for k, (src, rows) in enumerate(((q_near_t, FN), (q_far_t, FE))):
                    for t in range(NT):
                        for half in range(2):
                            n = 4 * k + 2 * t + half
                            if n >= 4:
                                pe.wait_ge(qT0_ok.sem, qT0_ok.at(r, n - 3))
                            plain(pe)
                            for h in range(4):
                                last = nc.tensor.transpose(pa[0:rows, n % 4, h * P:(h + 1) * P],
                                                           src[:, t, 4 * half + h, :], ident)
                            last.then_inc(qT0_ps.sem, 1)

            def a_gather(r, u):
                t = u // (NU // NT)
                if u == 0:
                    pe.wait_ge(qT0_ok.sem, qT0_ok.at(r))
                    pe.wait_ge(ksplit_ok.sem, ksplit_ok.at(r))
                    pe.wait_ge(hot_ok.sem, hot_ok.at(r, 1))
                if u == NU // NT:
                    pe.wait_ge(hot_ok.sem, hot_ok.at(r))
                if u > 0:
                    pe.wait_ge(got_ok.sem, got_ok.at(r, u))
                col = (u % (NU // NT)) * UQ * NR
                parts = [(idx_rows[:, 0], 0, J0)] if t == 0 else [(hot_low, 0, P), (idx_rows[:, 1], 1, J1 - P)]
                todo = [(m, k) for m in parts for k in range(3)]
                for i, ((hot, kt, rows), k) in enumerate(todo):
                    last = nc.tensor.matmul(pa[0:FE, 0, :], k_split[0:rows, k, kt, :], hot[0:rows, col:col + UQ * NR],
                                            start=(i == 0), stop=(i == len(todo) - 1))
                last.then_inc(got_ps.sem, 1)

            def a_scores(r, u):
                if u > 0:
                    pe.wait_ge(sc_ok.sem, sc_ok.at(r, u))
                nc.tensor.matmul(pa[:, 1, 0:AW], q_near[:, u, :], keysT[:, ws(u):ws(u) + AW], start=True, stop=True)
                pe.wait_ge(got_ok.sem, got_ok.at(r, u + 1))
                for k in range(4):
                    last = nc.tensor.matmul(pa[32 * k:32 * k + 32, 1, AW:AW + BW], q_far[:, u, 32 * k:32 * k + 32],
                                            got[:, u % 2, k, :], start=True, stop=True)
                last.then_inc(sc_ps.sem, 1)

            def a_values(r, u):
                pe.wait_ge(pr_ok.sem, pr_ok.at(r, u + 1))
                if u > 0:
                    pe.wait_ge(pt_ok.sem, pt_ok.at(r, u))
                nc.tensor.transpose(pa[:, 2, 0:P], probs[:, 0:P], ident)
                nc.tensor.transpose(pa[:, 2, P:2 * P], probs[:, AW:AW + BW], ident)
                for k in range(4):
                    last = nc.tensor.transpose(pa[:, 2, 2 * P + k * LAT:2 * P + (k + 1) * LAT], got[2 * ROPE:FE, u % 2, k, :],
                                               ident[2 * ROPE:FE, 2 * ROPE:FE])
                last.then_inc(pt_ps.sem, 1)
                pe.wait_ge(pt_ok.sem, pt_ok.at(r, u + 1))
                if u % 4 == 0 and u:
                    pe.wait_ge(o_ok.sem, o_ok.at(r, u // 4))
                o = pa[0:LAT, 3, (u % 4) * P:(u % 4 + 1) * P]
                nc.tensor.matmul(o, lat_win[:, u, :], probsT[0:AW, 0, :], start=True, stop=False, skip_group_check=True)
                for k in range(4):
                    last = nc.tensor.matmul(o[:, 32 * k:32 * k + 32], probsT[:, 2, k * LAT:(k + 1) * LAT], probsT[:, 1, 32 * k:32 * k + 32],
                                            start=False, stop=(k == 3), skip_group_check=True)
                last.then_inc(o_ps.sem, 1)

            def a_back(r):
                pe.wait_ge(o_ok.sem, o_ok.at(r))
                for t in range(NT):
                    for h in range(H0):
                        last = nc.tensor.matmul(pa[:, 0, t * D:(t + 1) * D], headsT[:, h, t * P:(t + 1) * P],
                                                wvo[:, h, :], start=(h == 0), stop=(h == H0 - 1))
                last.then_inc(y_ps.sem, 1)

            def ffn0(r):
                pe.wait_ge(x1_ok.sem, x1_ok.at(r))
                tiles_T(pb[:, 0, 0:S], x1).then_inc(r_ps.sem, 1)
                pe.wait_ge(xbT_ok.sem, xbT_ok.at(r))
                for t in range(NT):
                    last = nc.tensor.matmul(pb[:, 3, t * E:(t + 1) * E], xbT[:, t * P:(t + 1) * P], wg[:],
                                            start=True, stop=True)
                last.then_inc(lg_ps.sem, 1)
                for k in range(NBLK // 2):
                    if k == 1:
                        pe.wait_ge(sh_ok.sem, sh_ok.at(r))
                    if k >= 2:
                        pe.wait_ge(hid_ok.sem, hid_ok.at(r, k - 1))
                    for j in range(2):
                        bank = pb[0:BLK, 2 * (k % 2) + j, :]
                        nc.tensor.matmul(bank[:, 0:S], w1[:, 2 * k + j, :], xbT[:], start=True, stop=True)
                        last = nc.tensor.matmul(bank[:, S:2 * S], w2[:, 2 * k + j, :], xbT[:], start=True, stop=True)
                    last.then_inc(up_ps.sem, 1)
                pe.wait_ge(hid_ok.sem, hid_ok.at(r))
                for t in range(NT):
                    for j in range(4):
                        last = nc.tensor.matmul(pb[:, 2, t * D:(t + 1) * D], hid[0:BLK, NBLK - 4 + j, t * P:(t + 1) * P],
                                                w3[:, NBLK - 4 + j, :], start=(j == 0), stop=(j == 3))
                last.then_inc(dn_ps.sem, 1)
                for t in range(NT):
                    for half in range(2):
                        n = 2 * t + half
                        if n == 3:
                            pe.wait_ge(dn_ok.sem, dn_ok.at(r, 2))
                        bank = pb[:, (0, 1, 3, 0)[n], :]
                        for e in range(4):
                            for j in range(2):
                                b = 2 * (4 * half + e) + j
                                last = nc.tensor.matmul(bank[:, e * D:(e + 1) * D], hid[0:BLK, b, t * P:(t + 1) * P],
                                                        w3[:, b, :], start=(j == 0), stop=(j == 1))
                        last.then_inc(dn_ps.sem, 1)

            def attention1(r, a):
                src = x2 if a == 0 else x3[:, 0]
                if a == 0:
                    pe.wait_ge(x2_ok.sem, x2_ok.at(r))
                else:
                    pe.wait_ge(x3_ok.sem, x3_ok.at(r, 1))
                tiles_T(pb[:, 0, 0:S], src).then_inc(tx_ps.sem, 1)
                pe.wait_ge(tx_ok.sem, tx_ok.at(r, a + 1))
                for t in range(NT):
                    last = nc.tensor.matmul(pb[:, 1 + t, 0:NPJ], xbT[:, t * P:(t + 1) * P], wpj[:, a, :],
                                            start=True, stop=True)
                last.then_inc(pj_ps.sem, 1)
                pe.wait_ge(qk_ok.sem, qk_ok.at(r, a + 1))
                tiles_T(pb[:, 3, 0:S], qn)
                tiles_T(pb[:, 3, S:2 * S], kn[:].rearrange("p t g h d -> p t (g h d)")).then_inc(qkT_ps.sem, 1)
                pe.wait_ge(qT_ok.sem, qT_ok.at(r, a + 1))
                pe.wait_ge(kb_ok.sem, kb_ok.at(r, a + 1))

                def scores(g):
                    rows = slice(32 * g, 32 * g + 32)
                    n = a * KV + g
                    if g > 0:
                        pe.wait_ge(e_ok.sem, e_ok.at(r, n))
                    width = S if a == 0 else P
                    for h in range(GH):
                        nc.tensor.matmul(pb[:, h // 2, (h % 2) * S:(h % 2) * S + width], kbig[rows, h, 0:P],
                                         qT[rows, 0:width], start=True, stop=True)
                    for h in range(GH):
                        last = nc.tensor.matmul(pb[:, 2, h * P:(h + 1) * P], kbig[rows, h, P:S], qT[rows, P:S],
                                                start=True, stop=True)
                    last.then_inc(s_ps.sem, 1)

                def values(g):
                    n = a * KV + g
                    pe.wait_ge(m_ok.sem, m_ok.at(r, n + 1))
                    if g == 0 and a == 1:
                        pe.wait_ge(seam_ok.sem, seam_ok.at(r))
                    o = pb[:, 3, 0:NT * H1 * (HD + 1)].rearrange("p (t h d) -> p t h d", t=NT, h=H1)
                    for h in range(GH):
                        nc.tensor.matmul(o[:, 0, g * GH + h, :], pr0[:, g % 2, h, 0:P], v1[:, 0, g, :],
                                         start=True, stop=True)
                        hh = g * GH + h
                        if a == 0:
                            nc.tensor.matmul(o[:, 1, hh, :], pr0[:, g % 2, h, P:S], v1[:, 0, g, :],
                                             start=True, stop=False, skip_group_check=True)
                            last = nc.tensor.matmul(o[:, 1, hh, :], pr1[:, g % 2, h, :], v1[:, 1, g, :],
                                                    start=False, stop=True, skip_group_check=True)
                        else:
                            nc.tensor.matmul(o[:, 1, hh, :], pr1[:, g % 2, h, :], v1[:, 1, g, :],
                                             start=True, stop=False, skip_group_check=True)
                            last = nc.tensor.matmul(o[0:WIN1, 1, hh, :], prs[P - WIN1:P, hh, :], v1[P - WIN1:P, 0, g, :],
                                                    start=False, stop=True, skip_group_check=True)
                    last.then_inc(pv_ps.sem, 1)

                if a == 1:
                    plain(pe)
                    for hh in range(H1):
                        rows = slice(32 * (hh // GH), 32 * (hh // GH) + 32)
                        last = nc.tensor.matmul(pb[P - WIN1:P, hh // GH, hh % GH * WIN1:(hh % GH + 1) * WIN1],
                                                kbig[rows, hh % GH, P - WIN1:P], qT[rows, P:P + WIN1],
                                                start=True, stop=True)
                    last.then_inc(seam_ps.sem, 1)
                    pe.wait_ge(seam_e.sem, seam_e.at(r))
                scores(0)
                for g in range(KV):
                    if g + 1 < KV:
                        scores(g + 1)
                    values(g)
                pe.wait_ge(att_ok.sem, att_ok.at(r, a + 1))
                tiles_T(pb[:, 0, 0:S], att).then_inc(aT_ps.sem, 1)
                pe.wait_ge(aT_ok.sem, aT_ok.at(r, a + 1))
                for t in range(NT):
                    last = nc.tensor.matmul(pb[:, 1, t * D:(t + 1) * D], attT[:, t * P:(t + 1) * P], wo[:, a, :],
                                            start=True, stop=True)
                last.then_inc(wo_ps.sem, 1)

            def ffn1(r):
                pe.wait_ge(x4_ok.sem, x4_ok.at(r))
                tiles_T(pb[:, 0, 0:S], x1).then_inc(t4_ps.sem, 1)
                pe.wait_ge(t4_ok.sem, t4_ok.at(r))
                for t in range(NT):
                    nc.tensor.matmul(pb[:, 1, t * E:(t + 1) * E], xbT[:, t * P:(t + 1) * P], gate_w[:],
                                     start=True, stop=True)
                for t in range(NT):
                    nc.tensor.matmul(pb[:, 2 + t, 0:2 * D], xbT[:, t * P:(t + 1) * P], w01[:], start=True, stop=False)
                    last = nc.tensor.matmul(pb[:, 2 + t, 0:2 * D], ones_row[:], b01[:], start=False, stop=True)
                last.then_inc(f_ps.sem, 1)

            with nc.tensor.Fori(0, NB) as r:
                a_front(r)
                a_gather(r, 0)
                a_scores(r, 0)
                for u in range(NU):
                    if u + 1 < NU:
                        a_gather(r, u + 1)
                        a_scores(r, u + 1)
                    a_values(r, u)
                a_back(r)
                if stop >= 2:
                    ffn0(r)
                if stop >= 3:
                    attention1(r, 0)
                    attention1(r, 1)
                if stop >= 4:
                    ffn1(r)

        @block.scalar
        def _(act):
            act.wait_ge(loaded, ALL)
            nc.scalar.activation(dlt[:, 0:1], raw_delta[:], ACT.Tanh, scale=0.5).then_inc(derived_act, 1)
            act.wait_ge(derived_act, 1)
            nc.scalar.activation(dlt[:, 1:2], dlt[:, 0:1], ACT.Sin, scale=3.1415925)
            nc.scalar.activation(dlt[:, 2:3], dlt[:, 0:1], ACT.Sin, scale=3.1415925 / 2).then_inc(derived_act, 1)

            def a_front(r):
                act.wait_ge(xaT_ps.sem, xaT_ps.at(r))
                nc.scalar.activation(xaT[:], pa[:, 0, 0:S], ACT.Copy).then_inc(xaT_ok.sem, 1)
                act.wait_ge(idx_ps.sem, idx_ps.at(r))
                nc.scalar.activation(idxT[:].rearrange("p k s -> p (k s)"),
                                     pa[:, 1:3, :].rearrange("p b n -> p (b n)")[:, 0:3 * S],
                                     ACT.Copy).then_inc(idxT_ok.sem, 1)
                act.wait_ge(klow_ok.sem, klow_ok.at(r))
                nc.scalar.activation(k_exp[:], k_low[:], ACT.Exp).then_inc(act_a.sem, 1)
                act.wait_ge(act_a.sem, act_a.at(r, 1))
                nc.scalar.activation(k_log[:], k_exp[:], ACT.Ln, bias=1.0).then_inc(klog_ok.sem, 1)
                for t, n in ((0, J0), (1, J1)):
                    act.wait_ge(is_ps.sem, is_ps.at(r, t + 1))
                    if t == 1:
                        act.wait_ge(rin_ok.sem, rin_ok.at(r, 1))
                    nc.scalar.activation(relu_i[:, :, :, 0:n],
                                         pa[:, 2 * t:2 * t + 2, :].rearrange("p b (k s) -> p b k s", k=2)[:, :, :, 0:n],
                                         ACT.Relu).then_inc(relu_ok.sem, 1)
                act.wait_ge(keyT_ps.sem, keyT_ps.at(r))
                nc.scalar.activation(keysT[:], pa[0:FN, 0, 0:S], ACT.Copy).then_inc(keysT_ok.sem, 1)
                act.wait_ge(win_ps.sem, win_ps.at(r))
                nc.scalar.activation(lat_win[:].rearrange("p u l -> p (u l)"), pa[0:AW, 1, :],
                                     ACT.Copy).then_inc(win_ok.sem, 1)
                act.wait_ge(qlow_ok.sem, qlow_ok.at(r))
                nc.scalar.activation(q_low[:], q_low[:], ACT.Exp).then_inc(act_a.sem, 1)
                act.wait_ge(act_a.sem, act_a.at(r))
                nc.scalar.activation(q_low[:], q_low[:], ACT.Ln, bias=1.0)
                lat = pa[:, 0:2, :].rearrange("p t (h f) -> p t h f", f=FN)[:, :, :, ROPE:FN]
                nc.scalar.activation(q_near_t[:, :, :, ROPE:FN], lat, ACT.Copy)
                nc.scalar.activation(q_far_t[:, :, :, 2 * ROPE:FE], lat, ACT.Copy).then_inc(qlog_ok.sem, 1)
                for n in range(8):
                    k, t, half = n // 4, n // 2 % 2, n % 2
                    act.wait_ge(qT0_ps.sem, qT0_ps.at(r, n + 1))
                    dst, rows = ((q_near, FN), (q_far, FE))[k]
                    nc.scalar.activation(
                        dst[:, t * NU // 2:(t + 1) * NU // 2, :].rearrange("f u (c h q) -> f (u c) h q", c=4, h=H0)
                        [:, :, 4 * half:4 * half + 4, :],
                        pa[0:rows, n % 4, :].rearrange("f (h a q) -> f a h q", h=4, q=4), ACT.Copy)\
                        .then_inc(qT0_ok.sem, 1)

            def a_exp(r, u):
                act.wait_ge(sc_ok.sem, sc_ok.at(r, u + 1))
                if u > 0:
                    act.wait_ge(pt_ps.sem, pt_ps.at(r, u))
                nc.scalar.activation(probs[:], sc[:], ACT.Exp, bias=neg_top[:], scale=SCALE0,
                                     accum_out=total[:]).then_inc(pr_e.sem, 1)

            def a_probsT(r, u):
                act.wait_ge(pt_ps.sem, pt_ps.at(r, u + 1))
                if u > 0:
                    act.wait_ge(o_ps.sem, o_ps.at(r, u))
                nc.scalar.activation(probsT[:].rearrange("p k n -> p (k n)"), pa[:, 2, 0:3 * P],
                                     ACT.Copy).then_inc(pt_ok.sem, 1)

            def a_out(r, k):
                act.wait_ge(o_ps.sem, o_ps.at(r, 4 * k + 4))
                nc.scalar.activation(headsT[:, :, 4 * UQ * k:4 * UQ * (k + 1)].rearrange("l h (n q) -> l h n q", q=4),
                                     pa[0:LAT, 3, :].rearrange("l (n h q) -> l h n q", h=H0, q=4), ACT.Copy).then_inc(o_ok.sem, 1)

            def ffn0(r):
                act.wait_ge(r_ps.sem, r_ps.at(r))
                nc.scalar.activation(xbT[:], pb[:, 0, 0:S], ACT.Copy).then_inc(xbT_ok.sem, 1)
                act.wait_ge(sh_ok.sem, sh_ok.at(r))
                nc.scalar.activation(egate[:, 1], egate[:, 0], ACT.Exp).then_inc(eg_ok.sem, 1)
                for k in range(NBLK // 2):
                    act.wait_ge(up_ps.sem, up_ps.at(r, k + 1))
                    if k >= 2:
                        act.wait_ge(hid_ok.sem, hid_ok.at(r, k - 1))
                    nc.scalar.activation(th[:, k % 2], pb[0:BLK, 2 * (k % 2):2 * (k % 2) + 2, 0:S], ACT.Tanh,
                                         scale=0.5).then_inc(th_ok.sem, 1)

            def attention1(r, a):
                act.wait_ge(tx_ps.sem, tx_ps.at(r, a + 1))
                nc.scalar.activation(xbT[:], pb[:, 0, 0:S], ACT.Copy).then_inc(tx_ok.sem, 1)
                act.wait_ge(pj_ps.sem, pj_ps.at(r, a + 1))
                act.wait_ge(rs_ok.sem, rs_ok.at(r, a + 1))
                for t in range(NT):
                    last = nc.scalar.activation(pj[:, t, :], pb[:, 1 + t, 0:NPJ], ACT.Copy, scale=rsx[:, t:t + 1])
                last.then_inc(pj_ok.sem, 1)
                act.wait_ge(qkT_ps.sem, qkT_ps.at(r, a + 1))
                nc.scalar.activation(qT[:], pb[:, 3, 0:S], ACT.Copy).then_inc(qT_ok.sem, 1)
                if a == 1:
                    act.wait_ge(seam_ps.sem, seam_ps.at(r))
                    nc.scalar.activation(prs[P - WIN1:P].rearrange("p (g h) q -> p g (h q)", g=KV),
                                         pb[P - WIN1:P, :, 0:GH * WIN1], ACT.Exp,
                                         scale=SCALE1).then_inc(seam_e.sem, 1)
                width = S if a == 0 else P
                for g in range(KV):
                    n = a * KV + g
                    act.wait_ge(s_ps.sem, s_ps.at(r, n + 1))
                    if g >= 2:
                        act.wait_ge(pv_ps.sem, pv_ps.at(r, n - 1))
                    nc.scalar.activation(pr0[:, g % 2, :, 0:width],
                                         pb[:, 0:2, :].rearrange("p b (k s) -> p (b k) s", k=2)[:, :, 0:width],
                                         ACT.Exp, scale=SCALE1)
                    nc.scalar.activation(pr1[:, g % 2], pb[:, 2, :].rearrange("p (h q) -> p h q", h=GH), ACT.Exp,
                                         scale=SCALE1).then_inc(e_ok.sem, 1)
                act.wait_ge(aT_ps.sem, aT_ps.at(r, a + 1))
                nc.scalar.activation(attT[:], pb[:, 0, 0:S], ACT.Copy).then_inc(aT_ok.sem, 1)

            def ffn1(r):
                act.wait_ge(t4_ps.sem, t4_ps.at(r))
                nc.scalar.activation(xbT[:], pb[:, 0, 0:S], ACT.Copy).then_inc(t4_ok.sem, 1)
                act.wait_ge(f_ps.sem, f_ps.at(r))
                nc.scalar.activation(e01[:, 0], pb[:, 2:4, 0:2 * D], ACT.Tanh, scale=0.5).then_inc(fth_ok.sem, 1)
                act.wait_ge(fsh_ok.sem, fsh_ok.at(r))
                nc.scalar.activation(egate[:, 1], egate[:, 0], ACT.Exp).then_inc(feg_ok.sem, 1)

            with nc.scalar.Fori(0, NB) as r:
                a_front(r)
                a_exp(r, 0)
                for u in range(NU):
                    a_probsT(r, u)
                    if u + 1 < NU:
                        a_exp(r, u + 1)
                    if u % 4 == 3:
                        a_out(r, u // 4)
                if stop >= 2:
                    ffn0(r)
                if stop >= 3:
                    attention1(r, 0)
                    attention1(r, 1)
                if stop >= 4:
                    ffn1(r)

        @block.vector
        def _(dve):
            V = nc.vector
            dve.wait_ge(loaded, ALL)
            V.memset(ones_row[:], 1.0)
            V.memset(v1[:], 1.0)
            V.memset(rank_turn[2 * ROPE:FE, :], 1.0)
            dve.wait_ge(derived_pe, 1)
            V.tensor_copy(w_up3[:, :, ROPE:FN], pa[0:CQ, 0, 0:H0 * LAT].rearrange("q (h l) -> q h l", h=H0))
            V.tensor_copy(wvo[:].rearrange("l h d -> l (h d)"), pa[0:LAT, 2:4, :].rearrange("l b n -> l (b n)"))
            kk = KV * HD
            V.tensor_copy(wpj[:, 0, H1 * HD:NQK], pb[:, 0, 0:kk])
            V.tensor_copy(wpj[:, 0, NQK + H1 * HD:2 * NQK], pb[:, 0, kk:2 * kk])
            V.tensor_copy(wpj[:, 0, 2 * NQK:NPJ], pb[:, 0, 2 * kk:3 * kk]).then_inc(ready, 1)
            dve.wait_ge(ready, 1)
            for a in range(2):
                V.tensor_scalar(wpj[:, a, :], wpj[:, a, :], norm_w[:, a:a + 1], None, ALU.mult)
            dve.wait_ge(derived_act, 2)
            V.tensor_tensor(dlt[:, 3:4], dlt[:, 2:3], dlt[:, 2:3], ALU.mult).then_inc(ready, 1)
            dve.wait_ge(ready, 2)
            V.tensor_scalar(dlt[:, 4:5], dlt[:, 3:4], 2.0, -1.0, ALU.mult, ALU.add).then_inc(ready, 1)
            dve.wait_ge(ready, 3)
            V.tensor_scalar(turn[:], turn_v, dlt[:, 1:2], None, ALU.mult).then_inc(ready, 1)
            dve.wait_ge(ready, 4)
            V.scalar_tensor_tensor(turn[:], turn_u, dlt[:, 4:5], turn[:], ALU.mult, ALU.add).then_inc(ready, 1)
            dve.wait_ge(ready, 5)
            V.tensor_copy(rank_turn[0:2 * ROPE, :], turn[:, 2 * S:2 * S + NR]).then_inc(derived_dve, 1)
            dve.wait_ge(derived_pe, 2)
            V.tensor_copy(wq3[:].rearrange("d h f -> d (h f)"), pb[:, 1, :])
            V.tensor_copy(turns_t[:].rearrange("p k t f -> p (k t f)"), pb[:, 3, 0:2 * NT * 2 * ROPE]).then_inc(derived_dve, 1)
            dve.wait_ge(derived_dve, 2)

            def chained(r, chain, count):
                def link(ins):
                    count[0] += 1
                    ins.then_inc(chain.sem, 1)
                    dve.wait_ge(chain.sem, chain.at(r, count[0]))
                return link

            def layer_norm(link, r, src, dst, var, rs, done):
                for t in range(NT):
                    last = V.bn_stats(st6[:, t, :], src[:, t, :])
                link(last)
                plain(dve)
                for t in range(NT):
                    last = V.bn_aggr(mv[:, t, :], st6[:, t, :])
                link(last)
                V.tensor_scalar(var_e[:], mv[:, :, 1], 1e-5, None, ALU.add).then_inc(var.sem, 1)
                dve.wait_ge(rs.sem, rs.at(r))
                for t in range(NT):
                    last = V.tensor_scalar(dst[:, t, :], src[:, t, :], mv[:, t, 0:1], rstd[:, t:t + 1],
                                           ALU.subtract, ALU.mult)
                last.then_inc(done.sem, 1)

            def a_front(r, link):
                dve.wait_ge(key_ps.sem, key_ps.at(r))
                kp = pa[:, 3, 0:NT * FE].rearrange("p (t f) -> p t f", t=NT)
                V.tensor_copy(k_feat[:, :, 2 * ROPE:FE], kp[:, :, 2 * ROPE:FE]).then_inc(klat_ok.sem, 1)
                V.tensor_scalar(k_low[:], kp[:, :, 0:2 * ROPE], 40.0, None, ALU.min).then_inc(klow_ok.sem, 1)
                dve.wait_ge(klog_ok.sem, klog_ok.at(r))
                link(V.tensor_tensor(k_feat[:, :, 0:2 * ROPE], k_log[:], kp[:, :, 0:2 * ROPE], ALU.max))
                link(V.tensor_tensor(k_mul[:], k_feat[:, :, 0:2 * ROPE], turns_t[:, 1], ALU.mult))
                V.tensor_tensor(k_rot[:, :, 0:ROPE], k_mul[:, :, 0:ROPE], k_mul[:, :, ROPE:2 * ROPE], ALU.add)
                dve.wait_ge(klat_ok.sem, klat_ok.at(r))
                V.tensor_copy(k_rot[:, :, ROPE:FN], k_feat[:, :, 2 * ROPE:FE]).then_inc(krot_ok.sem, 1)
                link(V.tensor_copy(k_split[:, 0], k_feat[:]))
                link(V.tensor_tensor(k_rest[:, 0], k_feat[:], k_split[:, 0], ALU.subtract))
                link(V.tensor_copy(k_split[:, 1], k_rest[:, 0]))
                link(V.tensor_tensor(k_rest[:, 1], k_rest[:, 0], k_split[:, 1], ALU.subtract))
                V.tensor_copy(k_split[:, 2], k_rest[:, 1]).then_inc(ksplit_ok.sem, 1)
                for t, n in ((0, J0), (1, J1)):
                    dve.wait_ge(relu_ok.sem, relu_ok.at(r, t + 1))
                    for h in range(NI):
                        before = c(f"mask_rank{t}") if h == 0 else rank_in[:, t, 0:n]
                        ins = V.scalar_tensor_tensor(rank_in[:, t, 0:n], relu_i[:, h % 2, h // 2, 0:n],
                                                     idx_w[:, h:h + 1], before, ALU.mult, ALU.add)
                        if h < NI - 1:
                            link(ins)
                    ins.then_inc(rin_ok.sem, 1)
                    dve.wait_ge(rin_ok.sem, rin_ok.at(r, t + 1))
                    for k in range(NR // 8):
                        plain(dve)
                        link(V.max(top[:, 8 * k:8 * k + 8], rank_in[:, t, 0:n]))
                        plain(dve)
                        link(V.max_index(idx_u[:, t, 8 * k:8 * k + 8], top[:, 8 * k:8 * k + 8], rank_in[:, t, 0:n]))
                        if k < NR // 8 - 1:
                            plain(dve)
                            link(V.match_replace(rank_in[:, t, 0:n], top[:, 8 * k:8 * k + 8], rank_in[:, t, 0:n], GONE))
                V.tensor_copy(idx_b[:], idx_u[:]).then_inc(ib_ok.sem, 1)
                dve.wait_ge(q_ps.sem, q_ps.at(r))
                qp = pa[:, 0:2, :].rearrange("p t (h f) -> p t h f", f=FN)[:, :, :, 0:ROPE]
                V.tensor_scalar(q_low[:], qp, 40.0, None, ALU.min).then_inc(qlow_ok.sem, 1)
                dve.wait_ge(qlog_ok.sem, qlog_ok.at(r))
                link(V.tensor_tensor(q_low[:], q_low[:], qp, ALU.max))
                half = ROPE // 2
                for k in range(2):
                    def tab(lo, n):
                        return turns_t[:, k, :, lo:lo + n].unsqueeze(2).broadcast_to([P, NT, H0, n])
                    V.tensor_tensor(q_turn[:, 0], q_low[:], tab(0, ROPE), ALU.mult)
                    V.tensor_tensor(q_turn[:, 1, :, :, 0:half], q_low[:, :, :, half:ROPE], tab(ROPE, half), ALU.mult)
                    link(V.tensor_tensor(q_turn[:, 1, :, :, half:ROPE], q_low[:, :, :, 0:half], tab(ROPE + half, half),
                                         ALU.mult))
                    if k == 0:
                        link(V.tensor_tensor(q_near_t[:, :, :, 0:ROPE], q_turn[:, 0], q_turn[:, 1], ALU.add))
                    else:
                        for i in range(2):
                            last = V.tensor_tensor(q_far_t[:, :, :, i * ROPE:(i + 1) * ROPE], q_turn[:, 0], q_turn[:, 1],
                                                   ALU.add)
                        last.then_inc(qf_ok.sem, 1)
                dve.wait_ge(ir_ok.sem, ir_ok.at(r))
                V.tensor_scalar(idx_rows[0:J0, 0, :], idx_rows[0:J0, 0, :], c("iota", J0)[:, 0:1], None,
                                ALU.is_equal).then_inc(hot_ok.sem, 1)
                link(V.tensor_scalar(hot_low[:], idx_rows[:, 1, :], c("iota")[:, 0:1], None, ALU.is_equal))
                V.tensor_scalar(idx_rows[0:J1 - P, 1, :], idx_rows[0:J1 - P, 1, :], c("iota", J1 - P)[:, 1:2], None,
                                ALU.is_equal).then_inc(hot_ok.sem, 1)

            def a_got(r, u):
                dve.wait_ge(got_ps.sem, got_ps.at(r, u + 1))
                if u > 1:
                    dve.wait_ge(pt_ps.sem, pt_ps.at(r, u - 1))
                V.tensor_tensor(got[:, u % 2].rearrange("f k (q n) -> f (k q) n", n=NR),
                                pa[0:FE, 0, :].rearrange("f (q n) -> f q n", n=NR),
                                rank_turn[:, None, :].broadcast_to([FE, UQ, NR]), ALU.mult).then_inc(got_ok.sem, 1)

            def a_max(r, u, link):
                dve.wait_ge(sc_ps.sem, sc_ps.at(r, u + 1))
                if u > 0:
                    dve.wait_ge(pr_e.sem, pr_e.at(r, u))
                plain(dve)
                link(V.tensor_tensor_reduce(out=sc[:], in0=pa[:, 1, 0:AW + BW],
                                            in1=c("mask_first" if UQ * u < WIN0 else "mask_later"),
                                            scale=1.0, scalar=-3e38, op0=ALU.add, op1=ALU.max, accum_out=top_s[:]))
                V.tensor_scalar(neg_top[:], top_s[:], -SCALE0, None, ALU.mult).then_inc(sc_ok.sem, 1)

            def a_norm(r, u, link):
                dve.wait_ge(pr_e.sem, pr_e.at(r, u + 1))
                link(V.reciprocal(inv_total[:], total[:]))
                V.tensor_scalar(probs[:], probs[:], inv_total[:], None, ALU.mult).then_inc(pr_ok.sem, 1)

            def a_back(r, link):
                dve.wait_ge(y_ps.sem, y_ps.at(r))
                link(V.tensor_tensor(pre[:].rearrange("p t d -> p (t d)"), pa[:, 0, 0:S],
                                     xa[:].rearrange("p t d -> p (t d)"), ALU.add))
                layer_norm(link, r, pre, x1 if stop > 1 else fin, a_var, a_rstd, x1_ok if stop > 1 else fin_ok)

            def row_softmax_in(link, r, ps, done):
                link(V.tensor_copy(lg[:].rearrange("p t e -> p (t e)"), ps))
                link(V.reduce_max(small[:, 0, :], lg[:], axis=AX.X))
                V.tensor_tensor(egate[:, 0], lg[:], small[:, 0, :].unsqueeze(2).broadcast_to([P, NT, E]),
                                ALU.subtract).then_inc(done.sem, 1)

            def ffn0(r, link):
                dve.wait_ge(lg_ps.sem, lg_ps.at(r))
                row_softmax_in(link, r, pb[:, 3, 0:NT * E], sh_ok)
                for t in range(NT):
                    them = lg[:, t, None, :].broadcast_to([P, E, E])
                    me = lg[:, t, :].unsqueeze(2).broadcast_to([P, E, E])
                    V.tensor_tensor(gt[:, t], them, me, ALU.is_gt)
                    last = V.tensor_tensor(eq[:, t], them, me, ALU.is_equal)
                link(last)
                for t in range(NT):
                    last = V.tensor_tensor(eq[:, t], eq[:, t], c("before").rearrange("p (a b) -> p a b", a=E), ALU.mult)
                link(last)
                link(V.tensor_tensor(gt[:], gt[:], eq[:], ALU.add))
                link(V.reduce_sum(rank[:, 0], gt[:], axis=AX.X))
                dve.wait_ge(eg_ok.sem, eg_ok.at(r))
                link(V.scalar_tensor_tensor(rank[:, 1].rearrange("p t e -> p (t e)"),
                                            rank[:, 0].rearrange("p t e -> p (t e)"), 2.0,
                                            egate[:, 1].rearrange("p t e -> p (t e)"), ALU.is_lt, ALU.mult))
                link(V.reduce_sum(small[:, 1, :], rank[:, 1], axis=AX.X))
                link(V.reciprocal(small[:, 2, :], small[:, 1, :]))
                link(V.tensor_tensor(rank[:, 2], rank[:, 1], small[:, 2, :].unsqueeze(2).broadcast_to([P, NT, E]),
                                     ALU.mult))
                for k in range(NBLK // 2):
                    dve.wait_ge(th_ok.sem, th_ok.at(r, k + 1))
                    ps = pb[0:BLK, 2 * (k % 2):2 * (k % 2) + 2, :]
                    link(V.scalar_tensor_tensor(th[:, k % 2], th[:, k % 2], 1.0, ps[:, :, 0:S], ALU.add, ALU.mult))
                    V.scalar_tensor_tensor(hid[0:BLK, 2 * k:2 * k + 2, :], th[:, k % 2], 0.5, ps[:, :, S:2 * S],
                                           ALU.mult, ALU.mult).then_inc(hid_ok.sem, 1)
                dve.wait_ge(dn_ps.sem, dn_ps.at(r, 1))
                ins = V.tensor_tensor(preb[:].rearrange("p t d -> p (t d)"), pb[:, 2, 0:S],
                                      x1[:].rearrange("p t d -> p (t d)"), ALU.add)
                ins.then_inc(dn_ok.sem, 1)
                dve.wait_ge(dn_ok.sem, dn_ok.at(r, 1))
                for t in range(NT):
                    for half in range(2):
                        n = 2 * t + half
                        dve.wait_ge(dn_ps.sem, dn_ps.at(r, n + 2))
                        for e in range(4):
                            ins = V.scalar_tensor_tensor(preb[:, t, :], pb[:, (0, 1, 3, 0)[n], e * D:(e + 1) * D],
                                                         rank[:, 2, t, 4 * half + e:4 * half + e + 1], preb[:, t, :],
                                                         ALU.mult, ALU.add)
                            if e < 3:
                                link(ins)
                        ins.then_inc(dn_ok.sem, 1)
                        dve.wait_ge(dn_ok.sem, dn_ok.at(r, n + 2))
                layer_norm(link, r, preb, x2 if stop > 2 else fin, b_var, b_rstd, x2_ok if stop > 2 else fin_ok)

            def attention1(r, a, link):
                src = x2 if a == 0 else x3[:, 0]
                if a == 0:
                    dve.wait_ge(x2_ok.sem, x2_ok.at(r))
                else:
                    dve.wait_ge(x3_ok.sem, x3_ok.at(r, 1))
                for t in range(NT):
                    link(V.tensor_tensor_reduce(out=sqx[:], in0=src[:, t, :], in1=src[:, t, :], scale=1.0, scalar=0.0,
                                                op0=ALU.mult, op1=ALU.add, accum_out=ssx[:, t:t + 1]))
                V.tensor_scalar(msx[:], ssx[:], 1.0 / D, 1e-6, ALU.mult, ALU.add).then_inc(ms_ok.sem, 1)
                dve.wait_ge(pj_ok.sem, pj_ok.at(r, a + 1))
                link(V.tensor_tensor(ro[:, 0], pj[:, :, 0:NQK], pj[:, :, 0:NQK], ALU.mult))
                link(V.reduce_sum(ssh[:], ro[:, 0].rearrange("p t (h d) -> p t h d", d=HD), axis=AX.X))
                link(V.tensor_scalar(ssh[:], ssh[:], 1.0 / HD, 1e-6, ALU.mult, ALU.add))
                V.tensor_copy(v1[:, :, :, 0:HD], pj[:, :, 2 * NQK:NPJ].rearrange("p t (g d) -> p t g d", d=HD))\
                    .then_inc(mh_ok.sem, 1)
                cos, sin = (c(n + "_" + "gl"[a]).rearrange("p (t d) -> p t d", t=NT) for n in ("cos", "sin"))
                for k, tab in enumerate((cos, sin)):
                    last = V.tensor_tensor(ro[:, k].rearrange("p t (h d) -> p t h d", d=HD),
                                           pj[:, :, k * NQK:(k + 1) * NQK].rearrange("p t (h d) -> p t h d", d=HD),
                                           tab.unsqueeze(2).broadcast_to([P, NT, H1 + KV, HD]), ALU.mult)
                link(last)
                link(V.tensor_tensor(ro[:, 0], ro[:, 0], ro[:, 1], ALU.add))
                dve.wait_ge(rh_ok.sem, rh_ok.at(r, a + 1))
                rot = ro[:, 0].rearrange("p t (h d) -> p t h d", d=HD)
                V.tensor_tensor(qn[:].rearrange("p t (h d) -> p t h d", d=HD), rot[:, :, 0:H1, :],
                                rsh[:, :, 0:H1].unsqueeze(3).broadcast_to([P, NT, H1, HD]), ALU.mult)
                link(V.tensor_tensor(rot[:, :, H1:, :], rot[:, :, H1:, :],
                                     rsh[:, :, H1:].unsqueeze(3).broadcast_to([P, NT, KV, HD]), ALU.mult))
                for t in range(NT):
                    last = V.tensor_copy(kn[:, t], rot[:, t, H1:, :].unsqueeze(2).broadcast_to([P, KV, GH, HD]))
                last.then_inc(qk_ok.sem, 1)
                dve.wait_ge(qkT_ps.sem, qkT_ps.at(r, a + 1))
                dve.wait_ge(qT_ok.sem, qT_ok.at(r, a + 1))
                V.tensor_tensor(kbig[:], pb[:, 3, S:2 * S].unsqueeze(1).broadcast_to([P, GH, S]),
                                c("headsel").unsqueeze(2).broadcast_to([P, GH, S]), ALU.mult).then_inc(kb_ok.sem, 1)
                dve.wait_ge(pv_ps.sem, pv_ps.at(r, (a + 1) * KV))
                o = pb[:, 3, 0:NT * H1 * (HD + 1)].rearrange("p (t h d) -> p t h d", t=NT, h=H1)
                link(V.reciprocal(inv_l[:], o[:, :, :, HD]))
                V.tensor_tensor(att[:].rearrange("p t (h d) -> p t h d", d=HD), o[:, :, :, 0:HD],
                                inv_l[:].unsqueeze(3).broadcast_to([P, NT, H1, HD]), ALU.mult).then_inc(att_ok.sem, 1)
                dve.wait_ge(wo_ps.sem, wo_ps.at(r, a + 1))
                V.tensor_tensor(x3[:, a], pb[:, 1, 0:S].rearrange("p (t d) -> p t d", t=NT),
                                x2[:] if a == 0 else x3[:, 0], ALU.add).then_inc(x3_ok.sem, 1)
                dve.wait_ge(x3_ok.sem, x3_ok.at(r, a + 1))
                if a == 1:
                    link(V.tensor_tensor(x3[:, 1], x3[:, 1], x2[:], ALU.add))
                    layer_norm(link, r, x3[:, 1], x1 if stop > 3 else fin, c_var, c_rstd, x4_ok if stop > 3 else fin_ok)

            def ffn1(r, link):
                dve.wait_ge(x4_ok.sem, x4_ok.at(r))
                dve.wait_ge(f_ps.sem, f_ps.at(r))
                row_softmax_in(link, r, pb[:, 1, 0:NT * E], fsh_ok)
                dve.wait_ge(fth_ok.sem, fth_ok.at(r))
                link(V.scalar_tensor_tensor(e01[:, 0], e01[:, 0], 1.0, pb[:, 2:4, 0:2 * D], ALU.add, ALU.mult))
                dve.wait_ge(feg_ok.sem, feg_ok.at(r))
                link(V.reduce_sum(small[:, 1, :], egate[:, 1], axis=AX.X))
                link(V.reciprocal(small[:, 2, :], small[:, 1, :]))
                link(V.tensor_tensor(egate[:, 2], egate[:, 1], small[:, 2, :].unsqueeze(2).broadcast_to([P, NT, E]),
                                     ALU.mult))
                wt = egate[:, 2]
                link(V.reduce_max(small[:, 3, :], wt, axis=AX.X))
                link(V.tensor_tensor(small[:, 4, :], wt[:, :, 0], small[:, 3, :], ALU.is_ge))
                link(V.tensor_tensor(rank[:, 0], wt, wt[:, :, 1:2].broadcast_to([P, NT, E]), ALU.is_gt))
                link(V.reduce_sum(small[:, 5, :], rank[:, 0], axis=AX.X))
                link(V.tensor_tensor(small[:, 6, :], wt[:, :, 0], wt[:, :, 1], ALU.is_equal))
                link(V.tensor_tensor(small[:, 5, :], small[:, 5, :], small[:, 6, :], ALU.add))
                link(V.scalar_tensor_tensor(small[:, 4, :], small[:, 4, :], 0.5, wt[:, :, 0], ALU.mult, ALU.mult))
                link(V.tensor_scalar(small[:, 5, :], small[:, 5, :], 1.0, 0.5, ALU.is_equal, ALU.mult))
                link(V.tensor_tensor(small[:, 5, :], small[:, 5, :], wt[:, :, 1], ALU.mult))
                for k in range(2):
                    for t in range(NT):
                        ins = V.scalar_tensor_tensor(pre_b(t), e01[:, 0, t, k * D:(k + 1) * D],
                                                     small[:, 4 + k, t:t + 1], x1[:, t, :] if k == 0 else pre_b(t),
                                                     ALU.mult, ALU.add)
                    link(ins)
                if True:
                    dve.wait_ge(fin_free, r + 1)
                    layer_norm(link, r, preb, fin, d_var, d_rstd, fin_ok)

            def pre_b(t):
                return preb[:, t, :]

            with nc.vector.Fori(0, NB) as r:
                na, nb = [0], [0]
                la, lb = chained(r, chain_a, na), chained(r, chain_b, nb)
                a_front(r, la)
                a_got(r, 0)
                a_max(r, 0, la)
                for u in range(NU):
                    if u + 1 < NU:
                        a_got(r, u + 1)
                    a_norm(r, u, la)
                    if u + 1 < NU:
                        a_max(r, u + 1, la)
                a_back(r, la)
                if stop >= 2:
                    ffn0(r, lb)
                if stop >= 3:
                    attention1(r, 0, lb)
                    attention1(r, 1, lb)
                if stop >= 4:
                    ffn1(r, lb)
                assert na[0] == CHAIN_A, na[0]
                assert nb[0] == CHAIN_B or stop < 4, nb[0]


CHAIN_A, CHAIN_B = 74, 74
SCALE0 = float((DH0 + ROPE) ** -0.5)
SCALE1 = float(HD ** -0.5)


def kernel(**inputs):
    import concourse.bacc as _bacc
    from concourse import mybir as _mybir
    from concourse.bass_utils import run_bass_kernel_spmd as _run

    g = {k: np.asarray(v) for k, v in inputs.items()}
    half = ROPE // 2
    heads = lambda a, n: a.reshape(a.shape[0], n, -1)
    swap_half = lambda a: np.concatenate([a[..., half:], a[..., :half]], -1)
    swap_pair = lambda a: a.reshape(a.shape[0], -1, 2)[:, :, ::-1].reshape(a.shape[0], -1)
    qr = heads(g["L0_attn_W_qr"], H0)
    kr = g["L0_attn_W_kr"]
    up3 = np.concatenate([qr, np.zeros((CQ, H0, LAT), np.float32)], -1)
    ffn_in = lambda e, s: np.concatenate([g[e].transpose(1, 0, 2).reshape(D, E * HE), g[s]], 1).reshape(D, NBLK, BLK)
    w3 = np.concatenate([g["L0_ffn_W3"].reshape(E * HE, D), g["L0_ffn_Ws3"]]).reshape(NBLK, BLK, D).transpose(1, 0, 2)
    kk = np.zeros((D, KV * HD), np.float32)
    glob = np.concatenate([g["L1_attn_g_wq"], kk, swap_pair(g["L1_attn_g_wq"]), kk, kk], 1)
    loc = np.concatenate([g["L1_attn_l_wq"], g["L1_attn_l_wk"], swap_pair(g["L1_attn_l_wq"]),
                          swap_pair(g["L1_attn_l_wk"]), g["L1_attn_l_wv"]], 1)
    tables, where, turns = constants()
    arrays = {
        "x": g["L0_attn_x"], "consts": tables, "turns": turns,
        "w_dqT": g["L0_attn_W_dq"].T, "w_uqT": heads(g["L0_attn_W_uq"], H0).transpose(2, 1, 0),
        "w_ukT": heads(g["L0_attn_W_uk"], H0).transpose(2, 1, 0),
        "w_uvT": heads(g["L0_attn_W_uv"], H0).transpose(2, 1, 0),
        "w_out": g["L0_attn_W_out"].reshape(H0, DH0, D).transpose(1, 0, 2), "w_up3": up3,
        "w_key": np.concatenate([kr, swap_half(kr), g["L0_attn_W_dkv"]], 1),
        "idx_wq": g["L0_attn_idx_wq"], "idx_wk": g["L0_attn_idx_wk"], "idx_w": g["L0_attn_idx_w"],
        "raw_delta": g["L0_attn_raw_delta"], "wg": g["L0_ffn_Wg"],
        "w1": ffn_in("L0_ffn_W1", "L0_ffn_Ws1"), "w2": ffn_in("L0_ffn_W2", "L0_ffn_Ws2"), "w3": w3,
        "norm_w": np.stack([g["L1_attn_norm1_w"], g["L1_attn_norm2_w"]], 1), "wpj": np.stack([glob, loc], 1),
        "kv_downT": g["L1_attn_g_kv_down"].T,
        "kv_up": np.concatenate([g["L1_attn_g_k_up"], swap_pair(g["L1_attn_g_k_up"]), g["L1_attn_g_v_up"]], 1),
        "wo": np.stack([g["L1_attn_g_wo"], g["L1_attn_l_wo"]], 1), "gate_w": g["L1_ffn_gate_w"],
        "w01": np.concatenate([g["L1_ffn_w0"].T, g["L1_ffn_w1"].T], 1),
        "b01": np.concatenate([g["L1_ffn_b0"], g["L1_ffn_b1"]])[None],
    }
    arrays = {"in_" + k: np.ascontiguousarray(v) for k, v in arrays.items()}
    nc = _bacc.Bacc("TRN2", target_bir_lowering=False, num_devices=1)
    aps = {k[3:]: nc.dram_tensor(k, v.shape, _mybir.dt.from_np(v.dtype), kind="ExternalInput").ap()
           for k, v in arrays.items()}
    out = nc.dram_tensor("out", (NB, S, D), _mybir.dt.float32, kind="ExternalOutput").ap()
    layers(nc, aps["x"], aps["consts"], aps, out, where)
    r = _run(nc, [arrays], core_ids=[0])
    return r.results[0]["out"]
```

```python
import numpy as np
import concourse.bass as bass
from concourse import mybir
from concourse.alu_op_type import AluOpType as ALU
from contextlib import ExitStack

NB, S, D = 8, 256, 128
P = 128
NT = S // P
H0, DH0, LAT, CQ, ROPE = 8, 64, 32, 64, 32
NI, DI = 4, 64
TOPK, WIN0 = 96, 64
NR = TOPK - WIN0
FE = 2 * ROPE + LAT
UQ = 16
NU = S // UQ
AW = WIN0 + UQ
BW = 4 * NR
J0, J1 = TOPK, S - WIN0
E, HE, HS, BLK = 8, 176, 352, 88
NBLK = (E * HE + HS) // BLK
H1, KV, HD, WIN1 = 16, 4, 8, 32
GH = H1 // KV
NQK = (H1 + KV) * HD
NPJ = 2 * NQK + KV * HD
FAR, GONE = -1e30, -3e38
FN = ROPE + LAT
ANG = 2 * S + NR


def constants():
    p = np.arange(P)
    cols = {}
    cols["ident"] = np.eye(P)
    quad, qi = p // 32, p % 4
    dq = 4 * quad + qi
    jj = np.arange(AW)
    own = np.where(np.arange(BW)[None] // NR == qi[:, None], 0.0, FAR)
    first = np.where(np.broadcast_to(jj[None] < WIN0, (P, AW)), 0.0, FAR)
    later = np.where((jj[None] >= 1 + dq[:, None]) & (jj[None] <= WIN0 + dq[:, None]), 0.0, FAR)
    cols["mask_first"] = np.concatenate([first, own], 1)
    cols["mask_later"] = np.concatenate([later, own], 1)
    for t, n in ((0, J0), (1, J1)):
        q, j = (t * P + p)[:, None], np.arange(n)[None]
        m = np.where(j > np.maximum(q, WIN0 - 1), FAR * (1 + j / 256.0), GONE)
        cols[f"mask_rank{t}"] = np.where(j <= q - WIN0, 0.0, m)
    cols["iota"] = np.stack([p, p + P], 1)
    cols["causal"] = (p[None] >= p[:, None]) * 1.0
    diff = p[None] - p[:, None]
    cols["local"] = ((diff >= 0) & (diff < WIN1)) * 1.0
    cols["seam"] = np.where(p[:, None] >= P - WIN1, (p[:, None] - (P - WIN1)) > np.arange(WIN1)[None], 0) * 1.0
    cols["headsel"] = (p[:, None] // HD % GH == np.arange(GH)[None]) * 1.0
    cols["before"] = np.tile((np.arange(E)[None] < np.arange(E)[:, None]).reshape(1, -1), (P, 1)) * 1.0
    cols["power"] = np.full((P, 2 * (H1 + KV)), -0.5)
    pos = np.arange(S).reshape(NT, P).T
    for name, base in (("g", 1e6), ("l", 1e4)):
        f = (1.0 / np.float32(base) ** (np.arange(0, HD, 2, dtype=np.float32) / HD)).astype(np.float32)
        a = (pos[:, :, None].astype(np.float32) * f).astype(np.float64)
        c, s = np.cos(a), np.sin(a)
        cols[f"cos_{name}"] = np.stack([c, c], -1).reshape(P, -1)
        cols[f"sin_{name}"] = np.stack([-s, s], -1).reshape(P, -1)
    half = ROPE // 2
    theta = (1.0 / np.float32(10000.0) ** (2.0 * np.arange(half, dtype=np.float32) / ROPE)).astype(np.float32)
    q = np.arange(S)
    near = np.where(q < WIN0, q, 2 * q - (WIN0 - 1))
    at = np.concatenate([near, q, np.arange(WIN0, TOPK)]).astype(np.float32)
    a = (theta[:, None] * at[None]).astype(np.float64)
    a = np.concatenate([a, a])
    sign = np.where(np.arange(ROPE) < half, -1.0, 1.0)[:, None]
    u = np.concatenate([np.cos(a), sign * np.sin(a)])
    v = np.concatenate([-np.sin(a), sign * np.cos(a)])
    where, at = {}, 0
    for k, c in cols.items():
        where[k] = (at, at + c.shape[1])
        at += c.shape[1]
    return np.concatenate(list(cols.values()), 1).astype(np.float32), where, np.stack([u, v]).astype(np.float32)


def layers(nc, x, consts, w, out, where):
    F, BF, U32 = mybir.dt.float32, mybir.dt.bfloat16, mybir.dt.uint32
    ACT, AX = mybir.ActivationFunctionType, mybir.AxisListType
    ctx = ExitStack()
    with ctx:
        def sb(name, shape, dt=F):
            return ctx.enter_context(nc.sbuf_tensor(name, shape, dt))

        def sem(name):
            return ctx.enter_context(nc.semaphore(name))

        cst = sb("cst", [P, consts.shape[1]])

        def c(name, rows=P):
            return cst[0:rows, where[name][0]:where[name][1]]

        ident = c("ident")
        x_next = sb("x_next", [P, NT, D])
        hid = sb("hid", [P, NBLK, S])
        spare = hid[:].rearrange("p b s -> p (b s)")
        spare_at = [0]

        def early(rows, a, b):
            lo = spare_at[0]
            spare_at[0] += a * b
            return spare[0:rows, lo:lo + a * b].rearrange("p (a b) -> p a b", a=a)

        w_dqT = sb("w_dqT", [CQ, D])
        w_uqT = early(DH0, H0, CQ)
        w_ukT = early(DH0, H0, LAT)
        w_uvT = early(DH0, H0, LAT)
        w_out = early(DH0, H0, D)
        w_up3 = early(CQ, H0, FN)
        turn_u = early(2 * ROPE, 1, ANG)[:, 0, :]
        turn_v = early(2 * ROPE, 1, ANG)[:, 0, :]
        w_key = sb("w_key", [D, 2 * ROPE + LAT])
        idx_wq = sb("idx_wq", [D, NI * DI])
        idx_wk = sb("idx_wk", [D, 2 * DI])
        idx_w = sb("idx_w", [P, NI])
        raw_delta = sb("raw_delta", [2 * ROPE, 1])
        wg = sb("wg", [D, E])
        w1 = sb("w1", [D, NBLK, BLK])
        w2 = sb("w2", [D, NBLK, BLK])
        w3 = sb("w3", [BLK, NBLK, D])
        norm_w = sb("norm_w", [D, 2])
        wpj = sb("wpj", [D, 2, NPJ])
        kv_downT = sb("kv_downT", [LAT, D])
        kv_up = sb("kv_up", [LAT, 3 * KV * HD])
        wo = sb("wo", [D, 2, D])
        gate_w = sb("gate_w", [D, E])
        w01 = sb("w01", [D, 2 * D])
        b01 = sb("b01", [1, 2 * D])
        wq3 = sb("wq3", [D, H0, FN])
        wvo = sb("wvo", [LAT, H0, D])
        turn = sb("turn", [2 * ROPE, ANG])
        rank_turn = sb("rank_turn", [FE, NR])
        turns_t = sb("turns_t", [P, 2, NT, 2 * ROPE])
        dlt = sb("dlt", [2 * ROPE, 6])
        ones_row = sb("ones_row", [1, P])
        xa = sb("xa", [P, NT, D])
        xaT = sb("xaT", [D, S])
        idxT = sb("idxT", [P, 3, S])
        relu_i = sb("relu_i", [P, 2, 2, J1])
        rank_in = sb("rank_in", [P, NT, J1])
        top = sb("top", [P, NR])
        idx_u = sb("idx_u", [P, NT, NR], U32)
        idx_b = sb("idx_b", [P, NT, NR], BF)
        idx_rows = sb("idx_rows", [P, NT, P * NR], BF)
        hot_low = sb("hot_low", [P, P * NR], BF)
        k_low = sb("k_low", [P, NT, 2 * ROPE])
        k_exp = sb("k_exp", [P, NT, 2 * ROPE])
        k_log = sb("k_log", [P, NT, 2 * ROPE])
        k_feat = sb("k_feat", [P, NT, FE])
        k_mul = sb("k_mul", [P, NT, 2 * ROPE])
        k_rot = sb("k_rot", [P, NT, FN])
        k_rest = sb("k_rest", [P, 2, NT, FE])
        k_split = sb("k_split", [P, 3, NT, FE], BF)
        keysT = sb("keysT", [FN, S])
        q_low = sb("q_low", [P, NT, H0, ROPE])
        q_turn = sb("q_turn", [P, 2, NT, H0, ROPE])
        q_near_t = sb("q_near_t", [P, NT, H0, FN])
        q_far_t = sb("q_far_t", [P, NT, H0, FE])
        q_near = sb("q_near", [FN, NU, P])
        q_far = sb("q_far", [FE, NU, P])
        lat_win = sb("lat_win", [AW, NU, LAT])
        got = sb("got", [FE, 2, 4, BW])
        sc = sb("sc", [P, 2, AW + BW])
        top_s = sb("top_s", [P, 1])
        neg_top = sb("neg_top", [P, 2])
        probs = sb("probs", [P, 2, AW + BW])
        total = sb("total", [P, 2])
        inv_total = sb("inv_total", [P, 1])
        probsT = sb("probsT", [P, 2, 3, P])
        headsT = sb("headsT", [LAT, H0, S])
        pre = sb("pre", [P, NT, D])
        st6 = sb("st6", [P, 2, NT, 6])
        mv = sb("mv", [P, 2, NT, 2])
        var_e = sb("var_e", [P, 2, NT])
        rstd = sb("rstd", [P, 2, NT])
        x4 = sb("x4", [P, NT, D])
        x1 = sb("x1", [P, NT, D])
        xbT = sb("xbT", [D, S])
        lg = sb("lg", [P, NT, E])
        gt = sb("gt", [P, NT, E, E])
        eq = sb("eq", [P, NT, E, E])
        rank = sb("rank", [P, 4, NT, E])
        small = sb("small", [P, 8, NT])
        egate = sb("egate", [P, 3, NT, E])
        th = sb("th", [BLK, 2, 2, S])
        preb = sb("preb", [P, NT, D])
        x2 = sb("x2", [P, NT, D])
        ssx = sb("ssx", [P, NT])
        msx = sb("msx", [P, NT])
        rsx = sb("rsx", [P, NT])
        pj = sb("pj", [P, NT, NPJ])
        ssh = sb("ssh", [P, NT, H1 + KV])
        rsh = sb("rsh", [P, NT, H1 + KV])
        ro = sb("ro", [P, 2, NT, NQK])
        qn = sb("qn", [P, NT, H1 * HD])
        kn = sb("kn", [P, NT, KV, GH, HD])
        qT = sb("qT", [P, S])
        kbig = sb("kbig", [P, GH, S])
        v1 = sb("v1", [P, NT, KV, HD + 1])
        pr0 = sb("pr0", [P, 2, GH, S])
        pr1 = sb("pr1", [P, 2, GH, P])
        prs = sb("prs", [P, H1, WIN1])
        inv_l = sb("inv_l", [P, NT, H1])
        att = sb("att", [P, NT, D])
        attT = sb("attT", [D, S])
        x3 = sb("x3", [P, 2, NT, D])
        e01 = sb("e01", [P, 1, NT, 2 * D])
        fin = sb("fin", [P, NT, D])

        pa = ctx.enter_context(nc.psum_tensor("pa", [P, 4, 512], F))
        pb = ctx.enter_context(nc.psum_tensor("pb", [P, 4, 512], F))

        idx_dram = nc.dram_tensor("idx_dram", [NT, P * NR], BF, kind="Internal").ap()

        class Signal:
            def __init__(self, name, per_run):
                self.sem, self.n = sem(name), per_run

            def at(self, r, k=None):
                return r * self.n + (self.n if k is None else k)

        loaded = sem("loaded")
        derived_pe = sem("derived_pe")
        derived_act = sem("derived_act")
        derived_dve = sem("derived_dve")
        N = {}

        def signal(name, n):
            N[name] = Signal(name, n)
            return N[name]

        fin_free = sem("fin_free")
        x_free = sem("x_free")
        x_ok = signal("x_ok", 16)
        x_in = signal("x_in", 1)
        xaT_ps = signal("xaT_ps", 1)
        xaT_ok = signal("xaT_ok", 1)
        idx_ps = signal("idx_ps", 1)
        idxT_ok = signal("idxT_ok", 1)
        is_ps = signal("is_ps", 2)
        relu_ok = signal("relu_ok", 2)
        rin_ok = signal("rin_ok", 2)
        ib_ok = signal("ib_ok", 1)
        iw_ok = signal("iw_ok", 16)
        ir_ok = signal("ir_ok", 32)
        hot_ok = signal("hot_ok", 2)
        key_ps = signal("key_ps", 1)
        klow_ok = signal("klow_ok", 1)
        klog_ok = signal("klog_ok", 1)
        klat_ok = signal("klat_ok", 1)
        krot_ok = signal("krot_ok", 1)
        ksplit_ok = signal("ksplit_ok", 1)
        keyT_ps = signal("keyT_ps", 1)
        keysT_ok = signal("keysT_ok", 1)
        q_ps = signal("q_ps", 1)
        qlow_ok = signal("qlow_ok", 1)
        qlog_ok = signal("qlog_ok", 1)
        qT0_ps = signal("qT0_ps", 8)
        qT0_ok = signal("qT0_ok", 8)
        qf_ok = signal("qf_ok", 1)
        win_ps = signal("win_ps", 1)
        win_ok = signal("win_ok", 1)
        got_ps = signal("got_ps", NU)
        got_ok = signal("got_ok", NU)
        sc_ps = signal("sc_ps", NU)
        sc_ok = signal("sc_ok", NU)
        pr_e = signal("pr_e", NU)
        pr_ok = signal("pr_ok", NU)
        pt_ps = signal("pt_ps", NU)
        pt_ok = signal("pt_ok", NU)
        o_ps = signal("o_ps", NU)
        o_ok = signal("o_ok", 4)
        y_ps = signal("y_ps", 1)
        a_var = signal("a_var", 1)
        a_rstd = signal("a_rstd", 1)
        x1_ok = signal("x1_ok", 1)
        r_ps = signal("r_ps", 1)
        xbT_ok = signal("xbT_ok", 1)
        lg_ps = signal("lg_ps", 1)
        sh_ok = signal("sh_ok", 1)
        eg_ok = signal("eg_ok", 1)
        up_ps = signal("up_ps", NBLK // 2)
        th_ok = signal("th_ok", NBLK // 2)
        hid_ok = signal("hid_ok", NBLK // 2)
        dn_ps = signal("dn_ps", 5)
        dn_ok = signal("dn_ok", 5)
        b_var = signal("b_var", 1)
        b_rstd = signal("b_rstd", 1)
        x2_ok = signal("x2_ok", 1)
        tx_ps = signal("tx_ps", 2)
        tx_ok = signal("tx_ok", 2)
        ms_ok = signal("ms_ok", 2)
        rs_ok = signal("rs_ok", 2)
        pj_ps = signal("pj_ps", 2)
        pj_ok = signal("pj_ok", 2)
        mh_ok = signal("mh_ok", 2)
        rh_ok = signal("rh_ok", 2)
        qk_ok = signal("qk_ok", 2)
        qkT_ps = signal("qkT_ps", 2)
        qT_ok = signal("qT_ok", 2)
        kb_ok = signal("kb_ok", 2)
        s_ps = signal("s_ps", 2 * KV)
        e_ok = signal("e_ok", 2 * KV)
        m_ok = signal("m_ok", 2 * KV)
        seam_ps = signal("seam_ps", 1)
        seam_e = signal("seam_e", 1)
        seam_ok = signal("seam_ok", 1)
        pv_ps = signal("pv_ps", 2 * KV)
        att_ok = signal("att_ok", 2)
        aT_ps = signal("aT_ps", 2)
        aT_ok = signal("aT_ok", 2)
        wo_ps = signal("wo_ps", 2)
        x3_ok = signal("x3_ok", 2)
        c_var = signal("c_var", 1)
        c_rstd = signal("c_rstd", 1)
        x4_ok = signal("x4_ok", 1)
        t4_ps = signal("t4_ps", 1)
        t4_ok = signal("t4_ok", 1)
        f_ps = signal("f_ps", 1)
        fth_ok = signal("fth_ok", 1)
        fsh_ok = signal("fsh_ok", 1)
        feg_ok = signal("feg_ok", 1)
        d_var = signal("d_var", 1)
        d_rstd = signal("d_rstd", 1)
        fin_ok = signal("fin_ok", 1)
        out_ok = signal("out_ok", 16)
        chain_a = signal("chain_a", CHAIN_A)
        chain_b = signal("chain_b", CHAIN_B)
        act_a = signal("act_a", 2)
        pool_b = signal("pool_b", 4)
        ready = sem("ready")

        def bc(ap, shape):
            return ap.to_broadcast(shape) if False else ap.broadcast_to(shape)

        xv = x.rearrange("b (t p) d -> b p t d", p=P)
        ov = out.rearrange("b (t p) d -> b p t d", p=P)
        loads = []

        def plan(dst, src):
            loads.append((dst, src))

        plan(cst[:], consts)
        plan(turn_u, w["turns"][0])
        plan(turn_v, w["turns"][1])
        plan(w_dqT[:], w["w_dqT"])
        plan(w_uqT, w["w_uqT"])
        plan(w_ukT, w["w_ukT"])
        plan(w_uvT, w["w_uvT"])
        plan(w_out, w["w_out"])
        plan(w_up3, w["w_up3"])
        plan(w_key[:], w["w_key"])
        plan(idx_wq[:], w["idx_wq"])
        plan(idx_wk[:, 0:DI], w["idx_wk"])
        plan(idx_wk[:, DI:2 * DI], w["idx_wk"])
        plan(idx_w[:], w["idx_w"].rearrange("(a n) -> a n", a=1).broadcast_to([P, NI]))
        for k in range(4):
            plan(raw_delta[16 * k:16 * k + 16, :], w["raw_delta"].rearrange("(n a) -> n a", a=1))
        plan(wg[:], w["wg"])
        plan(w1[:], w["w1"])
        plan(w2[:], w["w2"])
        plan(w3[:], w["w3"])
        plan(norm_w[:], w["norm_w"])
        plan(wpj[:], w["wpj"])
        plan(kv_downT[:], w["kv_downT"])
        plan(kv_up[:], w["kv_up"])
        plan(wo[:], w["wo"])
        plan(gate_w[:], w["gate_w"])
        plan(w01[:], w["w01"])
        plan(b01[:], w["b01"])
        ALL = 16 * len(loads)

        passed = sem("passed")

        def pipeline(engine, front, back):
            def beside(r_front, r_back):
                gens = [front(r_front)] if r_front is not None else []
                gens += [back(r_back)] if r_back is not None else []
                counts = [A_STEPS] if r_front is not None else []
                counts += [B_STEPS] if r_back is not None else []
                total, done = max(counts), [0] * len(gens)
                for i in range(total):
                    for k, g in enumerate(gens):
                        while done[k] * total < counts[k] * (i + 1):
                            next(g)
                            done[k] += 1
                for g in gens:
                    assert next(g, "end") == "end"

            beside(0, None)
            with engine.Fori(0, NB - 1) as r:
                beside(r + 1, r)
            beside(None, NB - 1)

        def plain(eng):
            eng.sem_inc(passed, 1)

        def idle(steps):
            for _ in range(steps):
                yield

        def ws(u):
            return max(0, UQ * u - WIN0)

        nc.disable_value_cache = True
        block = ctx.enter_context(nc.Block())

        @block.sync
        def _(sp):
            for dst, src in loads:
                sp.dma_start(dst, src).then_inc(loaded, 16)
            with nc.sync.Fori(0, NB) as r:
                sp.wait_ge(x_free, r + 1)
                sp.dma_start(x_next[:], xv[bass.ds(r, 1)].rearrange("a p t d -> (a p) t d")).then_inc(x_ok.sem, 16)
                sp.wait_ge(ib_ok.sem, ib_ok.at(r))
                sp.dma_start(idx_dram.rearrange("t (p n) -> p t n", p=P), idx_b[:]).then_inc(iw_ok.sem, 16)
                sp.wait_ge(iw_ok.sem, iw_ok.at(r))
                sp.dma_start(idx_rows[0:J0, 0, :], idx_dram[0:1, :].broadcast_to([J0, P * NR])).then_inc(ir_ok.sem, 16)
                sp.dma_start(idx_rows[:, 1, :], idx_dram[1:2, :].broadcast_to([P, P * NR])).then_inc(ir_ok.sem, 16)
            sp.wait_ge(out_ok.sem, 16 * NB)

        @block.gpsimd
        def _(pool):
            pool.wait_ge(loaded, ALL)

            def rsqrt(dst, src, n):
                return nc.gpsimd.tensor_tensor(dst, src, c("power")[:, 0:n], ALU.pow)

            def front(r):
                pool.wait_ge(x_ok.sem, x_ok.at(r))
                plain(pool)
                nc.gpsimd.tensor_copy(xa[:], x_next[:]).then_inc(x_in.sem, 1)
                pool.wait_ge(x_in.sem, x_in.at(r))
                pool.sem_inc(x_free, 1)
                for _ in range(A_STEPS - 2):
                    yield
                pool.wait_ge(a_var.sem, a_var.at(r))
                rsqrt(rstd[:, 0], var_e[:, 0], NT).then_inc(a_rstd.sem, 1)
                yield
                yield

            def back(r):
                for _ in range(FFN_STEPS - 1):
                    yield
                pool.wait_ge(b_var.sem, b_var.at(r))
                rsqrt(rstd[:, 1], var_e[:, 1], NT).then_inc(b_rstd.sem, 1)
                yield
                for a in range(2):
                    pool.wait_ge(ms_ok.sem, ms_ok.at(r, a + 1))
                    rsqrt(rsx[:], msx[:], NT).then_inc(rs_ok.sem, 1)
                    yield
                    pool.wait_ge(mh_ok.sem, mh_ok.at(r, a + 1))
                    rsqrt(rsh[:].rearrange("p t h -> p (t h)"), ssh[:].rearrange("p t h -> p (t h)"),
                          NT * (H1 + KV)).then_inc(rh_ok.sem, 1)
                    yield
                    yield
                    for _ in range(KV + 2):
                        yield
                pool.wait_ge(c_var.sem, c_var.at(r))
                rsqrt(rstd[:, 1], var_e[:, 1], NT).then_inc(c_rstd.sem, 1)
                yield
                yield
                yield
                pool.wait_ge(d_var.sem, d_var.at(r))
                rsqrt(rstd[:, 1], var_e[:, 1], NT).then_inc(d_rstd.sem, 1)
                pool.wait_ge(fin_ok.sem, fin_ok.at(r))
                plain(pool)
                pool.dma_start(ov[bass.ds(r, 1)].rearrange("a p t d -> (a p) t d"), fin[:]).then_inc(out_ok.sem, 16)
                pool.wait_ge(out_ok.sem, out_ok.at(r))
                pool.sem_inc(fin_free, 1)
                yield

            pool.sem_inc(x_free, 1)
            pool.sem_inc(fin_free, 1)
            pipeline(nc.gpsimd, front, back)

        @block.tensor
        def _(pe):
            pe.wait_ge(loaded, ALL)
            for h in range(H0):
                last = nc.tensor.matmul(pa[0:CQ, 0, h * LAT:(h + 1) * LAT], w_uqT[:, h, :], w_ukT[:, h, :],
                                        start=True, stop=True)
            for h in range(H0):
                last = nc.tensor.matmul(pa[0:LAT, 2 + h // 4, (h % 4) * D:(h % 4 + 1) * D], w_uvT[:, h, :],
                                        w_out[:, h, :], start=True, stop=True)
            last = nc.tensor.matmul(pb[:, 0, 0:3 * KV * HD], kv_downT[:], kv_up[:], start=True, stop=True)
            last.then_inc(derived_pe, 1)
            pe.wait_ge(derived_dve, 1)
            nc.tensor.matmul(pb[:, 1, :], w_dqT[:], w_up3.rearrange("q h f -> q (h f)"), start=True, stop=True)
            for t in range(2 * NT):
                last = nc.tensor.transpose(pb[:, 3, t * 2 * ROPE:(t + 1) * 2 * ROPE], turn[:, t * P:(t + 1) * P],
                                           ident[0:2 * ROPE, 0:2 * ROPE])
            last.then_inc(derived_pe, 1)
            pe.wait_ge(derived_dve, 2)

            def tiles_T(dst, src):
                for t in range(NT):
                    last = nc.tensor.transpose(dst[:, t * P:(t + 1) * P], src[:, t, :], ident)
                return last

            def a_front(r):
                pe.wait_ge(x_in.sem, x_in.at(r))
                tiles_T(pa[:, 0, 0:S], xa).then_inc(xaT_ps.sem, 1)
                yield
                pe.wait_ge(xaT_ok.sem, xaT_ok.at(r))
                pj3 = pa[:, 1:3, :].rearrange("p b n -> p (b n)")
                nc.tensor.matmul(pj3[:, 0:S], idx_wk[:], xaT[:], start=True, stop=True)
                for k in range(2):
                    last = nc.tensor.matmul(pj3[:, (k + 1) * S:(k + 2) * S], idx_wq[:, k * P:(k + 1) * P], xaT[:],
                                            start=True, stop=True)
                last.then_inc(idx_ps.sem, 1)
                for t in range(NT):
                    last = nc.tensor.matmul(pa[:, 3, t * FE:(t + 1) * FE], xaT[:, t * P:(t + 1) * P], w_key[:],
                                            start=True, stop=True)
                last.then_inc(key_ps.sem, 1)
                yield
                yield
                pe.wait_ge(idxT_ok.sem, idxT_ok.at(r))
                pe.wait_ge(klow_ok.sem, klow_ok.at(r))
                pe.wait_ge(klat_ok.sem, klat_ok.at(r))
                pe.wait_ge(krot_ok.sem, krot_ok.at(r))
                for t, n in ((0, J0), (1, J1)):
                    for half in range(2):
                        for k in range(2):
                            lo = DI * half
                            last = nc.tensor.matmul(pa[:, 2 * t + half, k * S:k * S + n],
                                                    idxT[lo:lo + DI, 1 + k, t * P:(t + 1) * P],
                                                    idxT[lo:lo + DI, 0, 0:n], start=True, stop=True)
                    last.then_inc(is_ps.sem, 1)
                yield
                yield
                pe.wait_ge(relu_ok.sem, relu_ok.at(r))
                plain(pe)
                for t in range(NT):
                    last = nc.tensor.transpose(pa[0:FN, 0, t * P:(t + 1) * P], k_rot[:, t, :], ident)
                last.then_inc(keyT_ps.sem, 1)
                yield from idle(4)
                pe.wait_ge(keysT_ok.sem, keysT_ok.at(r))
                plain(pe)
                for u in range(NU):
                    last = nc.tensor.transpose(pa[0:AW, 1, u * LAT:(u + 1) * LAT], keysT[ROPE:FN, ws(u):ws(u) + AW],
                                               ident[ROPE:FN, ROPE:FN])
                last.then_inc(win_ps.sem, 1)
                yield
                pe.wait_ge(win_ok.sem, win_ok.at(r))
                for t in range(NT):
                    last = nc.tensor.matmul(pa[:, t, :], xaT[:, t * P:(t + 1) * P], wq3[:].rearrange("d h f -> d (h f)"),
                                            start=True, stop=True)
                last.then_inc(q_ps.sem, 1)
                yield from idle(4 + 1 + 3)
                pe.wait_ge(qf_ok.sem, qf_ok.at(r))
                for k, (src, rows) in enumerate(((q_near_t, FN), (q_far_t, FE))):
                    for t in range(NT):
                        for half in range(2):
                            n = 4 * k + 2 * t + half
                            if n >= 4:
                                pe.wait_ge(qT0_ok.sem, qT0_ok.at(r, n - 3))
                            plain(pe)
                            for h in range(4):
                                last = nc.tensor.transpose(pa[0:rows, n % 4, h * P:(h + 1) * P],
                                                           src[:, t, 4 * half + h, :], ident)
                            last.then_inc(qT0_ps.sem, 1)
                    yield
                yield

            def a_gather(r, u):
                t = u // (NU // NT)
                if u == 0:
                    pe.wait_ge(qT0_ok.sem, qT0_ok.at(r))
                    pe.wait_ge(ksplit_ok.sem, ksplit_ok.at(r))
                    pe.wait_ge(hot_ok.sem, hot_ok.at(r, 1))
                if u == NU // NT:
                    pe.wait_ge(hot_ok.sem, hot_ok.at(r))
                if u > 0:
                    pe.wait_ge(got_ok.sem, got_ok.at(r, u))
                col = (u % (NU // NT)) * UQ * NR
                parts = [(idx_rows[:, 0], 0, J0)] if t == 0 else [(hot_low, 0, P), (idx_rows[:, 1], 1, J1 - P)]
                todo = [(m, k) for m in parts for k in range(3)]
                for i, ((hot, kt, rows), k) in enumerate(todo):
                    last = nc.tensor.matmul(pa[0:FE, 0, :], k_split[0:rows, k, kt, :], hot[0:rows, col:col + UQ * NR],
                                            start=(i == 0), stop=(i == len(todo) - 1))
                last.then_inc(got_ps.sem, 1)

            def a_scores(r, u):
                if u > 0:
                    pe.wait_ge(sc_ok.sem, sc_ok.at(r, u))
                nc.tensor.matmul(pa[:, 1, 0:AW], q_near[:, u, :], keysT[:, ws(u):ws(u) + AW], start=True, stop=True)
                pe.wait_ge(got_ok.sem, got_ok.at(r, u + 1))
                for k in range(4):
                    last = nc.tensor.matmul(pa[32 * k:32 * k + 32, 1, AW:AW + BW], q_far[:, u, 32 * k:32 * k + 32],
                                            got[:, u % 2, k, :], start=True, stop=True)
                last.then_inc(sc_ps.sem, 1)

            def a_turn(r, u):
                pe.wait_ge(pr_ok.sem, pr_ok.at(r, u + 1))
                if u > 0:
                    pe.wait_ge(pt_ok.sem, pt_ok.at(r, u))
                nc.tensor.transpose(pa[:, 2, 0:P], probs[:, u % 2, 0:P], ident)
                nc.tensor.transpose(pa[:, 2, P:2 * P], probs[:, u % 2, AW:AW + BW], ident)
                for k in range(4):
                    last = nc.tensor.transpose(pa[:, 2, 2 * P + k * LAT:2 * P + (k + 1) * LAT], got[2 * ROPE:FE, u % 2, k, :],
                                               ident[2 * ROPE:FE, 2 * ROPE:FE])
                last.then_inc(pt_ps.sem, 1)

            def a_values(r, u):
                pe.wait_ge(pt_ok.sem, pt_ok.at(r, u + 1))
                if u % 4 == 0 and u:
                    pe.wait_ge(o_ok.sem, o_ok.at(r, u // 4))
                o = pa[0:LAT, 3, (u % 4) * P:(u % 4 + 1) * P]
                pt = probsT[:, u % 2]
                nc.tensor.matmul(o, lat_win[:, u, :], pt[0:AW, 0, :], start=True, stop=False, skip_group_check=True)
                for k in range(4):
                    last = nc.tensor.matmul(o[:, 32 * k:32 * k + 32], pt[:, 2, k * LAT:(k + 1) * LAT],
                                            pt[:, 1, 32 * k:32 * k + 32], start=False, stop=(k == 3), skip_group_check=True)
                last.then_inc(o_ps.sem, 1)

            def a_back(r):
                pe.wait_ge(o_ok.sem, o_ok.at(r))
                for t in range(NT):
                    for h in range(H0):
                        last = nc.tensor.matmul(pa[:, 0, t * D:(t + 1) * D], headsT[:, h, t * P:(t + 1) * P],
                                                wvo[:, h, :], start=(h == 0), stop=(h == H0 - 1))
                last.then_inc(y_ps.sem, 1)
                yield
                yield

            def ffn0(r):
                pe.wait_ge(x1_ok.sem, x1_ok.at(r))
                tiles_T(pb[:, 0, 0:S], x1).then_inc(r_ps.sem, 1)
                yield
                pe.wait_ge(xbT_ok.sem, xbT_ok.at(r))
                for t in range(NT):
                    last = nc.tensor.matmul(pb[:, 3, t * E:(t + 1) * E], xbT[:, t * P:(t + 1) * P], wg[:],
                                            start=True, stop=True)
                last.then_inc(lg_ps.sem, 1)
                yield
                for k in range(NBLK // 2):
                    if k == 1:
                        pe.wait_ge(sh_ok.sem, sh_ok.at(r))
                    if k >= 2:
                        pe.wait_ge(hid_ok.sem, hid_ok.at(r, k - 1))
                    for j in range(2):
                        bank = pb[0:BLK, 2 * (k % 2) + j, :]
                        nc.tensor.matmul(bank[:, 0:S], w1[:, 2 * k + j, :], xbT[:], start=True, stop=True)
                        last = nc.tensor.matmul(bank[:, S:2 * S], w2[:, 2 * k + j, :], xbT[:], start=True, stop=True)
                    last.then_inc(up_ps.sem, 1)
                    yield
                pe.wait_ge(hid_ok.sem, hid_ok.at(r))
                for t in range(NT):
                    for j in range(4):
                        last = nc.tensor.matmul(pb[:, 2, t * D:(t + 1) * D], hid[0:BLK, NBLK - 4 + j, t * P:(t + 1) * P],
                                                w3[:, NBLK - 4 + j, :], start=(j == 0), stop=(j == 3))
                last.then_inc(dn_ps.sem, 1)
                yield
                for t in range(NT):
                    for half in range(2):
                        n = 2 * t + half
                        if n == 3:
                            pe.wait_ge(dn_ok.sem, dn_ok.at(r, 2))
                        bank = pb[:, (0, 1, 3, 0)[n], :]
                        for e in range(4):
                            for j in range(2):
                                b = 2 * (4 * half + e) + j
                                last = nc.tensor.matmul(bank[:, e * D:(e + 1) * D], hid[0:BLK, b, t * P:(t + 1) * P],
                                                        w3[:, b, :], start=(j == 0), stop=(j == 1))
                        last.then_inc(dn_ps.sem, 1)
                        yield
                yield

            def attention1(r, a):
                src = x2 if a == 0 else x3[:, 0]
                if a == 0:
                    pe.wait_ge(x2_ok.sem, x2_ok.at(r))
                else:
                    pe.wait_ge(x3_ok.sem, x3_ok.at(r, 1))
                tiles_T(pb[:, 0, 0:S], src).then_inc(tx_ps.sem, 1)
                pe.wait_ge(tx_ok.sem, tx_ok.at(r, a + 1))
                for t in range(NT):
                    last = nc.tensor.matmul(pb[:, 1 + t, 0:NPJ], xbT[:, t * P:(t + 1) * P], wpj[:, a, :],
                                            start=True, stop=True)
                last.then_inc(pj_ps.sem, 1)
                yield
                yield
                pe.wait_ge(qk_ok.sem, qk_ok.at(r, a + 1))
                tiles_T(pb[:, 3, 0:S], qn)
                tiles_T(pb[:, 3, S:2 * S], kn[:].rearrange("p t g h d -> p t (g h d)")).then_inc(qkT_ps.sem, 1)
                pe.wait_ge(qT_ok.sem, qT_ok.at(r, a + 1))
                pe.wait_ge(kb_ok.sem, kb_ok.at(r, a + 1))
                yield

                def scores(g):
                    rows = slice(32 * g, 32 * g + 32)
                    n = a * KV + g
                    if g > 0:
                        pe.wait_ge(e_ok.sem, e_ok.at(r, n))
                    width = S if a == 0 else P
                    for h in range(GH):
                        nc.tensor.matmul(pb[:, h // 2, (h % 2) * S:(h % 2) * S + width], kbig[rows, h, 0:P],
                                         qT[rows, 0:width], start=True, stop=True)
                    for h in range(GH):
                        last = nc.tensor.matmul(pb[:, 2, h * P:(h + 1) * P], kbig[rows, h, P:S], qT[rows, P:S],
                                                start=True, stop=True)
                    last.then_inc(s_ps.sem, 1)

                def values(g):
                    n = a * KV + g
                    pe.wait_ge(m_ok.sem, m_ok.at(r, n + 1))
                    if g == 0 and a == 1:
                        pe.wait_ge(seam_ok.sem, seam_ok.at(r))
                    o = pb[:, 3, 0:NT * H1 * (HD + 1)].rearrange("p (t h d) -> p t h d", t=NT, h=H1)
                    for h in range(GH):
                        nc.tensor.matmul(o[:, 0, g * GH + h, :], pr0[:, g % 2, h, 0:P], v1[:, 0, g, :],
                                         start=True, stop=True)
                        hh = g * GH + h
                        if a == 0:
                            nc.tensor.matmul(o[:, 1, hh, :], pr0[:, g % 2, h, P:S], v1[:, 0, g, :],
                                             start=True, stop=False, skip_group_check=True)
                            last = nc.tensor.matmul(o[:, 1, hh, :], pr1[:, g % 2, h, :], v1[:, 1, g, :],
                                                    start=False, stop=True, skip_group_check=True)
                        else:
                            nc.tensor.matmul(o[:, 1, hh, :], pr1[:, g % 2, h, :], v1[:, 1, g, :],
                                             start=True, stop=False, skip_group_check=True)
                            last = nc.tensor.matmul(o[0:WIN1, 1, hh, :], prs[P - WIN1:P, hh, :], v1[P - WIN1:P, 0, g, :],
                                                    start=False, stop=True, skip_group_check=True)
                    last.then_inc(pv_ps.sem, 1)

                if a == 1:
                    plain(pe)
                    for hh in range(H1):
                        rows = slice(32 * (hh // GH), 32 * (hh // GH) + 32)
                        last = nc.tensor.matmul(pb[P - WIN1:P, hh // GH, hh % GH * WIN1:(hh % GH + 1) * WIN1],
                                                kbig[rows, hh % GH, P - WIN1:P], qT[rows, P:P + WIN1],
                                                start=True, stop=True)
                    last.then_inc(seam_ps.sem, 1)
                    pe.wait_ge(seam_e.sem, seam_e.at(r))
                scores(0)
                for g in range(KV):
                    if g + 1 < KV:
                        scores(g + 1)
                    values(g)
                    yield
                pe.wait_ge(att_ok.sem, att_ok.at(r, a + 1))
                tiles_T(pb[:, 0, 0:S], att).then_inc(aT_ps.sem, 1)
                pe.wait_ge(aT_ok.sem, aT_ok.at(r, a + 1))
                for t in range(NT):
                    last = nc.tensor.matmul(pb[:, 1, t * D:(t + 1) * D], attT[:, t * P:(t + 1) * P], wo[:, a, :],
                                            start=True, stop=True)
                last.then_inc(wo_ps.sem, 1)
                yield
                yield

            def ffn1(r):
                yield
                pe.wait_ge(x4_ok.sem, x4_ok.at(r))
                tiles_T(pb[:, 0, 0:S], x4).then_inc(t4_ps.sem, 1)
                pe.wait_ge(t4_ok.sem, t4_ok.at(r))
                for t in range(NT):
                    nc.tensor.matmul(pb[:, 1, t * E:(t + 1) * E], xbT[:, t * P:(t + 1) * P], gate_w[:],
                                     start=True, stop=True)
                for t in range(NT):
                    nc.tensor.matmul(pb[:, 2 + t, 0:2 * D], xbT[:, t * P:(t + 1) * P], w01[:], start=True, stop=False)
                    last = nc.tensor.matmul(pb[:, 2 + t, 0:2 * D], ones_row[:], b01[:], start=False, stop=True)
                last.then_inc(f_ps.sem, 1)
                yield
                yield
                yield

            def front(r):
                yield from a_front(r)
                for u in range(NU + 1):
                    if u < NU:
                        a_gather(r, u)
                    if u > 0:
                        a_turn(r, u - 1)
                    yield
                    if u < NU:
                        a_scores(r, u)
                    if u > 0:
                        a_values(r, u - 1)
                    yield
                yield from a_back(r)

            def back(r):
                yield from ffn0(r)
                yield from attention1(r, 0)
                yield from attention1(r, 1)
                yield from ffn1(r)

            pipeline(nc.tensor, front, back)

        @block.scalar
        def _(act):
            act.wait_ge(loaded, ALL)
            nc.scalar.activation(dlt[:, 0:1], raw_delta[:], ACT.Tanh, scale=0.5).then_inc(derived_act, 1)
            act.wait_ge(derived_act, 1)
            nc.scalar.activation(dlt[:, 1:2], dlt[:, 0:1], ACT.Sin, scale=3.1415925)
            nc.scalar.activation(dlt[:, 2:3], dlt[:, 0:1], ACT.Sin, scale=3.1415925 / 2).then_inc(derived_act, 1)

            def a_front(r):
                act.wait_ge(xaT_ps.sem, xaT_ps.at(r))
                nc.scalar.activation(xaT[:], pa[:, 0, 0:S], ACT.Copy).then_inc(xaT_ok.sem, 1)
                yield
                act.wait_ge(idx_ps.sem, idx_ps.at(r))
                nc.scalar.activation(idxT[:].rearrange("p k s -> p (k s)"),
                                     pa[:, 1:3, :].rearrange("p b n -> p (b n)")[:, 0:3 * S],
                                     ACT.Copy).then_inc(idxT_ok.sem, 1)
                yield
                act.wait_ge(klow_ok.sem, klow_ok.at(r))
                nc.scalar.activation(k_exp[:], k_low[:], ACT.Exp).then_inc(act_a.sem, 1)
                act.wait_ge(act_a.sem, act_a.at(r, 1))
                nc.scalar.activation(k_log[:], k_exp[:], ACT.Ln, bias=1.0).then_inc(klog_ok.sem, 1)
                yield
                for t, n in ((0, J0), (1, J1)):
                    act.wait_ge(is_ps.sem, is_ps.at(r, t + 1))
                    if t == 1:
                        act.wait_ge(rin_ok.sem, rin_ok.at(r, 1))
                    nc.scalar.activation(relu_i[:, :, :, 0:n],
                                         pa[:, 2 * t:2 * t + 2, :].rearrange("p b (k s) -> p b k s", k=2)[:, :, :, 0:n],
                                         ACT.Relu).then_inc(relu_ok.sem, 1)
                    yield
                act.wait_ge(keyT_ps.sem, keyT_ps.at(r))
                nc.scalar.activation(keysT[:], pa[0:FN, 0, 0:S], ACT.Copy).then_inc(keysT_ok.sem, 1)
                yield from idle(4)
                act.wait_ge(win_ps.sem, win_ps.at(r))
                nc.scalar.activation(lat_win[:].rearrange("p u l -> p (u l)"), pa[0:AW, 1, :],
                                     ACT.Copy).then_inc(win_ok.sem, 1)
                yield from idle(1 + 4)
                act.wait_ge(qlow_ok.sem, qlow_ok.at(r))
                nc.scalar.activation(q_low[:], q_low[:], ACT.Exp).then_inc(act_a.sem, 1)
                act.wait_ge(act_a.sem, act_a.at(r))
                nc.scalar.activation(q_low[:], q_low[:], ACT.Ln, bias=1.0)
                lat = pa[:, 0:2, :].rearrange("p t (h f) -> p t h f", f=FN)[:, :, :, ROPE:FN]
                nc.scalar.activation(q_near_t[:, :, :, ROPE:FN], lat, ACT.Copy)
                nc.scalar.activation(q_far_t[:, :, :, 2 * ROPE:FE], lat, ACT.Copy).then_inc(qlog_ok.sem, 1)
                yield from idle(1 + 3)
                for n in range(8):
                    k, t, half = n // 4, n // 2 % 2, n % 2
                    act.wait_ge(qT0_ps.sem, qT0_ps.at(r, n + 1))
                    dst, rows = ((q_near, FN), (q_far, FE))[k]
                    nc.scalar.activation(
                        dst[:, t * NU // 2:(t + 1) * NU // 2, :].rearrange("f u (c h q) -> f (u c) h q", c=4, h=H0)
                        [:, :, 4 * half:4 * half + 4, :],
                        pa[0:rows, n % 4, :].rearrange("f (h a q) -> f a h q", h=4, q=4), ACT.Copy)\
                        .then_inc(qT0_ok.sem, 1)
                    if n % 4 == 3:
                        yield
                yield

            def a_exp(r, u):
                act.wait_ge(sc_ok.sem, sc_ok.at(r, u + 1))
                if u > 1:
                    act.wait_ge(pt_ps.sem, pt_ps.at(r, u - 1))
                nc.scalar.activation(probs[:, u % 2], sc[:, u % 2], ACT.Exp, bias=neg_top[:, u % 2:u % 2 + 1], scale=SCALE0,
                                     accum_out=total[:, u % 2:u % 2 + 1]).then_inc(pr_e.sem, 1)

            def a_probsT(r, u):
                act.wait_ge(pt_ps.sem, pt_ps.at(r, u + 1))
                if u > 1:
                    act.wait_ge(o_ps.sem, o_ps.at(r, u - 1))
                nc.scalar.activation(probsT[:, u % 2].rearrange("p k n -> p (k n)"), pa[:, 2, 0:3 * P],
                                     ACT.Copy).then_inc(pt_ok.sem, 1)

            def a_out(r, k):
                act.wait_ge(o_ps.sem, o_ps.at(r, 4 * k + 4))
                nc.scalar.activation(headsT[:, :, 4 * UQ * k:4 * UQ * (k + 1)].rearrange("l h (n q) -> l h n q", q=4),
                                     pa[0:LAT, 3, :].rearrange("l (n h q) -> l h n q", h=H0, q=4), ACT.Copy).then_inc(o_ok.sem, 1)

            def ffn0(r):
                act.wait_ge(r_ps.sem, r_ps.at(r))
                nc.scalar.activation(xbT[:], pb[:, 0, 0:S], ACT.Copy).then_inc(xbT_ok.sem, 1)
                yield
                act.wait_ge(sh_ok.sem, sh_ok.at(r))
                nc.scalar.activation(egate[:, 1], egate[:, 0], ACT.Exp).then_inc(eg_ok.sem, 1)
                yield
                for k in range(NBLK // 2):
                    act.wait_ge(up_ps.sem, up_ps.at(r, k + 1))
                    if k >= 2:
                        act.wait_ge(hid_ok.sem, hid_ok.at(r, k - 1))
                    nc.scalar.activation(th[:, k % 2], pb[0:BLK, 2 * (k % 2):2 * (k % 2) + 2, 0:S], ACT.Tanh,
                                         scale=0.5).then_inc(th_ok.sem, 1)
                    yield
                for _ in range(6):
                    yield

            def attention1(r, a):
                act.wait_ge(tx_ps.sem, tx_ps.at(r, a + 1))
                nc.scalar.activation(xbT[:], pb[:, 0, 0:S], ACT.Copy).then_inc(tx_ok.sem, 1)
                yield
                act.wait_ge(pj_ps.sem, pj_ps.at(r, a + 1))
                act.wait_ge(rs_ok.sem, rs_ok.at(r, a + 1))
                for t in range(NT):
                    last = nc.scalar.activation(pj[:, t, :], pb[:, 1 + t, 0:NPJ], ACT.Copy, scale=rsx[:, t:t + 1])
                last.then_inc(pj_ok.sem, 1)
                yield
                act.wait_ge(qkT_ps.sem, qkT_ps.at(r, a + 1))
                nc.scalar.activation(qT[:], pb[:, 3, 0:S], ACT.Copy).then_inc(qT_ok.sem, 1)
                yield
                if a == 1:
                    act.wait_ge(seam_ps.sem, seam_ps.at(r))
                    nc.scalar.activation(prs[P - WIN1:P].rearrange("p (g h) q -> p g (h q)", g=KV),
                                         pb[P - WIN1:P, :, 0:GH * WIN1], ACT.Exp,
                                         scale=SCALE1).then_inc(seam_e.sem, 1)
                width = S if a == 0 else P
                for g in range(KV):
                    n = a * KV + g
                    act.wait_ge(s_ps.sem, s_ps.at(r, n + 1))
                    if g >= 2:
                        act.wait_ge(pv_ps.sem, pv_ps.at(r, n - 1))
                    nc.scalar.activation(pr0[:, g % 2, :, 0:width],
                                         pb[:, 0:2, :].rearrange("p b (k s) -> p (b k) s", k=2)[:, :, 0:width],
                                         ACT.Exp, scale=SCALE1)
                    nc.scalar.activation(pr1[:, g % 2], pb[:, 2, :].rearrange("p (h q) -> p h q", h=GH), ACT.Exp,
                                         scale=SCALE1).then_inc(e_ok.sem, 1)
                    yield
                act.wait_ge(aT_ps.sem, aT_ps.at(r, a + 1))
                nc.scalar.activation(attT[:], pb[:, 0, 0:S], ACT.Copy).then_inc(aT_ok.sem, 1)
                yield
                yield

            def ffn1(r):
                yield
                act.wait_ge(t4_ps.sem, t4_ps.at(r))
                nc.scalar.activation(xbT[:], pb[:, 0, 0:S], ACT.Copy).then_inc(t4_ok.sem, 1)
                act.wait_ge(f_ps.sem, f_ps.at(r))
                nc.scalar.activation(e01[:, 0], pb[:, 2:4, 0:2 * D], ACT.Tanh, scale=0.5).then_inc(fth_ok.sem, 1)
                act.wait_ge(fsh_ok.sem, fsh_ok.at(r))
                nc.scalar.activation(egate[:, 1], egate[:, 0], ACT.Exp).then_inc(feg_ok.sem, 1)
                yield
                yield
                yield

            def front(r):
                yield from a_front(r)
                for u in range(NU + 1):
                    if u > 0:
                        a_probsT(r, u - 1)
                    yield
                    if u < NU:
                        a_exp(r, u)
                    if u > 0 and u % 4 == 0:
                        a_out(r, u // 4 - 1)
                    yield
                yield
                yield

            def back(r):
                yield from ffn0(r)
                yield from attention1(r, 0)
                yield from attention1(r, 1)
                yield from ffn1(r)

            pipeline(nc.scalar, front, back)

        @block.vector
        def _(dve):
            V = nc.vector
            dve.wait_ge(loaded, ALL)
            V.memset(ones_row[:], 1.0)
            V.memset(v1[:], 1.0)
            V.memset(rank_turn[2 * ROPE:FE, :], 1.0)
            dve.wait_ge(derived_pe, 1)
            V.tensor_copy(w_up3[:, :, ROPE:FN], pa[0:CQ, 0, 0:H0 * LAT].rearrange("q (h l) -> q h l", h=H0))
            V.tensor_copy(wvo[:].rearrange("l h d -> l (h d)"), pa[0:LAT, 2:4, :].rearrange("l b n -> l (b n)"))
            kk = KV * HD
            V.tensor_copy(wpj[:, 0, H1 * HD:NQK], pb[:, 0, 0:kk])
            V.tensor_copy(wpj[:, 0, NQK + H1 * HD:2 * NQK], pb[:, 0, kk:2 * kk])
            V.tensor_copy(wpj[:, 0, 2 * NQK:NPJ], pb[:, 0, 2 * kk:3 * kk]).then_inc(ready, 1)
            dve.wait_ge(ready, 1)
            for a in range(2):
                V.tensor_scalar(wpj[:, a, :], wpj[:, a, :], norm_w[:, a:a + 1], None, ALU.mult)
            dve.wait_ge(derived_act, 2)
            V.tensor_tensor(dlt[:, 3:4], dlt[:, 2:3], dlt[:, 2:3], ALU.mult).then_inc(ready, 1)
            dve.wait_ge(ready, 2)
            V.tensor_scalar(dlt[:, 4:5], dlt[:, 3:4], 2.0, -1.0, ALU.mult, ALU.add).then_inc(ready, 1)
            dve.wait_ge(ready, 3)
            V.tensor_scalar(turn[:], turn_v, dlt[:, 1:2], None, ALU.mult).then_inc(ready, 1)
            dve.wait_ge(ready, 4)
            V.scalar_tensor_tensor(turn[:], turn_u, dlt[:, 4:5], turn[:], ALU.mult, ALU.add).then_inc(ready, 1)
            dve.wait_ge(ready, 5)
            V.tensor_copy(rank_turn[0:2 * ROPE, :], turn[:, 2 * S:2 * S + NR]).then_inc(derived_dve, 1)
            dve.wait_ge(derived_pe, 2)
            V.tensor_copy(wq3[:].rearrange("d h f -> d (h f)"), pb[:, 1, :])
            V.tensor_copy(turns_t[:].rearrange("p k t f -> p (k t f)"), pb[:, 3, 0:2 * NT * 2 * ROPE]).then_inc(derived_dve, 1)
            dve.wait_ge(derived_dve, 2)

            def chained(r, chain, count):
                def link(ins):
                    count[0] += 1
                    ins.then_inc(chain.sem, 1)
                    dve.wait_ge(chain.sem, chain.at(r, count[0]))
                return link

            def layer_norm(link, r, k, src, dst, var, rs, done):
                for t in range(NT):
                    last = V.bn_stats(st6[:, k, t, :], src[:, t, :])
                link(last)
                plain(dve)
                for t in range(NT):
                    last = V.bn_aggr(mv[:, k, t, :], st6[:, k, t, :])
                link(last)
                V.tensor_scalar(var_e[:, k], mv[:, k, :, 1], 1e-5, None, ALU.add).then_inc(var.sem, 1)
                yield
                dve.wait_ge(rs.sem, rs.at(r))
                for t in range(NT):
                    last = V.tensor_scalar(dst[:, t, :], src[:, t, :], mv[:, k, t, 0:1], rstd[:, k, t:t + 1],
                                           ALU.subtract, ALU.mult)
                last.then_inc(done.sem, 1)

            def a_front(r, link):
                yield
                dve.wait_ge(key_ps.sem, key_ps.at(r))
                kp = pa[:, 3, 0:NT * FE].rearrange("p (t f) -> p t f", t=NT)
                V.tensor_copy(k_feat[:, :, 2 * ROPE:FE], kp[:, :, 2 * ROPE:FE]).then_inc(klat_ok.sem, 1)
                V.tensor_scalar(k_low[:], kp[:, :, 0:2 * ROPE], 40.0, None, ALU.min).then_inc(klow_ok.sem, 1)
                yield
                dve.wait_ge(klog_ok.sem, klog_ok.at(r))
                link(V.tensor_tensor(k_feat[:, :, 0:2 * ROPE], k_log[:], kp[:, :, 0:2 * ROPE], ALU.max))
                link(V.tensor_tensor(k_mul[:], k_feat[:, :, 0:2 * ROPE], turns_t[:, 1], ALU.mult))
                V.tensor_tensor(k_rot[:, :, 0:ROPE], k_mul[:, :, 0:ROPE], k_mul[:, :, ROPE:2 * ROPE], ALU.add)
                dve.wait_ge(klat_ok.sem, klat_ok.at(r))
                V.tensor_copy(k_rot[:, :, ROPE:FN], k_feat[:, :, 2 * ROPE:FE]).then_inc(krot_ok.sem, 1)
                yield
                link(V.tensor_copy(k_split[:, 0], k_feat[:]))
                link(V.tensor_tensor(k_rest[:, 0], k_feat[:], k_split[:, 0], ALU.subtract))
                link(V.tensor_copy(k_split[:, 1], k_rest[:, 0]))
                link(V.tensor_tensor(k_rest[:, 1], k_rest[:, 0], k_split[:, 1], ALU.subtract))
                V.tensor_copy(k_split[:, 2], k_rest[:, 1]).then_inc(ksplit_ok.sem, 1)
                yield
                for t, n in ((0, J0), (1, J1)):
                    dve.wait_ge(relu_ok.sem, relu_ok.at(r, t + 1))
                    for h in range(NI):
                        before = c(f"mask_rank{t}") if h == 0 else rank_in[:, t, 0:n]
                        ins = V.scalar_tensor_tensor(rank_in[:, t, 0:n], relu_i[:, h % 2, h // 2, 0:n],
                                                     idx_w[:, h:h + 1], before, ALU.mult, ALU.add)
                        if h < NI - 1:
                            link(ins)
                    ins.then_inc(rin_ok.sem, 1)
                    yield
                    dve.wait_ge(rin_ok.sem, rin_ok.at(r, t + 1))
                    for k in range(NR // 8):
                        plain(dve)
                        link(V.max(top[:, 8 * k:8 * k + 8], rank_in[:, t, 0:n]))
                        plain(dve)
                        link(V.max_index(idx_u[:, t, 8 * k:8 * k + 8], top[:, 8 * k:8 * k + 8], rank_in[:, t, 0:n]))
                        if k < NR // 8 - 1:
                            plain(dve)
                            link(V.match_replace(rank_in[:, t, 0:n], top[:, 8 * k:8 * k + 8], rank_in[:, t, 0:n], GONE))
                            yield
                    if t == 0:
                        yield
                V.tensor_copy(idx_b[:], idx_u[:]).then_inc(ib_ok.sem, 1)
                yield
                dve.wait_ge(q_ps.sem, q_ps.at(r))
                qp = pa[:, 0:2, :].rearrange("p t (h f) -> p t h f", f=FN)[:, :, :, 0:ROPE]
                V.tensor_scalar(q_low[:], qp, 40.0, None, ALU.min).then_inc(qlow_ok.sem, 1)
                yield
                dve.wait_ge(qlog_ok.sem, qlog_ok.at(r))
                link(V.tensor_tensor(q_low[:], q_low[:], qp, ALU.max))
                half = ROPE // 2
                for k in range(2):
                    def tab(lo, n):
                        return turns_t[:, k, :, lo:lo + n].unsqueeze(2).broadcast_to([P, NT, H0, n])
                    V.tensor_tensor(q_turn[:, 0], q_low[:], tab(0, ROPE), ALU.mult)
                    V.tensor_tensor(q_turn[:, 1, :, :, 0:half], q_low[:, :, :, half:ROPE], tab(ROPE, half), ALU.mult)
                    link(V.tensor_tensor(q_turn[:, 1, :, :, half:ROPE], q_low[:, :, :, 0:half], tab(ROPE + half, half),
                                         ALU.mult))
                    yield
                    if k == 0:
                        link(V.tensor_tensor(q_near_t[:, :, :, 0:ROPE], q_turn[:, 0], q_turn[:, 1], ALU.add))
                    else:
                        for i in range(2):
                            last = V.tensor_tensor(q_far_t[:, :, :, i * ROPE:(i + 1) * ROPE], q_turn[:, 0], q_turn[:, 1],
                                                   ALU.add)
                        last.then_inc(qf_ok.sem, 1)
                yield
                yield
                yield
                dve.wait_ge(ir_ok.sem, ir_ok.at(r))
                V.tensor_scalar(idx_rows[0:J0, 0, :], idx_rows[0:J0, 0, :], c("iota", J0)[:, 0:1], None,
                                ALU.is_equal).then_inc(hot_ok.sem, 1)
                link(V.tensor_scalar(hot_low[:], idx_rows[:, 1, :], c("iota")[:, 0:1], None, ALU.is_equal))
                V.tensor_scalar(idx_rows[0:J1 - P, 1, :], idx_rows[0:J1 - P, 1, :], c("iota", J1 - P)[:, 1:2], None,
                                ALU.is_equal).then_inc(hot_ok.sem, 1)
                yield

            def a_got(r, u):
                dve.wait_ge(got_ps.sem, got_ps.at(r, u + 1))
                if u > 1:
                    dve.wait_ge(pt_ps.sem, pt_ps.at(r, u - 1))
                V.tensor_tensor(got[:, u % 2].rearrange("f k (q n) -> f (k q) n", n=NR),
                                pa[0:FE, 0, :].rearrange("f (q n) -> f q n", n=NR),
                                rank_turn[:, None, :].broadcast_to([FE, UQ, NR]), ALU.mult).then_inc(got_ok.sem, 1)

            def a_max(r, u, link):
                dve.wait_ge(sc_ps.sem, sc_ps.at(r, u + 1))
                if u > 1:
                    dve.wait_ge(pr_e.sem, pr_e.at(r, u - 1))
                plain(dve)
                link(V.tensor_tensor_reduce(out=sc[:, u % 2], in0=pa[:, 1, 0:AW + BW],
                                            in1=c("mask_first" if UQ * u < WIN0 else "mask_later"),
                                            scale=1.0, scalar=-3e38, op0=ALU.add, op1=ALU.max, accum_out=top_s[:]))
                V.tensor_scalar(neg_top[:, u % 2:u % 2 + 1], top_s[:], -SCALE0, None, ALU.mult).then_inc(sc_ok.sem, 1)

            def a_norm(r, u, link):
                dve.wait_ge(pr_e.sem, pr_e.at(r, u + 1))
                link(V.reciprocal(inv_total[:], total[:, u % 2:u % 2 + 1]))
                V.tensor_scalar(probs[:, u % 2], probs[:, u % 2], inv_total[:], None, ALU.mult).then_inc(pr_ok.sem, 1)

            def a_back(r, link):
                dve.wait_ge(y_ps.sem, y_ps.at(r))
                link(V.tensor_tensor(pre[:].rearrange("p t d -> p (t d)"), pa[:, 0, 0:S],
                                     xa[:].rearrange("p t d -> p (t d)"), ALU.add))
                yield from layer_norm(link, r, 0, pre, x1, a_var, a_rstd, x1_ok)

            def row_softmax_in(link, r, ps, done):
                link(V.tensor_copy(lg[:].rearrange("p t e -> p (t e)"), ps))
                link(V.reduce_max(small[:, 0, :], lg[:], axis=AX.X))
                V.tensor_tensor(egate[:, 0], lg[:], small[:, 0, :].unsqueeze(2).broadcast_to([P, NT, E]),
                                ALU.subtract).then_inc(done.sem, 1)

            def ffn0(r, link):
                yield
                dve.wait_ge(lg_ps.sem, lg_ps.at(r))
                row_softmax_in(link, r, pb[:, 3, 0:NT * E], sh_ok)
                for t in range(NT):
                    them = lg[:, t, None, :].broadcast_to([P, E, E])
                    me = lg[:, t, :].unsqueeze(2).broadcast_to([P, E, E])
                    V.tensor_tensor(gt[:, t], them, me, ALU.is_gt)
                    last = V.tensor_tensor(eq[:, t], them, me, ALU.is_equal)
                link(last)
                for t in range(NT):
                    last = V.tensor_tensor(eq[:, t], eq[:, t], c("before").rearrange("p (a b) -> p a b", a=E), ALU.mult)
                link(last)
                link(V.tensor_tensor(gt[:], gt[:], eq[:], ALU.add))
                link(V.reduce_sum(rank[:, 0], gt[:], axis=AX.X))
                dve.wait_ge(eg_ok.sem, eg_ok.at(r))
                link(V.scalar_tensor_tensor(rank[:, 1].rearrange("p t e -> p (t e)"),
                                            rank[:, 0].rearrange("p t e -> p (t e)"), 2.0,
                                            egate[:, 1].rearrange("p t e -> p (t e)"), ALU.is_lt, ALU.mult))
                link(V.reduce_sum(small[:, 1, :], rank[:, 1], axis=AX.X))
                link(V.reciprocal(small[:, 2, :], small[:, 1, :]))
                link(V.tensor_tensor(rank[:, 2], rank[:, 1], small[:, 2, :].unsqueeze(2).broadcast_to([P, NT, E]),
                                     ALU.mult))
                yield
                for k in range(NBLK // 2):
                    dve.wait_ge(th_ok.sem, th_ok.at(r, k + 1))
                    ps = pb[0:BLK, 2 * (k % 2):2 * (k % 2) + 2, :]
                    link(V.scalar_tensor_tensor(th[:, k % 2], th[:, k % 2], 1.0, ps[:, :, 0:S], ALU.add, ALU.mult))
                    V.scalar_tensor_tensor(hid[0:BLK, 2 * k:2 * k + 2, :], th[:, k % 2], 0.5, ps[:, :, S:2 * S],
                                           ALU.mult, ALU.mult).then_inc(hid_ok.sem, 1)
                    yield
                dve.wait_ge(dn_ps.sem, dn_ps.at(r, 1))
                ins = V.tensor_tensor(preb[:].rearrange("p t d -> p (t d)"), pb[:, 2, 0:S],
                                      x1[:].rearrange("p t d -> p (t d)"), ALU.add)
                ins.then_inc(dn_ok.sem, 1)
                dve.wait_ge(dn_ok.sem, dn_ok.at(r, 1))
                yield
                for t in range(NT):
                    for half in range(2):
                        n = 2 * t + half
                        dve.wait_ge(dn_ps.sem, dn_ps.at(r, n + 2))
                        for e in range(4):
                            ins = V.scalar_tensor_tensor(preb[:, t, :], pb[:, (0, 1, 3, 0)[n], e * D:(e + 1) * D],
                                                         rank[:, 2, t, 4 * half + e:4 * half + e + 1], preb[:, t, :],
                                                         ALU.mult, ALU.add)
                            if e < 3:
                                link(ins)
                        ins.then_inc(dn_ok.sem, 1)
                        dve.wait_ge(dn_ok.sem, dn_ok.at(r, n + 2))
                        if n < 3:
                            yield
                yield from layer_norm(link, r, 1, preb, x2, b_var, b_rstd, x2_ok)
                yield

            def attention1(r, a, link):
                src = x2 if a == 0 else x3[:, 0]
                if a == 0:
                    dve.wait_ge(x2_ok.sem, x2_ok.at(r))
                else:
                    dve.wait_ge(x3_ok.sem, x3_ok.at(r, 1))
                for t in range(NT):
                    link(V.tensor_tensor_reduce(out=att[:, t, :], in0=src[:, t, :], in1=src[:, t, :], scale=1.0, scalar=0.0,
                                                op0=ALU.mult, op1=ALU.add, accum_out=ssx[:, t:t + 1]))
                V.tensor_scalar(msx[:], ssx[:], 1.0 / D, 1e-6, ALU.mult, ALU.add).then_inc(ms_ok.sem, 1)
                yield
                dve.wait_ge(pj_ok.sem, pj_ok.at(r, a + 1))
                link(V.tensor_tensor(ro[:, 0], pj[:, :, 0:NQK], pj[:, :, 0:NQK], ALU.mult))
                link(V.reduce_sum(ssh[:], ro[:, 0].rearrange("p t (h d) -> p t h d", d=HD), axis=AX.X))
                link(V.tensor_scalar(ssh[:], ssh[:], 1.0 / HD, 1e-6, ALU.mult, ALU.add))
                V.tensor_copy(v1[:, :, :, 0:HD], pj[:, :, 2 * NQK:NPJ].rearrange("p t (g d) -> p t g d", d=HD))\
                    .then_inc(mh_ok.sem, 1)
                cos, sin = (c(n + "_" + "gl"[a]).rearrange("p (t d) -> p t d", t=NT) for n in ("cos", "sin"))
                for k, tab in enumerate((cos, sin)):
                    last = V.tensor_tensor(ro[:, k].rearrange("p t (h d) -> p t h d", d=HD),
                                           pj[:, :, k * NQK:(k + 1) * NQK].rearrange("p t (h d) -> p t h d", d=HD),
                                           tab.unsqueeze(2).broadcast_to([P, NT, H1 + KV, HD]), ALU.mult)
                link(last)
                link(V.tensor_tensor(ro[:, 0], ro[:, 0], ro[:, 1], ALU.add))
                yield
                dve.wait_ge(rh_ok.sem, rh_ok.at(r, a + 1))
                rot = ro[:, 0].rearrange("p t (h d) -> p t h d", d=HD)
                V.tensor_tensor(qn[:].rearrange("p t (h d) -> p t h d", d=HD), rot[:, :, 0:H1, :],
                                rsh[:, :, 0:H1].unsqueeze(3).broadcast_to([P, NT, H1, HD]), ALU.mult)
                link(V.tensor_tensor(rot[:, :, H1:, :], rot[:, :, H1:, :],
                                     rsh[:, :, H1:].unsqueeze(3).broadcast_to([P, NT, KV, HD]), ALU.mult))
                for t in range(NT):
                    last = V.tensor_copy(kn[:, t], rot[:, t, H1:, :].unsqueeze(2).broadcast_to([P, KV, GH, HD]))
                last.then_inc(qk_ok.sem, 1)
                dve.wait_ge(qkT_ps.sem, qkT_ps.at(r, a + 1))
                dve.wait_ge(qT_ok.sem, qT_ok.at(r, a + 1))
                V.tensor_tensor(kbig[:], pb[:, 3, S:2 * S].unsqueeze(1).broadcast_to([P, GH, S]),
                                c("headsel").unsqueeze(2).broadcast_to([P, GH, S]), ALU.mult).then_inc(kb_ok.sem, 1)
                yield
                mask = (c("causal") if a == 0 else c("local"))[:, None, :].broadcast_to([P, GH, P])
                if a == 1:
                    dve.wait_ge(seam_e.sem, seam_e.at(r))
                    V.tensor_tensor(prs[P - WIN1:P], prs[P - WIN1:P],
                                    c("seam")[P - WIN1:P, None, :].broadcast_to([WIN1, H1, WIN1]),
                                    ALU.mult).then_inc(seam_ok.sem, 1)
                for g in range(KV):
                    dve.wait_ge(e_ok.sem, e_ok.at(r, a * KV + g + 1))
                    V.tensor_tensor(pr0[:, g % 2, :, 0:P], pr0[:, g % 2, :, 0:P], mask, ALU.mult)
                    V.tensor_tensor(pr1[:, g % 2], pr1[:, g % 2], mask, ALU.mult).then_inc(m_ok.sem, 1)
                    yield
                dve.wait_ge(pv_ps.sem, pv_ps.at(r, (a + 1) * KV))
                o = pb[:, 3, 0:NT * H1 * (HD + 1)].rearrange("p (t h d) -> p t h d", t=NT, h=H1)
                link(V.reciprocal(inv_l[:], o[:, :, :, HD]))
                V.tensor_tensor(att[:].rearrange("p t (h d) -> p t h d", d=HD), o[:, :, :, 0:HD],
                                inv_l[:].unsqueeze(3).broadcast_to([P, NT, H1, HD]), ALU.mult).then_inc(att_ok.sem, 1)
                dve.wait_ge(wo_ps.sem, wo_ps.at(r, a + 1))
                V.tensor_tensor(x3[:, a], pb[:, 1, 0:S].rearrange("p (t d) -> p t d", t=NT),
                                x2[:] if a == 0 else x3[:, 0], ALU.add).then_inc(x3_ok.sem, 1)
                dve.wait_ge(x3_ok.sem, x3_ok.at(r, a + 1))
                yield
                if a == 1:
                    link(V.tensor_tensor(x3[:, 1], x3[:, 1], x2[:], ALU.add))
                    yield from layer_norm(link, r, 1, x3[:, 1], x4, c_var, c_rstd, x4_ok)
                    yield
                else:
                    yield

            def ffn1(r, link):
                dve.wait_ge(x4_ok.sem, x4_ok.at(r))
                dve.wait_ge(f_ps.sem, f_ps.at(r))
                row_softmax_in(link, r, pb[:, 1, 0:NT * E], fsh_ok)
                yield
                dve.wait_ge(fth_ok.sem, fth_ok.at(r))
                link(V.scalar_tensor_tensor(e01[:, 0], e01[:, 0], 1.0, pb[:, 2:4, 0:2 * D], ALU.add, ALU.mult))
                dve.wait_ge(feg_ok.sem, feg_ok.at(r))
                link(V.reduce_sum(small[:, 1, :], egate[:, 1], axis=AX.X))
                link(V.reciprocal(small[:, 2, :], small[:, 1, :]))
                link(V.tensor_tensor(egate[:, 2], egate[:, 1], small[:, 2, :].unsqueeze(2).broadcast_to([P, NT, E]),
                                     ALU.mult))
                wt = egate[:, 2]
                link(V.reduce_max(small[:, 3, :], wt, axis=AX.X))
                link(V.tensor_tensor(small[:, 4, :], wt[:, :, 0], small[:, 3, :], ALU.is_ge))
                link(V.tensor_tensor(rank[:, 0], wt, wt[:, :, 1:2].broadcast_to([P, NT, E]), ALU.is_gt))
                link(V.reduce_sum(small[:, 5, :], rank[:, 0], axis=AX.X))
                link(V.tensor_tensor(small[:, 6, :], wt[:, :, 0], wt[:, :, 1], ALU.is_equal))
                link(V.tensor_tensor(small[:, 5, :], small[:, 5, :], small[:, 6, :], ALU.add))
                link(V.scalar_tensor_tensor(small[:, 4, :], small[:, 4, :], 0.5, wt[:, :, 0], ALU.mult, ALU.mult))
                link(V.tensor_scalar(small[:, 5, :], small[:, 5, :], 1.0, 0.5, ALU.is_equal, ALU.mult))
                link(V.tensor_tensor(small[:, 5, :], small[:, 5, :], wt[:, :, 1], ALU.mult))
                for k in range(2):
                    for t in range(NT):
                        ins = V.scalar_tensor_tensor(preb[:, t, :], e01[:, 0, t, k * D:(k + 1) * D],
                                                     small[:, 4 + k, t:t + 1], x4[:, t, :] if k == 0 else preb[:, t, :],
                                                     ALU.mult, ALU.add)
                    link(ins)
                dve.wait_ge(fin_free, r + 1)
                yield from layer_norm(link, r, 1, preb, fin, d_var, d_rstd, fin_ok)
                yield

            def front(r):
                count = [0]
                link = chained(r, chain_a, count)
                yield from a_front(r, link)
                for u in range(NU + 1):
                    if u > 0:
                        a_norm(r, u - 1, link)
                    if u < NU:
                        a_got(r, u)
                    yield
                    if u < NU:
                        a_max(r, u, link)
                    yield
                yield from a_back(r, link)
                yield
                assert count[0] == CHAIN_A, count[0]

            def back(r):
                count = [0]
                link = chained(r, chain_b, count)
                yield from ffn0(r, link)
                yield from attention1(r, 0, link)
                yield from attention1(r, 1, link)
                yield from ffn1(r, link)
                assert count[0] == CHAIN_B, count[0]

            pipeline(nc.vector, front, back)


CHAIN_A, CHAIN_B = 74, 74
FRONT_STEPS = 13 + 2 * (NR // 8 - 1) + 2
A_STEPS = FRONT_STEPS + 2 * (NU + 1) + 2
FFN_STEPS = 2 + NBLK // 2 + 6
B_STEPS = FFN_STEPS + 2 * (5 + KV) + 1 + 3
SCALE0 = float((DH0 + ROPE) ** -0.5)
SCALE1 = float(HD ** -0.5)


def kernel(**inputs):
    import concourse.bacc as _bacc
    from concourse import mybir as _mybir
    from concourse.bass_utils import run_bass_kernel_spmd as _run

    g = {k: np.asarray(v) for k, v in inputs.items()}
    half = ROPE // 2
    heads = lambda a, n: a.reshape(a.shape[0], n, -1)
    swap_half = lambda a: np.concatenate([a[..., half:], a[..., :half]], -1)
    swap_pair = lambda a: a.reshape(a.shape[0], -1, 2)[:, :, ::-1].reshape(a.shape[0], -1)
    qr = heads(g["L0_attn_W_qr"], H0)
    kr = g["L0_attn_W_kr"]
    up3 = np.concatenate([qr, np.zeros((CQ, H0, LAT), np.float32)], -1)
    ffn_in = lambda e, s: np.concatenate([g[e].transpose(1, 0, 2).reshape(D, E * HE), g[s]], 1).reshape(D, NBLK, BLK)
    w3 = np.concatenate([g["L0_ffn_W3"].reshape(E * HE, D), g["L0_ffn_Ws3"]]).reshape(NBLK, BLK, D).transpose(1, 0, 2)
    kk = np.zeros((D, KV * HD), np.float32)
    glob = np.concatenate([g["L1_attn_g_wq"], kk, swap_pair(g["L1_attn_g_wq"]), kk, kk], 1)
    loc = np.concatenate([g["L1_attn_l_wq"], g["L1_attn_l_wk"], swap_pair(g["L1_attn_l_wq"]),
                          swap_pair(g["L1_attn_l_wk"]), g["L1_attn_l_wv"]], 1)
    tables, where, turns = constants()
    arrays = {
        "x": g["L0_attn_x"], "consts": tables, "turns": turns,
        "w_dqT": g["L0_attn_W_dq"].T, "w_uqT": heads(g["L0_attn_W_uq"], H0).transpose(2, 1, 0),
        "w_ukT": heads(g["L0_attn_W_uk"], H0).transpose(2, 1, 0),
        "w_uvT": heads(g["L0_attn_W_uv"], H0).transpose(2, 1, 0),
        "w_out": g["L0_attn_W_out"].reshape(H0, DH0, D).transpose(1, 0, 2), "w_up3": up3,
        "w_key": np.concatenate([kr, swap_half(kr), g["L0_attn_W_dkv"]], 1),
        "idx_wq": g["L0_attn_idx_wq"], "idx_wk": g["L0_attn_idx_wk"], "idx_w": g["L0_attn_idx_w"],
        "raw_delta": g["L0_attn_raw_delta"], "wg": g["L0_ffn_Wg"],
        "w1": ffn_in("L0_ffn_W1", "L0_ffn_Ws1"), "w2": ffn_in("L0_ffn_W2", "L0_ffn_Ws2"), "w3": w3,
        "norm_w": np.stack([g["L1_attn_norm1_w"], g["L1_attn_norm2_w"]], 1), "wpj": np.stack([glob, loc], 1),
        "kv_downT": g["L1_attn_g_kv_down"].T,
        "kv_up": np.concatenate([g["L1_attn_g_k_up"], swap_pair(g["L1_attn_g_k_up"]), g["L1_attn_g_v_up"]], 1),
        "wo": np.stack([g["L1_attn_g_wo"], g["L1_attn_l_wo"]], 1), "gate_w": g["L1_ffn_gate_w"],
        "w01": np.concatenate([g["L1_ffn_w0"].T, g["L1_ffn_w1"].T], 1),
        "b01": np.concatenate([g["L1_ffn_b0"], g["L1_ffn_b1"]])[None],
    }
    arrays = {"in_" + k: np.ascontiguousarray(v) for k, v in arrays.items()}
    nc = _bacc.Bacc("TRN2", target_bir_lowering=False, num_devices=1)
    aps = {k[3:]: nc.dram_tensor(k, v.shape, _mybir.dt.from_np(v.dtype), kind="ExternalInput").ap()
           for k, v in arrays.items()}
    out = nc.dram_tensor("out", (NB, S, D), _mybir.dt.float32, kind="ExternalOutput").ap()
    layers(nc, aps["x"], aps["consts"], aps, out, where)
    r = _run(nc, [arrays], core_ids=[0])
    return r.results[0]["out"]
```

```python
import numpy as np
import concourse.bass as bass
from concourse import mybir
from concourse.alu_op_type import AluOpType as ALU
from contextlib import ExitStack

NB, S, D = 8, 256, 128
P = 128
NT = S // P
H0, DH0, LAT, CQ, ROPE = 8, 64, 32, 64, 32
NI, DI = 4, 64
TOPK, WIN0 = 96, 64
NR = TOPK - WIN0
FE = 2 * ROPE + LAT
UQ = 16
NU = S // UQ
AW = WIN0 + UQ
BW = 4 * NR
J0, J1 = TOPK, S - WIN0
E, HE, HS, BLK = 8, 176, 352, 88
NBLK = (E * HE + HS) // BLK
H1, KV, HD, WIN1 = 16, 4, 8, 32
GH = H1 // KV
NQK = (H1 + KV) * HD
NPJ = 2 * NQK + KV * HD
FAR, GONE = -1e30, -3e38
FN = ROPE + LAT
ANG = 2 * S + NR


def constants():
    p = np.arange(P)
    cols = {}
    cols["ident"] = np.eye(P)
    quad, qi = p // 32, p % 4
    dq = 4 * quad + qi
    jj = np.arange(AW)
    own = np.where(np.arange(BW)[None] // NR == qi[:, None], 0.0, FAR)
    first = np.where(np.broadcast_to(jj[None] < WIN0, (P, AW)), 0.0, FAR)
    later = np.where((jj[None] >= 1 + dq[:, None]) & (jj[None] <= WIN0 + dq[:, None]), 0.0, FAR)
    cols["mask_first"] = np.concatenate([first, own], 1)
    cols["mask_later"] = np.concatenate([later, own], 1)
    for t, n in ((0, J0), (1, J1)):
        q, j = (t * P + p)[:, None], np.arange(n)[None]
        m = np.where(j > np.maximum(q, WIN0 - 1), FAR * (1 + j / 256.0), GONE)
        cols[f"mask_rank{t}"] = np.where(j <= q - WIN0, 0.0, m)
    cols["iota"] = np.stack([p, p + P], 1)
    cols["causal"] = (p[None] >= p[:, None]) * 1.0
    diff = p[None] - p[:, None]
    cols["local"] = ((diff >= 0) & (diff < WIN1)) * 1.0
    cols["seam"] = np.where(p[:, None] >= P - WIN1, (p[:, None] - (P - WIN1)) > np.arange(WIN1)[None], 0) * 1.0
    cols["before"] = np.tile((np.arange(E)[None] < np.arange(E)[:, None]).reshape(1, -1), (P, 1)) * 1.0
    cols["power"] = np.full((P, NT), -0.5)
    pos = np.arange(S).reshape(NT, P).T
    for name, base in (("g", 1e6), ("l", 1e4)):
        f = (1.0 / np.float32(base) ** (np.arange(0, HD, 2, dtype=np.float32) / HD)).astype(np.float32)
        a = (pos[:, :, None].astype(np.float32) * f).astype(np.float64)
        c, s = np.cos(a), np.sin(a)
        cols[f"cos_{name}"] = np.stack([c, c], -1).reshape(P, -1)
        cols[f"sin_{name}"] = np.stack([-s, s], -1).reshape(P, -1)
    half = ROPE // 2
    theta = (1.0 / np.float32(10000.0) ** (2.0 * np.arange(half, dtype=np.float32) / ROPE)).astype(np.float32)
    q = np.arange(S)
    near = np.where(q < WIN0, q, 2 * q - (WIN0 - 1))
    at = np.concatenate([near, q, np.arange(WIN0, TOPK)]).astype(np.float32)
    a = (theta[:, None] * at[None]).astype(np.float64)
    a = np.concatenate([a, a])
    sign = np.where(np.arange(ROPE) < half, -1.0, 1.0)[:, None]
    u = np.concatenate([np.cos(a), sign * np.sin(a)])
    v = np.concatenate([-np.sin(a), sign * np.cos(a)])
    where, at = {}, 0
    for k, c in cols.items():
        where[k] = (at, at + c.shape[1])
        at += c.shape[1]
    return np.concatenate(list(cols.values()), 1).astype(np.float32), where, np.stack([u, v]).astype(np.float32)


def blocks(a):
    return [(g, qt, kt) for g in range(KV) for qt, kt in ((0, 0), (1, 0), (1, 1)) if a == 0 or qt == kt]


def first(a):
    return sum(len(blocks(b)) for b in range(a))


def layers(nc, x, consts, w, out, where):
    F, BF, U32 = mybir.dt.float32, mybir.dt.bfloat16, mybir.dt.uint32
    ACT, AX = mybir.ActivationFunctionType, mybir.AxisListType
    ctx = ExitStack()
    with ctx:
        def sb(name, shape, dt=F):
            return ctx.enter_context(nc.sbuf_tensor(name, shape, dt))

        def sem(name):
            return ctx.enter_context(nc.semaphore(name))

        cst = sb("cst", [P, consts.shape[1]])

        def c(name, rows=P):
            return cst[0:rows, where[name][0]:where[name][1]]

        ident = c("ident")
        x_next = sb("x_next", [P, NT, D])
        hid = sb("hid", [P, NBLK, S])
        spare = hid[:].rearrange("p b s -> p (b s)")
        spare_at = [0]

        def early(rows, a, b):
            lo = spare_at[0]
            spare_at[0] += a * b
            return spare[0:rows, lo:lo + a * b].rearrange("p (a b) -> p a b", a=a)

        w_dqT = sb("w_dqT", [CQ, D])
        w_uqT = early(DH0, H0, CQ)
        w_ukT = early(DH0, H0, LAT)
        w_uvT = early(DH0, H0, LAT)
        w_out = early(DH0, H0, D)
        w_up3 = early(CQ, H0, FN)
        turn_u = early(2 * ROPE, 1, ANG)[:, 0, :]
        turn_v = early(2 * ROPE, 1, ANG)[:, 0, :]
        w_key = sb("w_key", [D, 2 * ROPE + LAT])
        idx_wq = sb("idx_wq", [D, NI * DI])
        idx_wk = sb("idx_wk", [D, 2 * DI])
        idx_w = sb("idx_w", [P, NI])
        raw_delta = sb("raw_delta", [2 * ROPE, 1])
        wg = sb("wg", [D, E])
        w1 = sb("w1", [D, NBLK, BLK])
        w2 = sb("w2", [D, NBLK, BLK])
        w3 = sb("w3", [BLK, NBLK, D])
        norm_w = sb("norm_w", [D, 2])
        wpj = sb("wpj", [D, 2, NPJ])
        kv_downT = sb("kv_downT", [LAT, D])
        kv_up = sb("kv_up", [LAT, 3 * KV * HD])
        wo = sb("wo", [D, 2, D])
        gate_w = sb("gate_w", [D, E])
        w01 = sb("w01", [D, 2 * D])
        b01 = sb("b01", [1, 2 * D])
        wq3 = sb("wq3", [D, H0, FN])
        wvo = sb("wvo", [4 * LAT, H0 // 4, D])
        turn = sb("turn", [2 * ROPE, ANG])
        rank_turn = sb("rank_turn", [FE, NR])
        turns_t = sb("turns_t", [P, 2, NT, 2 * ROPE])
        dlt = sb("dlt", [2 * ROPE, 6])
        ones_row = sb("ones_row", [1, P])
        xa = sb("xa", [P, NT, D])
        xaT = sb("xaT", [D, S])
        idxT = sb("idxT", [P, 3, S])
        relu_i = sb("relu_i", [P, 2, 2, J1])
        rank_in = sb("rank_in", [P, NT, J1])
        top = sb("top", [P, NR])
        idx_u = sb("idx_u", [P, NT, NR], U32)
        idx_b = sb("idx_b", [P, NT, NR], BF)
        idx_rows = sb("idx_rows", [P, NT, P * NR], BF)
        hot_low = sb("hot_low", [P, P * NR], BF)
        k_low = sb("k_low", [P, NT, 2 * ROPE])
        k_exp = sb("k_exp", [P, NT, 2 * ROPE])
        k_log = sb("k_log", [P, NT, 2 * ROPE])
        k_feat = sb("k_feat", [P, NT, FE])
        k_mul = sb("k_mul", [P, NT, 2 * ROPE])
        k_rot = sb("k_rot", [P, NT, FN])
        k_rest = sb("k_rest", [P, 2, NT, FE])
        k_split = sb("k_split", [P, 3, NT, FE], BF)
        keysT = sb("keysT", [FN, S])
        q_low = sb("q_low", [P, NT, H0, ROPE])
        q_turn = sb("q_turn", [P, 2, NT, H0, ROPE])
        q_turn_f = sb("q_turn_f", [P, 2, NT, H0, ROPE])
        q_near_t = sb("q_near_t", [P, NT, H0, FN])
        q_far_t = sb("q_far_t", [P, NT, H0, FE])
        q_near = sb("q_near", [FN, NU, P])
        q_far = sb("q_far", [FE, NU, P])
        lat_win = sb("lat_win", [AW, NU, LAT])
        got = sb("got", [FE, 2, 4, BW])
        sc = sb("sc", [P, 2, AW + BW])
        top_s = sb("top_s", [P, 1])
        neg_top = sb("neg_top", [P, 2])
        probs = sb("probs", [P, 2, AW + BW])
        total = sb("total", [P, 2])
        inv_total = sb("inv_total", [P, 1])
        probsT = sb("probsT", [P, 2, 3, P])
        headsT = sb("headsT", [4 * LAT, H0 // 4, S])
        pre = sb("pre", [P, NT, D])
        st6 = sb("st6", [P, 2, NT, 6])
        mv = sb("mv", [P, 2, NT, 2])
        var_e = sb("var_e", [P, 2, NT])
        rstd = sb("rstd", [P, 2, NT])
        x4 = sb("x4", [P, NT, D])
        x1 = sb("x1", [P, NT, D])
        xbT = sb("xbT", [D, S])
        lg = sb("lg", [P, NT, E])
        gt = sb("gt", [P, NT, E, E])
        eq = sb("eq", [P, NT, E, E])
        rank = sb("rank", [P, 4, NT, E])
        small = sb("small", [P, 8, NT])
        egate = sb("egate", [P, 3, NT, E])
        th = sb("th", [BLK, 2, 2, S])
        preb = sb("preb", [P, NT, D])
        x2 = sb("x2", [P, NT, D])
        ssx = sb("ssx", [P, NT])
        eps = sb("eps", [P, 1])
        msx = sb("msx", [P, NT])
        rsx = sb("rsx", [P, NT])
        pj = sb("pj", [P, NT, NPJ])
        ssh = sb("ssh", [P, NT, H1 + KV])
        rsh = sb("rsh", [P, NT, H1 + KV])
        ro = sb("ro", [P, 2, NT, NQK])
        parts = sb("parts", [P, 3, NT, NQK], BF)
        q_terms = sb("q_terms", [P, NT, GH, KV, 64], BF)
        k_terms = sb("k_terms", [P, NT, KV, 64], BF)
        qT = sb("qT", [P, 2, GH, S], BF)
        kT = sb("kT", [P, 2, S], BF)
        ident_b = sb("ident_b", [P, P], BF)
        hide = sb("hide", [P, 2, P], BF)
        v1 = sb("v1", [P, NT, KV, 32])
        pr = spare[:, 0:3 * GH * P].rearrange("p (n c) -> p n c", n=3)
        oT_both = spare[:, 3 * GH * P:(3 + NT) * GH * P].rearrange("p (t c) -> p t c", t=NT)
        prs = sb("prs", [P, H1, WIN1])
        inv_l = sb("inv_l", [P, NT * H1])
        attT = sb("attT", [D, S])
        att = sb("att", [P, NT, D])
        x3 = sb("x3", [P, 2, NT, D])
        e01 = sb("e01", [P, 1, NT, 2 * D])
        fin = sb("fin", [P, NT, D])

        pa = ctx.enter_context(nc.psum_tensor("pa", [P, 4, 512], F))
        pb = ctx.enter_context(nc.psum_tensor("pb", [P, 4, 512], F))

        idx_dram = nc.dram_tensor("idx_dram", [NT, P * NR], BF, kind="Internal").ap()

        class Signal:
            def __init__(self, name, per_run):
                self.sem, self.n = sem(name), per_run

            def at(self, r, k=None):
                return r * self.n + (self.n if k is None else k)

        loaded = sem("loaded")
        loaded_late = sem("loaded_late")
        derived_pe = sem("derived_pe")
        derived_act = sem("derived_act")
        derived_dve = sem("derived_dve")
        signal = Signal

        fin_free = sem("fin_free")
        x_ok = signal("x_ok", 16)
        x_in = signal("x_in", 1)
        xaT_ps = signal("xaT_ps", 1)
        xaT_ok = signal("xaT_ok", 1)
        idx_ps = signal("idx_ps", 1)
        idxT_ok = signal("idxT_ok", 1)
        is_ps = signal("is_ps", 2)
        relu_ok = signal("relu_ok", 2)
        rin_ok = signal("rin_ok", 2)
        ib_ok = signal("ib_ok", 1)
        iw_ok = signal("iw_ok", 16)
        ir_ok = signal("ir_ok", 32)
        hot_ok = signal("hot_ok", 2)
        key_ps = signal("key_ps", 1)
        klow_ok = signal("klow_ok", 1)
        klog_ok = signal("klog_ok", 1)
        klat_ok = signal("klat_ok", 1)
        krot_ok = signal("krot_ok", 1)
        ksplit_ok = signal("ksplit_ok", 1)
        keyT_ps = signal("keyT_ps", 1)
        keysT_ok = signal("keysT_ok", 1)
        q_ps = signal("q_ps", 1)
        qlow_ok = signal("qlow_ok", 1)
        qlog_ok = signal("qlog_ok", 1)
        qT0_ps = signal("qT0_ps", 8)
        qT0_ok = signal("qT0_ok", 8)
        qsoft_ok = signal("qsoft_ok", 1)
        qf_turned = signal("qf_turned", 1)
        qn_ok = signal("qn_ok", 1)
        qf_ok = signal("qf_ok", 1)
        win_ps = signal("win_ps", 1)
        win_ok = signal("win_ok", 1)
        got_ps = signal("got_ps", NU)
        got_ok = signal("got_ok", NU)
        sc_ps = signal("sc_ps", NU)
        sc_ok = signal("sc_ok", NU)
        pr_e = signal("pr_e", NU)
        pr_ok = signal("pr_ok", NU)
        pt_ps = signal("pt_ps", NU)
        pt_ok = signal("pt_ok", NU)
        o_ps = signal("o_ps", NU)
        o_ok = signal("o_ok", 4)
        y_ps = signal("y_ps", 1)
        a_var = signal("a_var", 1)
        a_rstd = signal("a_rstd", 1)
        x1_ok = signal("x1_ok", 1)
        r_ps = signal("r_ps", 1)
        xbT_ok = signal("xbT_ok", 1)
        lg_ps = signal("lg_ps", 1)
        sh_ok = signal("sh_ok", 1)
        eg_ok = signal("eg_ok", 1)
        up_ps = signal("up_ps", NBLK // 2)
        th_ok = signal("th_ok", NBLK // 2)
        hid_ok = signal("hid_ok", NBLK // 2)
        dn_ps = signal("dn_ps", 5)
        dn_ok = signal("dn_ok", 5)
        b_var = signal("b_var", 1)
        b_rstd = signal("b_rstd", 1)
        x2_ok = signal("x2_ok", 1)
        tx_ps = signal("tx_ps", 2)
        tx_ok = signal("tx_ok", 2)
        ms_ok = signal("ms_ok", 2)
        rs_ok = signal("rs_ok", 2)
        pj_ps = signal("pj_ps", 2)
        pj_ok = signal("pj_ok", 2)
        mh_ok = signal("mh_ok", 2)
        rh_ok = signal("rh_ok", 2)
        qk_ok = signal("qk_ok", 2)
        qkT_ps = signal("qkT_ps", 4)
        p0_ok = signal("p0_ok", 2)
        kT_ok = signal("kT_ok", 2)
        spread_ok = signal("spread_ok", 2)
        qb_ok = signal("qb_ok", 4)
        s_ps = signal("s_ps", BLOCKS)
        e_ok = signal("e_ok", BLOCKS)
        seam_ps = signal("seam_ps", 1)
        seam_e = signal("seam_e", 1)
        seam_ok = signal("seam_ok", 1)
        pv_ps = signal("pv_ps", BLOCKS)
        o0_ok = signal("o0_ok", 2)
        o1_ok = signal("o1_ok", 2)
        ot_ps = signal("ot_ps", 2)
        aT_ps = signal("aT_ps", 2)
        aT_ok = signal("aT_ok", 2)
        att_ok = signal("att_ok", 2)
        wo_ps = signal("wo_ps", 2)
        x3_ok = signal("x3_ok", 2)
        c_var = signal("c_var", 1)
        c_rstd = signal("c_rstd", 1)
        x4_ok = signal("x4_ok", 1)
        t4_ps = signal("t4_ps", 1)
        t4_ok = signal("t4_ok", 1)
        f_ps = signal("f_ps", 1)
        fth_ok = signal("fth_ok", 1)
        fsh_ok = signal("fsh_ok", 1)
        feg_ok = signal("feg_ok", 1)
        d_var = signal("d_var", 1)
        d_rstd = signal("d_rstd", 1)
        fin_ok = signal("fin_ok", 1)
        out_ok = signal("out_ok", 16)
        chain_a = signal("chain_a", CHAIN_A)
        chain_b = signal("chain_b", CHAIN_B)
        act_a = signal("act_a", 2)
        act_b = signal("act_b", 2)
        ready = sem("ready")

        xv = x.rearrange("b (t p) d -> b p t d", p=P)
        ov = out.rearrange("b (t p) d -> b p t d", p=P)
        loads = []

        def plan(dst, src):
            loads.append((dst, src))

        plan(cst[:], consts)
        plan(turn_u, w["turns"][0])
        plan(turn_v, w["turns"][1])
        plan(w_dqT[:], w["w_dqT"])
        plan(w_uqT, w["w_uqT"])
        plan(w_ukT, w["w_ukT"])
        plan(w_uvT, w["w_uvT"])
        plan(w_out, w["w_out"])
        plan(w_up3, w["w_up3"])
        plan(w_key[:], w["w_key"])
        plan(idx_wq[:], w["idx_wq"])
        plan(idx_wk[:, 0:DI], w["idx_wk"])
        plan(idx_wk[:, DI:2 * DI], w["idx_wk"])
        plan(idx_w[:], w["idx_w"].rearrange("(a n) -> a n", a=1).broadcast_to([P, NI]))
        for k in range(4):
            plan(raw_delta[16 * k:16 * k + 16, :], w["raw_delta"].rearrange("(n a) -> n a", a=1))
        plan(wg[:], w["wg"])
        plan(norm_w[:], w["norm_w"])
        plan(wpj[:], w["wpj"])
        plan(kv_downT[:], w["kv_downT"])
        plan(kv_up[:], w["kv_up"])
        late_loads = [(w1[:], w["w1"]), (w2[:], w["w2"]), (w3[:], w["w3"]), (wo[:], w["wo"]), (gate_w[:], w["gate_w"]),
                      (w01[:], w["w01"]), (b01[:], w["b01"])]
        ALL = 16 * len(loads)

        passed = sem("passed")

        def pipeline(engine, front, back):
            def beside(r_front, r_back):
                gens = [front(r_front)] if r_front is not None else []
                gens += [back(r_back)] if r_back is not None else []
                weights = [A_WEIGHTS] if r_front is not None else []
                weights += [B_WEIGHTS] if r_back is not None else []
                done = [0] * len(gens)
                for _ in range(sum(len(w) for w in weights)):
                    k = min((k for k in range(len(gens)) if done[k] < len(weights[k])),
                            key=lambda k: sum(weights[k][:done[k] + 1]) / sum(weights[k]))
                    next(gens[k])
                    done[k] += 1
                for g in gens:
                    assert next(g, "end") == "end"

            beside(0, None)
            if engine is nc.tensor:
                nc.tensor.wait_ge(loaded_late, 16 * len(late_loads))
            with engine.Fori(0, NB - 1) as r:
                beside(r + 1, r)
            beside(None, NB - 1)

        def plain(eng):
            eng.sem_inc(passed, 1)

        def idle(steps):
            for _ in range(steps):
                yield

        def spread_queries(copy, n, t):
            lo, hi = ((0, 3), (3, 5), (5, 6))[n]
            dst = q_terms[:, t].rearrange("p h g (c d) -> p h g c d", d=HD)
            for g in range(KV):
                last = copy(dst[:, :, g, lo:hi, :], parts[:, n, t, g * GH * HD:(g + 1) * GH * HD]
                            .rearrange("p (h d) -> p h d", d=HD).unsqueeze(2).broadcast_to([P, GH, hi - lo, HD]))
            return last

        def turn_queries(engine, dst, k):
            half = ROPE // 2

            def tab(lo, n):
                return turns_t[:, k, :, lo:lo + n].unsqueeze(2).broadcast_to([P, NT, H0, n])
            engine.tensor_tensor(dst[:, 0], q_low[:], tab(0, ROPE), ALU.mult)
            engine.tensor_tensor(dst[:, 1, :, :, 0:half], q_low[:, :, :, half:ROPE], tab(ROPE, half), ALU.mult)
            return engine.tensor_tensor(dst[:, 1, :, :, half:ROPE], q_low[:, :, :, 0:half], tab(ROPE + half, half),
                                        ALU.mult)

        def spread_keys(copy, n):
            for k in ((0, 3, 5), (1, 4), (2,))[n]:
                last = copy(k_terms[:, :, :, k * HD:(k + 1) * HD],
                            parts[:, n, :, H1 * HD:].rearrange("p t (g d) -> p t g d", d=HD))
            return last

        def oT(t):
            return oT_both[:, t, :]

        def ws(u):
            return max(0, UQ * u - WIN0)

        nc.disable_value_cache = True
        block = ctx.enter_context(nc.Block())

        @block.sync
        def _(sp):
            for dst, src in loads:
                sp.dma_start(dst, src).then_inc(loaded, 16)

            def load_row(r):
                sp.dma_start(x_next[:], xv[r].rearrange("a p t d -> (a p) t d")).then_inc(x_ok.sem, 16)

            def spread_indices(r):
                sp.wait_ge(ib_ok.sem, ib_ok.at(r))
                sp.dma_start(idx_dram.rearrange("t (p n) -> p t n", p=P), idx_b[:]).then_inc(iw_ok.sem, 16)
                sp.wait_ge(iw_ok.sem, iw_ok.at(r))
                sp.dma_start(idx_rows[0:J0, 0, :], idx_dram[0:1, :].broadcast_to([J0, P * NR])).then_inc(ir_ok.sem, 16)
                sp.dma_start(idx_rows[:, 1, :], idx_dram[1:2, :].broadcast_to([P, P * NR])).then_inc(ir_ok.sem, 16)

            load_row(slice(0, 1))
            for dst, src in late_loads:
                sp.dma_start(dst, src).then_inc(loaded_late, 16)
            with nc.sync.Fori(0, NB - 1) as r:
                sp.wait_ge(x_in.sem, x_in.at(r))
                load_row(bass.ds(r + 1, 1))
                spread_indices(r)
            spread_indices(NB - 1)
            sp.wait_ge(out_ok.sem, 16 * NB)

        @block.gpsimd
        def _(pool):
            pool.wait_ge(loaded, ALL)

            def rsqrt(dst, src):
                return nc.gpsimd.tensor_tensor(dst, src, c("power"), ALU.pow)

            def front(r):
                yield from idle(FRONT_STEPS - 5)
                pool.wait_ge(qsoft_ok.sem, qsoft_ok.at(r))
                turn_queries(nc.gpsimd, q_turn_f, 1).then_inc(qf_turned.sem, 1)
                pool.wait_ge(qf_turned.sem, qf_turned.at(r))
                for i in range(2):
                    last = nc.gpsimd.tensor_tensor(q_far_t[:, :, :, i * ROPE:(i + 1) * ROPE], q_turn_f[:, 0],
                                                   q_turn_f[:, 1], ALU.add)
                last.then_inc(qf_ok.sem, 1)
                yield from idle(A_STEPS - 2 - (FRONT_STEPS - 5))
                pool.wait_ge(a_var.sem, a_var.at(r))
                rsqrt(rstd[:, 0], var_e[:, 0]).then_inc(a_rstd.sem, 1)
                yield
                yield

            def back(r):
                yield from idle(FFN_STEPS - 1)
                pool.wait_ge(b_var.sem, b_var.at(r))
                rsqrt(rstd[:, 1], var_e[:, 1]).then_inc(b_rstd.sem, 1)
                yield
                for a in range(2):
                    pool.wait_ge(ms_ok.sem, ms_ok.at(r, a + 1))
                    rsqrt(rsx[:], msx[:]).then_inc(rs_ok.sem, 1)
                    yield from idle(ATT_STEPS[a] - 2 * a)
                pool.wait_ge(c_var.sem, c_var.at(r))
                rsqrt(rstd[:, 1], var_e[:, 1]).then_inc(c_rstd.sem, 1)
                yield from idle(2 + 3)
                pool.wait_ge(d_var.sem, d_var.at(r))
                rsqrt(rstd[:, 1], var_e[:, 1]).then_inc(d_rstd.sem, 1)
                yield
                pool.wait_ge(fin_ok.sem, fin_ok.at(r))
                plain(pool)
                pool.dma_start(ov[bass.ds(r, 1)].rearrange("a p t d -> (a p) t d"), fin[:]).then_inc(out_ok.sem, 16)
                pool.wait_ge(out_ok.sem, out_ok.at(r))
                pool.sem_inc(fin_free, 1)
                yield

            pool.sem_inc(fin_free, 1)
            pipeline(nc.gpsimd, front, back)

        @block.tensor
        def _(pe):
            pe.wait_ge(loaded, ALL)
            for h in range(H0):
                last = nc.tensor.matmul(pa[0:CQ, 0, h * LAT:(h + 1) * LAT], w_uqT[:, h, :], w_ukT[:, h, :],
                                        start=True, stop=True)
            for h in range(H0):
                last = nc.tensor.matmul(pa[0:LAT, 2 + h // 4, (h % 4) * D:(h % 4 + 1) * D], w_uvT[:, h, :],
                                        w_out[:, h, :], start=True, stop=True)
            last = nc.tensor.matmul(pb[:, 0, 0:3 * KV * HD], kv_downT[:], kv_up[:], start=True, stop=True)
            last.then_inc(derived_pe, 1)
            pe.wait_ge(derived_dve, 1)
            nc.tensor.matmul(pb[:, 1, :], w_dqT[:], w_up3.rearrange("q h f -> q (h f)"), start=True, stop=True)
            for t in range(2 * NT):
                last = nc.tensor.transpose(pb[:, 3, t * 2 * ROPE:(t + 1) * 2 * ROPE], turn[:, t * P:(t + 1) * P],
                                           ident[0:2 * ROPE, 0:2 * ROPE])
            last.then_inc(derived_pe, 1)
            pe.wait_ge(derived_dve, 2)

            def tiles_T(dst, src):
                for t in range(NT):
                    last = nc.tensor.transpose(dst[:, t * P:(t + 1) * P], src[:, t, :], ident)
                return last

            def a_front(r):
                yield
                pe.wait_ge(x_in.sem, x_in.at(r))
                tiles_T(pa[:, 0, 0:S], xa).then_inc(xaT_ps.sem, 1)
                yield
                pe.wait_ge(xaT_ok.sem, xaT_ok.at(r))
                pj3 = pa[:, 1:3, :].rearrange("p b n -> p (b n)")
                nc.tensor.matmul(pj3[:, 0:S], idx_wk[:], xaT[:], start=True, stop=True)
                for k in range(2):
                    last = nc.tensor.matmul(pj3[:, (k + 1) * S:(k + 2) * S], idx_wq[:, k * P:(k + 1) * P], xaT[:],
                                            start=True, stop=True)
                last.then_inc(idx_ps.sem, 1)
                for t in range(NT):
                    last = nc.tensor.matmul(pa[:, 3, t * FE:(t + 1) * FE], xaT[:, t * P:(t + 1) * P], w_key[:],
                                            start=True, stop=True)
                last.then_inc(key_ps.sem, 1)
                yield
                yield
                pe.wait_ge(idxT_ok.sem, idxT_ok.at(r))
                pe.wait_ge(klow_ok.sem, klow_ok.at(r))
                pe.wait_ge(klat_ok.sem, klat_ok.at(r))
                pe.wait_ge(krot_ok.sem, krot_ok.at(r))
                for t, n in ((0, J0), (1, J1)):
                    for half in range(2):
                        for k in range(2):
                            lo = DI * half
                            last = nc.tensor.matmul(pa[:, 2 * t + half, k * S:k * S + n],
                                                    idxT[lo:lo + DI, 1 + k, t * P:(t + 1) * P],
                                                    idxT[lo:lo + DI, 0, 0:n], start=True, stop=True)
                    last.then_inc(is_ps.sem, 1)
                yield
                yield
                pe.wait_ge(relu_ok.sem, relu_ok.at(r))
                plain(pe)
                for t in range(NT):
                    last = nc.tensor.transpose(pa[0:FN, 0, t * P:(t + 1) * P], k_rot[:, t, :], ident)
                last.then_inc(keyT_ps.sem, 1)
                yield from idle(4)
                pe.wait_ge(keysT_ok.sem, keysT_ok.at(r))
                plain(pe)
                for u in range(NU):
                    last = nc.tensor.transpose(pa[0:AW, 1, u * LAT:(u + 1) * LAT], keysT[ROPE:FN, ws(u):ws(u) + AW],
                                               ident[ROPE:FN, ROPE:FN])
                last.then_inc(win_ps.sem, 1)
                yield
                pe.wait_ge(win_ok.sem, win_ok.at(r))
                for t in range(NT):
                    last = nc.tensor.matmul(pa[:, t, :], xaT[:, t * P:(t + 1) * P], wq3[:].rearrange("d h f -> d (h f)"),
                                            start=True, stop=True)
                last.then_inc(q_ps.sem, 1)
                yield from idle(NR // 8 + 3)
                for k, (src, rows, ready_q) in enumerate(((q_near_t, FN, qn_ok), (q_far_t, FE, qf_ok))):
                    pe.wait_ge(ready_q.sem, ready_q.at(r))
                    for t in range(NT):
                        for half in range(2):
                            n = 4 * k + 2 * t + half
                            if n >= 4:
                                pe.wait_ge(qT0_ok.sem, qT0_ok.at(r, n - 3))
                            plain(pe)
                            for h in range(4):
                                last = nc.tensor.transpose(pa[0:rows, n % 4, h * P:(h + 1) * P],
                                                           src[:, t, 4 * half + h, :], ident)
                            last.then_inc(qT0_ps.sem, 1)
                    yield
                yield

            def a_gather(r, u):
                t = u // (NU // NT)
                if u == 0:
                    pe.wait_ge(qT0_ok.sem, qT0_ok.at(r))
                    pe.wait_ge(ksplit_ok.sem, ksplit_ok.at(r))
                    pe.wait_ge(hot_ok.sem, hot_ok.at(r, 1))
                if u == NU // NT:
                    pe.wait_ge(hot_ok.sem, hot_ok.at(r))
                if u > 0:
                    pe.wait_ge(got_ok.sem, got_ok.at(r, u))
                col = (u % (NU // NT)) * UQ * NR
                parts = [(idx_rows[:, 0], 0, J0)] if t == 0 else [(hot_low, 0, P), (idx_rows[:, 1], 1, J1 - P)]
                if (u + 1) * UQ - WIN0 <= P:
                    parts = parts[:1]
                todo = [(m, k) for m in parts for k in range(3)]
                for i, ((hot, kt, rows), k) in enumerate(todo):
                    last = nc.tensor.matmul(pa[0:FE, 0, :], k_split[0:rows, k, kt, :], hot[0:rows, col:col + UQ * NR],
                                            start=(i == 0), stop=(i == len(todo) - 1))
                last.then_inc(got_ps.sem, 1)

            def a_scores(r, u):
                if u > 0:
                    pe.wait_ge(sc_ok.sem, sc_ok.at(r, u))
                nc.tensor.matmul(pa[:, 1, 0:AW], q_near[:, u, :], keysT[:, ws(u):ws(u) + AW], start=True, stop=True)
                pe.wait_ge(got_ok.sem, got_ok.at(r, u + 1))
                for k in range(4):
                    last = nc.tensor.matmul(pa[32 * k:32 * k + 32, 1, AW:AW + BW], q_far[:, u, 32 * k:32 * k + 32],
                                            got[:, u % 2, k, :], start=True, stop=True)
                last.then_inc(sc_ps.sem, 1)

            def a_turn(r, u):
                pe.wait_ge(pr_ok.sem, pr_ok.at(r, u + 1))
                if u > 0:
                    pe.wait_ge(pt_ok.sem, pt_ok.at(r, u))
                nc.tensor.transpose(pa[:, 2, 0:P], probs[:, u % 2, 0:P], ident)
                nc.tensor.transpose(pa[:, 2, P:2 * P], probs[:, u % 2, AW:AW + BW], ident)
                for k in range(4):
                    last = nc.tensor.transpose(pa[:, 2, 2 * P + k * LAT:2 * P + (k + 1) * LAT], got[2 * ROPE:FE, u % 2, k, :],
                                               ident[2 * ROPE:FE, 2 * ROPE:FE])
                last.then_inc(pt_ps.sem, 1)

            def a_values(r, u):
                pe.wait_ge(pt_ok.sem, pt_ok.at(r, u + 1))
                if u % 4 == 0 and u:
                    pe.wait_ge(o_ok.sem, o_ok.at(r, u // 4))
                o = pa[0:LAT, 3, (u % 4) * P:(u % 4 + 1) * P]
                pt = probsT[:, u % 2]
                nc.tensor.matmul(o, lat_win[:, u, :], pt[0:AW, 0, :], start=True, stop=False, skip_group_check=True)
                for k in range(4):
                    last = nc.tensor.matmul(o[:, 32 * k:32 * k + 32], pt[:, 2, k * LAT:(k + 1) * LAT],
                                            pt[:, 1, 32 * k:32 * k + 32], start=False, stop=(k == 3), skip_group_check=True)
                last.then_inc(o_ps.sem, 1)

            def a_back(r):
                pe.wait_ge(o_ok.sem, o_ok.at(r))
                for t in range(NT):
                    for k in range(H0 // 4):
                        last = nc.tensor.matmul(pa[:, 0, t * D:(t + 1) * D], headsT[:, k, t * P:(t + 1) * P],
                                                wvo[:, k, :], start=(k == 0), stop=(k == H0 // 4 - 1))
                last.then_inc(y_ps.sem, 1)
                yield
                yield

            def ffn0(r):
                pe.wait_ge(x1_ok.sem, x1_ok.at(r))
                tiles_T(pb[:, 0, 0:S], x1).then_inc(r_ps.sem, 1)
                yield
                pe.wait_ge(xbT_ok.sem, xbT_ok.at(r))
                for t in range(NT):
                    last = nc.tensor.matmul(pb[:, 3, t * E:(t + 1) * E], xbT[:, t * P:(t + 1) * P], wg[:],
                                            start=True, stop=True)
                last.then_inc(lg_ps.sem, 1)
                yield
                for k in range(NBLK // 2):
                    if k == 1:
                        pe.wait_ge(sh_ok.sem, sh_ok.at(r))
                    if k >= 2:
                        pe.wait_ge(hid_ok.sem, hid_ok.at(r, k - 1))
                    for j in range(2):
                        bank = pb[0:BLK, 2 * (k % 2) + j, :]
                        nc.tensor.matmul(bank[:, 0:S], w1[:, 2 * k + j, :], xbT[:], start=True, stop=True)
                        last = nc.tensor.matmul(bank[:, S:2 * S], w2[:, 2 * k + j, :], xbT[:], start=True, stop=True)
                    last.then_inc(up_ps.sem, 1)
                    yield
                pe.wait_ge(hid_ok.sem, hid_ok.at(r))
                for t in range(NT):
                    for j in range(4):
                        last = nc.tensor.matmul(pb[:, 2, t * D:(t + 1) * D], hid[0:BLK, NBLK - 4 + j, t * P:(t + 1) * P],
                                                w3[:, NBLK - 4 + j, :], start=(j == 0), stop=(j == 3))
                last.then_inc(dn_ps.sem, 1)
                yield
                for t in range(NT):
                    for half in range(2):
                        n = 2 * t + half
                        if n == 3:
                            pe.wait_ge(dn_ok.sem, dn_ok.at(r, 2))
                        bank = pb[:, (0, 1, 3, 0)[n], :]
                        for e in range(4):
                            for j in range(2):
                                b = 2 * (4 * half + e) + j
                                last = nc.tensor.matmul(bank[:, e * D:(e + 1) * D], hid[0:BLK, b, t * P:(t + 1) * P],
                                                        w3[:, b, :], start=(j == 0), stop=(j == 1))
                        last.then_inc(dn_ps.sem, 1)
                        yield
                yield

            def attention1(r, a):
                src = x2 if a == 0 else x3[:, 0]
                if a == 0:
                    pe.wait_ge(x2_ok.sem, x2_ok.at(r))
                else:
                    pe.wait_ge(x3_ok.sem, x3_ok.at(r, 1))
                tiles_T(pb[:, 0, 0:S], src).then_inc(tx_ps.sem, 1)
                yield
                pe.wait_ge(tx_ok.sem, tx_ok.at(r, a + 1))
                for t in range(NT):
                    last = nc.tensor.matmul(pb[:, 1 + t, 0:NPJ], xbT[:, t * P:(t + 1) * P], wpj[:, a, :],
                                            start=True, stop=True)
                last.then_inc(pj_ps.sem, 1)
                yield from idle(3)
                pe.wait_ge(qk_ok.sem, qk_ok.at(r, a + 1))
                pe.wait_ge(spread_ok.sem, spread_ok.at(r, a + 1))

                def turn_tile(t, pair, bank):
                    for h in range(GH):
                        last = nc.tensor.matmul(pb[:, bank, h * P:(h + 1) * P],
                                                q_terms[:, t, h, 2 * pair:2 * pair + 2, :].rearrange("p g c -> p (g c)"),
                                                ident_b[:], start=True, stop=True)
                    return last

                turn_tile(0, 0, 0)
                turn_tile(0, 1, 1)
                turn_tile(1, 0, 2)
                for pair in range(2):
                    for t in range(NT):
                        last = nc.tensor.matmul(pb[:, 3, pair * S + t * P:pair * S + (t + 1) * P],
                                                k_terms[:, t, 2 * pair:2 * pair + 2, :].rearrange("p g c -> p (g c)"),
                                                ident_b[:], start=True, stop=True)
                last.then_inc(qkT_ps.sem, 1)
                yield
                pe.wait_ge(qb_ok.sem, qb_ok.at(r, 2 * a + 1))
                turn_tile(1, 1, 0).then_inc(qkT_ps.sem, 1)
                yield
                pe.wait_ge(qb_ok.sem, qb_ok.at(r, 2 * a + 2))
                pe.wait_ge(kT_ok.sem, kT_ok.at(r, a + 1))
                todo = blocks(a)

                def scores(i):
                    g, qt, kt = todo[i]
                    rows = slice(64 * (g % 2), 64 * (g % 2) + 64)
                    if i >= 2:
                        pe.wait_ge(e_ok.sem, e_ok.at(r, first(a) + i - 1))
                    last = nc.tensor.matmul(pb[:, i % 2, :], kT[rows, g // 2, kt * P:(kt + 1) * P],
                                            qT[rows, g // 2, :, qt * P:(qt + 1) * P], start=True, stop=(qt != kt),
                                            skip_group_check=True)
                    if qt == kt:
                        last = nc.tensor.matmul(pb[:, i % 2, :], ident_b[:],
                                                hide[:, a, None, :].broadcast_to([P, GH, P]), start=False, stop=True,
                                                skip_group_check=True)
                    last.then_inc(s_ps.sem, 1)

                def values(i):
                    g, qt, kt = todo[i]
                    rows = slice(32 * g, 32 * g + 32)
                    pe.wait_ge(e_ok.sem, e_ok.at(r, first(a) + i + 1))
                    last = nc.tensor.matmul(pb[rows, 2 + qt, :], v1[:, kt, g, :], pr[:, i % 3, :],
                                            start=(qt == 0 or a == 1 or kt == 0), stop=(qt == kt and (qt == 0 or a == 0)),
                                            skip_group_check=True)
                    if a == 1 and qt == 1:
                        if g == 0:
                            pe.wait_ge(seam_ok.sem, seam_ok.at(r))
                        plain(pe)
                        last = nc.tensor.matmul(pb[rows, 3, :].rearrange("p (h q) -> p h q", h=GH)[:, :, 0:WIN1],
                                                v1[P - WIN1:P, 0, g, :],
                                                prs[P - WIN1:P, g * GH:(g + 1) * GH, :], start=False, stop=True,
                                                skip_group_check=True)
                    last.then_inc(pv_ps.sem, 1)

                if a == 1:
                    plain(pe)
                    for g in range(KV):
                        rows = slice(64 * (g % 2), 64 * (g % 2) + 64)
                        last = nc.tensor.matmul(pb[P - WIN1:P, g, 0:GH * WIN1], kT[rows, g // 2, P - WIN1:P],
                                                qT[rows, g // 2, :, P:P + WIN1], start=True, stop=True)
                    last.then_inc(seam_ps.sem, 1)
                    yield
                    pe.wait_ge(seam_e.sem, seam_e.at(r))
                scores(0)
                scores(1)
                yield
                for i in range(len(todo)):
                    values(i)
                    if i + 2 < len(todo):
                        scores(i + 2)
                    if i % 2:
                        yield
                for t in range(NT):
                    done = (o0_ok, o1_ok)[t]
                    pe.wait_ge(done.sem, done.at(r, a + 1))
                    plain(pe)
                    for h in range(GH):
                        last = nc.tensor.transpose(pb[:, t, h * P:(h + 1) * P], oT(t)[:, h * P:(h + 1) * P], ident)
                last.then_inc(ot_ps.sem, 1)
                yield
                pe.wait_ge(att_ok.sem, att_ok.at(r, a + 1))
                tiles_T(pb[:, 3, 0:S], att).then_inc(aT_ps.sem, 1)
                yield
                pe.wait_ge(aT_ok.sem, aT_ok.at(r, a + 1))
                for t in range(NT):
                    last = nc.tensor.matmul(pb[:, 2, t * D:(t + 1) * D], attT[:, t * P:(t + 1) * P], wo[:, a, :],
                                            start=True, stop=True)
                last.then_inc(wo_ps.sem, 1)
                yield from idle(1 + a)

            def ffn1(r):
                pe.wait_ge(x4_ok.sem, x4_ok.at(r))
                tiles_T(pb[:, 0, 0:S], x4).then_inc(t4_ps.sem, 1)
                yield
                pe.wait_ge(t4_ok.sem, t4_ok.at(r))
                for t in range(NT):
                    nc.tensor.matmul(pb[:, 1, t * E:(t + 1) * E], xbT[:, t * P:(t + 1) * P], gate_w[:],
                                     start=True, stop=True)
                for t in range(NT):
                    nc.tensor.matmul(pb[:, 2 + t, 0:2 * D], xbT[:, t * P:(t + 1) * P], w01[:], start=True, stop=False)
                    last = nc.tensor.matmul(pb[:, 2 + t, 0:2 * D], ones_row[:], b01[:], start=False, stop=True)
                last.then_inc(f_ps.sem, 1)
                yield from idle(4)

            def front(r):
                yield from a_front(r)
                for u in range(NU + 2):
                    if u < NU:
                        a_gather(r, u)
                    if u > 1:
                        a_values(r, u - 2)
                    yield
                    if 0 < u <= NU:
                        a_turn(r, u - 1)
                    if u < NU:
                        a_scores(r, u)
                    if u <= NU:
                        yield
                yield from a_back(r)

            def back(r):
                yield from ffn0(r)
                yield from attention1(r, 0)
                yield from attention1(r, 1)
                yield from ffn1(r)

            pipeline(nc.tensor, front, back)

        @block.scalar
        def _(act):
            act.wait_ge(loaded, ALL)
            nc.scalar.activation(dlt[:, 0:1], raw_delta[:], ACT.Tanh, scale=0.5).then_inc(derived_act, 1)
            act.wait_ge(derived_act, 1)
            nc.scalar.activation(dlt[:, 1:2], dlt[:, 0:1], ACT.Sin, scale=3.1415925)
            nc.scalar.activation(dlt[:, 2:3], dlt[:, 0:1], ACT.Sin, scale=3.1415925 / 2).then_inc(derived_act, 1)

            def a_front(r):
                yield
                act.wait_ge(xaT_ps.sem, xaT_ps.at(r))
                nc.scalar.activation(xaT[:], pa[:, 0, 0:S], ACT.Copy).then_inc(xaT_ok.sem, 1)
                yield
                act.wait_ge(idx_ps.sem, idx_ps.at(r))
                nc.scalar.activation(idxT[:].rearrange("p k s -> p (k s)"),
                                     pa[:, 1:3, :].rearrange("p b n -> p (b n)")[:, 0:3 * S],
                                     ACT.Copy).then_inc(idxT_ok.sem, 1)
                yield
                act.wait_ge(klow_ok.sem, klow_ok.at(r))
                nc.scalar.activation(k_exp[:], k_low[:], ACT.Exp).then_inc(act_a.sem, 1)
                act.wait_ge(act_a.sem, act_a.at(r, 1))
                nc.scalar.activation(k_log[:], k_exp[:], ACT.Ln, bias=1.0).then_inc(klog_ok.sem, 1)
                yield
                for t, n in ((0, J0), (1, J1)):
                    act.wait_ge(is_ps.sem, is_ps.at(r, t + 1))
                    if t == 1:
                        act.wait_ge(rin_ok.sem, rin_ok.at(r, 1))
                    nc.scalar.activation(relu_i[:, :, :, 0:n],
                                         pa[:, 2 * t:2 * t + 2, :].rearrange("p b (k s) -> p b k s", k=2)[:, :, :, 0:n],
                                         ACT.Relu).then_inc(relu_ok.sem, 1)
                    yield
                act.wait_ge(keyT_ps.sem, keyT_ps.at(r))
                nc.scalar.activation(keysT[:], pa[0:FN, 0, 0:S], ACT.Copy).then_inc(keysT_ok.sem, 1)
                yield from idle(4)
                act.wait_ge(win_ps.sem, win_ps.at(r))
                nc.scalar.activation(lat_win[:].rearrange("p u l -> p (u l)"), pa[0:AW, 1, :],
                                     ACT.Copy).then_inc(win_ok.sem, 1)
                yield from idle(1 + 4)
                act.wait_ge(qlow_ok.sem, qlow_ok.at(r))
                nc.scalar.activation(q_low[:], q_low[:], ACT.Exp).then_inc(act_a.sem, 1)
                act.wait_ge(act_a.sem, act_a.at(r, 2))
                nc.scalar.activation(q_low[:], q_low[:], ACT.Ln, bias=1.0)
                lat = pa[:, 0:2, :].rearrange("p t (h f) -> p t h f", f=FN)[:, :, :, ROPE:FN]
                nc.scalar.activation(q_near_t[:, :, :, ROPE:FN], lat, ACT.Copy)
                nc.scalar.activation(q_far_t[:, :, :, 2 * ROPE:FE], lat, ACT.Copy).then_inc(qlog_ok.sem, 1)
                yield from idle(3)
                for n in range(8):
                    k, t, half = n // 4, n // 2 % 2, n % 2
                    act.wait_ge(qT0_ps.sem, qT0_ps.at(r, n + 1))
                    dst, rows = ((q_near, FN), (q_far, FE))[k]
                    nc.scalar.activation(
                        dst[:, t * NU // 2:(t + 1) * NU // 2, :].rearrange("f u (c h q) -> f (u c) h q", c=4, h=H0)
                        [:, :, 4 * half:4 * half + 4, :],
                        pa[0:rows, n % 4, :].rearrange("f (h a q) -> f a h q", h=4, q=4), ACT.Copy)\
                        .then_inc(qT0_ok.sem, 1)
                    if n % 4 == 3:
                        yield
                yield

            def a_exp(r, u):
                act.wait_ge(sc_ok.sem, sc_ok.at(r, u + 1))
                if u > 1:
                    act.wait_ge(pt_ps.sem, pt_ps.at(r, u - 1))
                nc.scalar.activation(probs[:, u % 2], sc[:, u % 2], ACT.Exp, bias=neg_top[:, u % 2:u % 2 + 1], scale=SCALE0,
                                     accum_out=total[:, u % 2:u % 2 + 1]).then_inc(pr_e.sem, 1)

            def a_probsT(r, u):
                act.wait_ge(pt_ps.sem, pt_ps.at(r, u + 1))
                if u > 1:
                    act.wait_ge(o_ps.sem, o_ps.at(r, u - 1))
                nc.scalar.activation(probsT[:, u % 2].rearrange("p k n -> p (k n)"), pa[:, 2, 0:3 * P],
                                     ACT.Copy).then_inc(pt_ok.sem, 1)

            def a_out(r, k):
                act.wait_ge(o_ps.sem, o_ps.at(r, 4 * k + 4))
                for h in range(4):
                    last = nc.scalar.activation(
                        headsT[h * LAT:(h + 1) * LAT, :, 4 * UQ * k:4 * UQ * (k + 1)].rearrange("l a (n q) -> l a n q", q=4),
                        pa[0:LAT, 3, :].rearrange("l (n a h q) -> l h a n q", a=H0 // 4, h=4, q=4)[:, h], ACT.Copy)
                last.then_inc(o_ok.sem, 1)

            def ffn0(r):
                act.wait_ge(r_ps.sem, r_ps.at(r))
                nc.scalar.activation(xbT[:], pb[:, 0, 0:S], ACT.Copy).then_inc(xbT_ok.sem, 1)
                yield
                act.wait_ge(sh_ok.sem, sh_ok.at(r))
                nc.scalar.activation(egate[:, 1], egate[:, 0], ACT.Exp).then_inc(eg_ok.sem, 1)
                yield
                for k in range(NBLK // 2):
                    act.wait_ge(up_ps.sem, up_ps.at(r, k + 1))
                    if k >= 2:
                        act.wait_ge(hid_ok.sem, hid_ok.at(r, k - 1))
                    nc.scalar.activation(th[:, k % 2], pb[0:BLK, 2 * (k % 2):2 * (k % 2) + 2, 0:S], ACT.Tanh,
                                         scale=0.5).then_inc(th_ok.sem, 1)
                    yield
                yield from idle(6)

            def attention1(r, a):
                act.wait_ge(tx_ps.sem, tx_ps.at(r, a + 1))
                nc.scalar.activation(xbT[:], pb[:, 0, 0:S], ACT.Copy).then_inc(tx_ok.sem, 1)
                yield
                act.wait_ge(pj_ps.sem, pj_ps.at(r, a + 1))
                act.wait_ge(rs_ok.sem, rs_ok.at(r, a + 1))
                for t in range(NT):
                    last = nc.scalar.activation(pj[:, t, :], pb[:, 1 + t, 0:NPJ], ACT.Copy, scale=rsx[:, t:t + 1])
                last.then_inc(pj_ok.sem, 1)
                yield
                act.wait_ge(mh_ok.sem, mh_ok.at(r, a + 1))
                nc.scalar.activation(rsh[:].rearrange("p t h -> p (t h)"), ssh[:].rearrange("p t h -> p (t h)"), ACT.Ln,
                                     bias=eps[:], scale=1.0 / HD).then_inc(act_b.sem, 1)
                act.wait_ge(act_b.sem, act_b.at(r, a + 1))
                nc.scalar.activation(rsh[:].rearrange("p t h -> p (t h)"), rsh[:].rearrange("p t h -> p (t h)"), ACT.Exp,
                                     scale=-0.5).then_inc(rh_ok.sem, 1)
                yield
                act.wait_ge(p0_ok.sem, p0_ok.at(r, a + 1))
                for t in range(NT):
                    spread_queries(lambda o, i: nc.scalar.activation(o, i, ACT.Copy), 0, t)
                spread_keys(lambda o, i: nc.scalar.activation(o, i, ACT.Copy), 0).then_inc(spread_ok.sem, 1)
                yield
                act.wait_ge(qkT_ps.sem, qkT_ps.at(r, 2 * a + 1))
                nc.scalar.activation(kT[:].rearrange("p n s -> p (n s)"), pb[:, 3, :], ACT.Copy)
                nc.scalar.activation(qT[:, 1, :, 0:P], pb[:, 1, :].rearrange("p (h q) -> p h q", h=GH), ACT.Copy)
                yield
                act.wait_ge(qkT_ps.sem, qkT_ps.at(r, 2 * a + 2))
                nc.scalar.activation(qT[:, 1, :, P:S], pb[:, 0, :].rearrange("p (h q) -> p h q", h=GH),
                                     ACT.Copy).then_inc(kT_ok.sem, 1)
                yield
                if a == 1:
                    act.wait_ge(seam_ps.sem, seam_ps.at(r))
                    nc.scalar.activation(prs[P - WIN1:P].rearrange("p (g h) q -> p g (h q)", g=KV),
                                         pb[P - WIN1:P, :, 0:GH * WIN1], ACT.Exp,
                                         scale=SCALE1).then_inc(seam_e.sem, 1)
                    yield
                def exps(i):
                    for i in range(i, min(i + 2, len(blocks(a)))):
                        act.wait_ge(s_ps.sem, s_ps.at(r, first(a) + i + 1))
                        nc.scalar.activation(pr[:, i % 3, :], pb[:, i % 2, :], ACT.Exp, scale=SCALE1)\
                            .then_inc(e_ok.sem, 1)

                exps(0)
                yield
                for i in range(0, len(blocks(a)), 2):
                    exps(i + 2)
                    if i + 2 == len(blocks(a)):
                        act.wait_ge(pv_ps.sem, pv_ps.at(r, first(a + 1)))
                        nc.scalar.activation(oT(0), pb[:, 2, :], ACT.Copy).then_inc(o0_ok.sem, 1)
                    yield
                yield
                act.wait_ge(aT_ps.sem, aT_ps.at(r, a + 1))
                nc.scalar.activation(attT[:], pb[:, 3, 0:S], ACT.Copy).then_inc(aT_ok.sem, 1)
                yield from idle(2 + a)

            def ffn1(r):
                act.wait_ge(t4_ps.sem, t4_ps.at(r))
                nc.scalar.activation(xbT[:], pb[:, 0, 0:S], ACT.Copy).then_inc(t4_ok.sem, 1)
                yield
                act.wait_ge(f_ps.sem, f_ps.at(r))
                nc.scalar.activation(e01[:, 0], pb[:, 2:4, 0:2 * D], ACT.Tanh, scale=0.5).then_inc(fth_ok.sem, 1)
                yield
                act.wait_ge(fsh_ok.sem, fsh_ok.at(r))
                nc.scalar.activation(egate[:, 1], egate[:, 0], ACT.Exp).then_inc(feg_ok.sem, 1)
                yield from idle(3)

            def front(r):
                yield from a_front(r)
                for u in range(NU + 2):
                    if u > 1 and u % 4 == 1:
                        a_out(r, u // 4 - 1)
                    yield
                    if 0 < u <= NU:
                        a_probsT(r, u - 1)
                    if u < NU:
                        a_exp(r, u)
                    if u <= NU:
                        yield
                yield
                yield

            def back(r):
                yield from ffn0(r)
                yield from attention1(r, 0)
                yield from attention1(r, 1)
                yield from ffn1(r)

            pipeline(nc.scalar, front, back)

        @block.vector
        def _(dve):
            V = nc.vector
            dve.wait_ge(loaded, ALL)
            V.memset(ones_row[:], 1.0)
            V.memset(eps[:], 1e-6)
            V.memset(q_terms[:], 0.0)
            V.memset(k_terms[:], 0.0)
            V.tensor_copy(ident_b[:], ident)
            for a, name in enumerate(("causal", "local")):
                V.tensor_scalar(hide[:, a, :], c(name), 30000.0, -30000.0, ALU.mult, ALU.add)
            V.memset(v1[:], 0.0).then_inc(ready, 1)
            dve.wait_ge(ready, 1)
            V.memset(v1[:, :, :, HD:HD + 1], 1.0)
            V.memset(rank_turn[2 * ROPE:FE, :], 1.0)
            dve.wait_ge(derived_pe, 1)
            V.tensor_copy(w_up3[:, :, ROPE:FN], pa[0:CQ, 0, 0:H0 * LAT].rearrange("q (h l) -> q h l", h=H0))
            for h in range(4):
                V.tensor_copy(wvo[h * LAT:(h + 1) * LAT], pa[0:LAT, 2:4, h * D:(h + 1) * D])
            kk = KV * HD
            V.tensor_copy(wpj[:, 0, H1 * HD:NQK], pb[:, 0, 0:kk])
            V.tensor_copy(wpj[:, 0, NQK + H1 * HD:2 * NQK], pb[:, 0, kk:2 * kk])
            V.tensor_copy(wpj[:, 0, 2 * NQK:NPJ], pb[:, 0, 2 * kk:3 * kk]).then_inc(ready, 1)
            dve.wait_ge(ready, 2)
            for a in range(2):
                V.tensor_scalar(wpj[:, a, :], wpj[:, a, :], norm_w[:, a:a + 1], None, ALU.mult)
            dve.wait_ge(derived_act, 2)
            V.tensor_tensor(dlt[:, 3:4], dlt[:, 2:3], dlt[:, 2:3], ALU.mult).then_inc(ready, 1)
            dve.wait_ge(ready, 3)
            V.tensor_scalar(dlt[:, 4:5], dlt[:, 3:4], 2.0, -1.0, ALU.mult, ALU.add).then_inc(ready, 1)
            dve.wait_ge(ready, 4)
            V.tensor_scalar(turn[:], turn_v, dlt[:, 1:2], None, ALU.mult).then_inc(ready, 1)
            dve.wait_ge(ready, 5)
            V.scalar_tensor_tensor(turn[:], turn_u, dlt[:, 4:5], turn[:], ALU.mult, ALU.add).then_inc(ready, 1)
            dve.wait_ge(ready, 6)
            V.tensor_copy(rank_turn[0:2 * ROPE, :], turn[:, 2 * S:2 * S + NR]).then_inc(derived_dve, 1)
            dve.wait_ge(derived_pe, 2)
            V.tensor_copy(wq3[:].rearrange("d h f -> d (h f)"), pb[:, 1, :])
            V.tensor_copy(turns_t[:].rearrange("p k t f -> p (k t f)"), pb[:, 3, 0:2 * NT * 2 * ROPE]).then_inc(derived_dve, 1)
            dve.wait_ge(derived_dve, 2)

            def chained(r, chain, count):
                def link(ins):
                    count[0] += 1
                    ins.then_inc(chain.sem, 1)
                    dve.wait_ge(chain.sem, chain.at(r, count[0]))
                return link

            def layer_norm(link, r, k, src, dst, var, rs, done):
                for t in range(NT):
                    last = V.bn_stats(st6[:, k, t, :], src[:, t, :])
                link(last)
                plain(dve)
                for t in range(NT):
                    last = V.bn_aggr(mv[:, k, t, :], st6[:, k, t, :])
                link(last)
                V.tensor_scalar(var_e[:, k], mv[:, k, :, 1], 1e-5, None, ALU.add).then_inc(var.sem, 1)
                yield
                dve.wait_ge(rs.sem, rs.at(r))
                for t in range(NT):
                    last = V.tensor_scalar(dst[:, t, :], src[:, t, :], mv[:, k, t, 0:1], rstd[:, k, t:t + 1],
                                           ALU.subtract, ALU.mult)
                last.then_inc(done.sem, 1)

            def a_front(r, link):
                dve.wait_ge(x_ok.sem, x_ok.at(r))
                V.tensor_copy(xa[:], x_next[:]).then_inc(x_in.sem, 1)
                yield
                yield
                dve.wait_ge(key_ps.sem, key_ps.at(r))
                kp = pa[:, 3, 0:NT * FE].rearrange("p (t f) -> p t f", t=NT)
                V.tensor_copy(k_feat[:, :, 2 * ROPE:FE], kp[:, :, 2 * ROPE:FE]).then_inc(klat_ok.sem, 1)
                V.tensor_scalar(k_low[:], kp[:, :, 0:2 * ROPE], 40.0, None, ALU.min).then_inc(klow_ok.sem, 1)
                yield
                dve.wait_ge(klog_ok.sem, klog_ok.at(r))
                link(V.tensor_tensor(k_feat[:, :, 0:2 * ROPE], k_log[:], kp[:, :, 0:2 * ROPE], ALU.max))
                link(V.tensor_tensor(k_mul[:], k_feat[:, :, 0:2 * ROPE], turns_t[:, 1], ALU.mult))
                V.tensor_tensor(k_rot[:, :, 0:ROPE], k_mul[:, :, 0:ROPE], k_mul[:, :, ROPE:2 * ROPE], ALU.add)
                dve.wait_ge(klat_ok.sem, klat_ok.at(r))
                V.tensor_copy(k_rot[:, :, ROPE:FN], k_feat[:, :, 2 * ROPE:FE]).then_inc(krot_ok.sem, 1)
                yield
                link(V.tensor_copy(k_split[:, 0], k_feat[:]))
                link(V.tensor_tensor(k_rest[:, 0], k_feat[:], k_split[:, 0], ALU.subtract))
                link(V.tensor_copy(k_split[:, 1], k_rest[:, 0]))
                link(V.tensor_tensor(k_rest[:, 1], k_rest[:, 0], k_split[:, 1], ALU.subtract))
                V.tensor_copy(k_split[:, 2], k_rest[:, 1]).then_inc(ksplit_ok.sem, 1)
                yield
                for t, n in ((0, J0), (1, J1)):
                    dve.wait_ge(relu_ok.sem, relu_ok.at(r, t + 1))
                    for h in range(NI):
                        before = c(f"mask_rank{t}") if h == 0 else rank_in[:, t, 0:n]
                        ins = V.scalar_tensor_tensor(rank_in[:, t, 0:n], relu_i[:, h % 2, h // 2, 0:n],
                                                     idx_w[:, h:h + 1], before, ALU.mult, ALU.add)
                        if h < NI - 1:
                            link(ins)
                    ins.then_inc(rin_ok.sem, 1)
                    yield
                    dve.wait_ge(rin_ok.sem, rin_ok.at(r, t + 1))
                    for k in range(NR // 8):
                        plain(dve)
                        link(V.max(top[:, 8 * k:8 * k + 8], rank_in[:, t, 0:n]))
                        plain(dve)
                        link(V.max_index(idx_u[:, t, 8 * k:8 * k + 8], top[:, 8 * k:8 * k + 8], rank_in[:, t, 0:n]))
                        if k < NR // 8 - 1:
                            plain(dve)
                            link(V.match_replace(rank_in[:, t, 0:n], top[:, 8 * k:8 * k + 8], rank_in[:, t, 0:n], GONE))
                            yield
                    if t == 0:
                        yield
                V.tensor_copy(idx_b[:], idx_u[:]).then_inc(ib_ok.sem, 1)
                yield
                dve.wait_ge(q_ps.sem, q_ps.at(r))
                qp = pa[:, 0:2, :].rearrange("p t (h f) -> p t h f", f=FN)[:, :, :, 0:ROPE]
                V.tensor_scalar(q_low[:], qp, 40.0, None, ALU.min).then_inc(qlow_ok.sem, 1)
                yield
                dve.wait_ge(qlog_ok.sem, qlog_ok.at(r))
                V.tensor_tensor(q_low[:], q_low[:], qp, ALU.max).then_inc(qsoft_ok.sem, 1)
                dve.wait_ge(qsoft_ok.sem, qsoft_ok.at(r))
                link(turn_queries(V, q_turn, 0))
                yield
                V.tensor_tensor(q_near_t[:, :, :, 0:ROPE], q_turn[:, 0], q_turn[:, 1], ALU.add).then_inc(qn_ok.sem, 1)
                yield
                yield
                yield
                dve.wait_ge(ir_ok.sem, ir_ok.at(r))
                V.tensor_scalar(idx_rows[0:J0, 0, :], idx_rows[0:J0, 0, :], c("iota", J0)[:, 0:1], None,
                                ALU.is_equal).then_inc(hot_ok.sem, 1)
                link(V.tensor_scalar(hot_low[:], idx_rows[:, 1, :], c("iota")[:, 0:1], None, ALU.is_equal))
                V.tensor_scalar(idx_rows[0:J1 - P, 1, :], idx_rows[0:J1 - P, 1, :], c("iota", J1 - P)[:, 1:2], None,
                                ALU.is_equal).then_inc(hot_ok.sem, 1)
                yield

            def a_got(r, u):
                dve.wait_ge(got_ps.sem, got_ps.at(r, u + 1))
                if u > 1:
                    dve.wait_ge(pt_ps.sem, pt_ps.at(r, u - 1))
                V.tensor_tensor(got[:, u % 2].rearrange("f k (q n) -> f (k q) n", n=NR),
                                pa[0:FE, 0, :].rearrange("f (q n) -> f q n", n=NR),
                                rank_turn[:, None, :].broadcast_to([FE, UQ, NR]), ALU.mult).then_inc(got_ok.sem, 1)

            def a_max(r, u, link):
                dve.wait_ge(sc_ps.sem, sc_ps.at(r, u + 1))
                if u > 1:
                    dve.wait_ge(pr_e.sem, pr_e.at(r, u - 1))
                plain(dve)
                link(V.tensor_tensor_reduce(out=sc[:, u % 2], in0=pa[:, 1, 0:AW + BW],
                                            in1=c("mask_first" if UQ * u < WIN0 else "mask_later"),
                                            scale=1.0, scalar=-3e38, op0=ALU.add, op1=ALU.max, accum_out=top_s[:]))
                V.tensor_scalar(neg_top[:, u % 2:u % 2 + 1], top_s[:], -SCALE0, None, ALU.mult).then_inc(sc_ok.sem, 1)

            def a_norm(r, u, link):
                dve.wait_ge(pr_e.sem, pr_e.at(r, u + 1))
                link(V.reciprocal(inv_total[:], total[:, u % 2:u % 2 + 1]))
                V.tensor_scalar(probs[:, u % 2], probs[:, u % 2], inv_total[:], None, ALU.mult).then_inc(pr_ok.sem, 1)

            def a_back(r, link):
                dve.wait_ge(y_ps.sem, y_ps.at(r))
                link(V.tensor_tensor(pre[:].rearrange("p t d -> p (t d)"), pa[:, 0, 0:S],
                                     xa[:].rearrange("p t d -> p (t d)"), ALU.add))
                yield from layer_norm(link, r, 0, pre, x1, a_var, a_rstd, x1_ok)

            def row_softmax_in(link, r, ps, done):
                link(V.tensor_copy(lg[:].rearrange("p t e -> p (t e)"), ps))
                link(V.reduce_max(small[:, 0, :], lg[:], axis=AX.X))
                V.tensor_tensor(egate[:, 0], lg[:], small[:, 0, :].unsqueeze(2).broadcast_to([P, NT, E]),
                                ALU.subtract).then_inc(done.sem, 1)

            def ffn0(r, link):
                yield
                dve.wait_ge(lg_ps.sem, lg_ps.at(r))
                row_softmax_in(link, r, pb[:, 3, 0:NT * E], sh_ok)
                for t in range(NT):
                    them = lg[:, t, None, :].broadcast_to([P, E, E])
                    me = lg[:, t, :].unsqueeze(2).broadcast_to([P, E, E])
                    V.tensor_tensor(gt[:, t], them, me, ALU.is_gt)
                    last = V.tensor_tensor(eq[:, t], them, me, ALU.is_equal)
                link(last)
                for t in range(NT):
                    last = V.tensor_tensor(eq[:, t], eq[:, t], c("before").rearrange("p (a b) -> p a b", a=E), ALU.mult)
                link(last)
                link(V.tensor_tensor(gt[:], gt[:], eq[:], ALU.add))
                link(V.reduce_sum(rank[:, 0], gt[:], axis=AX.X))
                dve.wait_ge(eg_ok.sem, eg_ok.at(r))
                link(V.scalar_tensor_tensor(rank[:, 1].rearrange("p t e -> p (t e)"),
                                            rank[:, 0].rearrange("p t e -> p (t e)"), 2.0,
                                            egate[:, 1].rearrange("p t e -> p (t e)"), ALU.is_lt, ALU.mult))
                link(V.reduce_sum(small[:, 1, :], rank[:, 1], axis=AX.X))
                link(V.reciprocal(small[:, 2, :], small[:, 1, :]))
                link(V.tensor_tensor(rank[:, 2], rank[:, 1], small[:, 2, :].unsqueeze(2).broadcast_to([P, NT, E]),
                                     ALU.mult))
                yield
                for k in range(NBLK // 2):
                    dve.wait_ge(th_ok.sem, th_ok.at(r, k + 1))
                    ps = pb[0:BLK, 2 * (k % 2):2 * (k % 2) + 2, :]
                    link(V.scalar_tensor_tensor(th[:, k % 2], th[:, k % 2], 1.0, ps[:, :, 0:S], ALU.add, ALU.mult))
                    V.scalar_tensor_tensor(hid[0:BLK, 2 * k:2 * k + 2, :], th[:, k % 2], 0.5, ps[:, :, S:2 * S],
                                           ALU.mult, ALU.mult).then_inc(hid_ok.sem, 1)
                    yield
                dve.wait_ge(dn_ps.sem, dn_ps.at(r, 1))
                ins = V.tensor_tensor(preb[:].rearrange("p t d -> p (t d)"), pb[:, 2, 0:S],
                                      x1[:].rearrange("p t d -> p (t d)"), ALU.add)
                ins.then_inc(dn_ok.sem, 1)
                dve.wait_ge(dn_ok.sem, dn_ok.at(r, 1))
                yield
                for t in range(NT):
                    for half in range(2):
                        n = 2 * t + half
                        dve.wait_ge(dn_ps.sem, dn_ps.at(r, n + 2))
                        for e in range(4):
                            ins = V.scalar_tensor_tensor(preb[:, t, :], pb[:, (0, 1, 3, 0)[n], e * D:(e + 1) * D],
                                                         rank[:, 2, t, 4 * half + e:4 * half + e + 1], preb[:, t, :],
                                                         ALU.mult, ALU.add)
                            if e < 3:
                                link(ins)
                        ins.then_inc(dn_ok.sem, 1)
                        dve.wait_ge(dn_ok.sem, dn_ok.at(r, n + 2))
                        if n < 3:
                            yield
                yield from layer_norm(link, r, 1, preb, x2, b_var, b_rstd, x2_ok)
                yield

            def attention1(r, a, link):
                src = x2 if a == 0 else x3[:, 0]
                if a == 0:
                    dve.wait_ge(x2_ok.sem, x2_ok.at(r))
                else:
                    dve.wait_ge(x3_ok.sem, x3_ok.at(r, 1))
                for t in range(NT):
                    last = V.tensor_tensor_reduce(out=att[:, t, :], in0=src[:, t, :], in1=src[:, t, :], scale=1.0,
                                                  scalar=0.0, op0=ALU.mult, op1=ALU.add, accum_out=ssx[:, t:t + 1])
                link(last)
                V.tensor_scalar(msx[:], ssx[:], 1.0 / D, 1e-6, ALU.mult, ALU.add).then_inc(ms_ok.sem, 1)
                yield
                dve.wait_ge(pj_ok.sem, pj_ok.at(r, a + 1))
                link(V.tensor_tensor(ro[:, 0], pj[:, :, 0:NQK], pj[:, :, 0:NQK], ALU.mult))
                V.reduce_sum(ssh[:], ro[:, 0].rearrange("p t (h d) -> p t h d", d=HD), axis=AX.X).then_inc(mh_ok.sem, 1)
                dve.wait_ge(mh_ok.sem, mh_ok.at(r, a + 1))
                V.tensor_copy(v1[:, :, :, 0:HD], pj[:, :, 2 * NQK:NPJ].rearrange("p t (g d) -> p t g d", d=HD))
                cos, sin = (c(n + "_" + "gl"[a]).rearrange("p (t d) -> p t d", t=NT) for n in ("cos", "sin"))
                for k, tab in enumerate((cos, sin)):
                    last = V.tensor_tensor(ro[:, k].rearrange("p t (h d) -> p t h d", d=HD),
                                           pj[:, :, k * NQK:(k + 1) * NQK].rearrange("p t (h d) -> p t h d", d=HD),
                                           tab.unsqueeze(2).broadcast_to([P, NT, H1 + KV, HD]), ALU.mult)
                link(last)
                link(V.tensor_tensor(ro[:, 0], ro[:, 0], ro[:, 1], ALU.add))
                yield
                dve.wait_ge(rh_ok.sem, rh_ok.at(r, a + 1))
                rot = ro[:, 0].rearrange("p t (h d) -> p t h d", d=HD)
                link(V.tensor_tensor(rot, rot, rsh[:].unsqueeze(3).broadcast_to([P, NT, H1 + KV, HD]), ALU.mult))
                V.tensor_copy(parts[:, 0], ro[:, 0]).then_inc(p0_ok.sem, 1)
                dve.wait_ge(p0_ok.sem, p0_ok.at(r, a + 1))
                link(V.tensor_tensor(ro[:, 0], ro[:, 0], parts[:, 0], ALU.subtract))
                link(V.tensor_copy(parts[:, 1], ro[:, 0]))
                yield
                link(V.tensor_tensor(ro[:, 0], ro[:, 0], parts[:, 1], ALU.subtract))
                link(V.tensor_copy(parts[:, 2], ro[:, 0]))
                for n in (1, 2):
                    for t in range(NT):
                        spread_queries(V.tensor_copy, n, t)
                    last = spread_keys(V.tensor_copy, n)
                last.then_inc(qk_ok.sem, 1)
                yield
                dve.wait_ge(qkT_ps.sem, qkT_ps.at(r, 2 * a + 1))
                for t, bank in ((0, 0), (1, 2)):
                    V.tensor_copy(qT[:, 0, :, t * P:(t + 1) * P],
                                  pb[:, bank, :].rearrange("p (h q) -> p h q", h=GH)).then_inc(qb_ok.sem, 1)
                yield
                yield
                if a == 1:
                    dve.wait_ge(seam_e.sem, seam_e.at(r))
                    V.tensor_tensor(prs[P - WIN1:P], prs[P - WIN1:P],
                                    c("seam")[P - WIN1:P, None, :].broadcast_to([WIN1, H1, WIN1]),
                                    ALU.mult).then_inc(seam_ok.sem, 1)
                    yield
                yield
                yield from idle(len(blocks(a)) // 2 - 1)
                dve.wait_ge(pv_ps.sem, pv_ps.at(r, first(a + 1)))
                V.tensor_copy(oT(1), pb[:, 3, :]).then_inc(o1_ok.sem, 1)
                yield
                dve.wait_ge(ot_ps.sem, ot_ps.at(r, a + 1))
                o = pb[:, 0:NT, :].rearrange("p t (h g d) -> p (t h) g d", h=GH, g=KV)
                inv = inv_l[:].rearrange("p (n g) -> p n g", g=KV)
                link(V.reciprocal(inv, o[:, :, :, HD]))
                for t in range(NT):
                    last = V.tensor_tensor(att[:, t, :].rearrange("p (g h d) -> p h g d", g=KV, h=GH),
                                           o[:, t * GH:(t + 1) * GH, :, 0:HD],
                                           inv[:, t * GH:(t + 1) * GH, :].unsqueeze(3).broadcast_to([P, GH, KV, HD]),
                                           ALU.mult)
                last.then_inc(att_ok.sem, 1)
                yield
                yield
                dve.wait_ge(wo_ps.sem, wo_ps.at(r, a + 1))
                V.tensor_tensor(x3[:, a], pb[:, 2, 0:S].rearrange("p (t d) -> p t d", t=NT),
                                x2[:] if a == 0 else x3[:, 0], ALU.add).then_inc(x3_ok.sem, 1)
                dve.wait_ge(x3_ok.sem, x3_ok.at(r, a + 1))
                if a == 1:
                    link(V.tensor_tensor(x3[:, 1], x3[:, 1], x2[:], ALU.add))
                    yield from layer_norm(link, r, 1, x3[:, 1], x4, c_var, c_rstd, x4_ok)
                yield

            def ffn1(r, link):
                yield
                dve.wait_ge(x4_ok.sem, x4_ok.at(r))
                dve.wait_ge(f_ps.sem, f_ps.at(r))
                row_softmax_in(link, r, pb[:, 1, 0:NT * E], fsh_ok)
                yield
                dve.wait_ge(fth_ok.sem, fth_ok.at(r))
                link(V.scalar_tensor_tensor(e01[:, 0], e01[:, 0], 1.0, pb[:, 2:4, 0:2 * D], ALU.add, ALU.mult))
                dve.wait_ge(feg_ok.sem, feg_ok.at(r))
                link(V.reduce_sum(small[:, 1, :], egate[:, 1], axis=AX.X))
                link(V.reciprocal(small[:, 2, :], small[:, 1, :]))
                link(V.tensor_tensor(egate[:, 2], egate[:, 1], small[:, 2, :].unsqueeze(2).broadcast_to([P, NT, E]),
                                     ALU.mult))
                wt = egate[:, 2]
                link(V.reduce_max(small[:, 3, :], wt, axis=AX.X))
                link(V.tensor_tensor(small[:, 4, :], wt[:, :, 0], small[:, 3, :], ALU.is_ge))
                link(V.tensor_tensor(rank[:, 0], wt, wt[:, :, 1:2].broadcast_to([P, NT, E]), ALU.is_gt))
                link(V.reduce_sum(small[:, 5, :], rank[:, 0], axis=AX.X))
                link(V.tensor_tensor(small[:, 6, :], wt[:, :, 0], wt[:, :, 1], ALU.is_equal))
                link(V.tensor_tensor(small[:, 5, :], small[:, 5, :], small[:, 6, :], ALU.add))
                link(V.scalar_tensor_tensor(small[:, 4, :], small[:, 4, :], 0.5, wt[:, :, 0], ALU.mult, ALU.mult))
                link(V.tensor_scalar(small[:, 5, :], small[:, 5, :], 1.0, 0.5, ALU.is_equal, ALU.mult))
                link(V.tensor_tensor(small[:, 5, :], small[:, 5, :], wt[:, :, 1], ALU.mult))
                for k in range(2):
                    for t in range(NT):
                        ins = V.scalar_tensor_tensor(preb[:, t, :], e01[:, 0, t, k * D:(k + 1) * D],
                                                     small[:, 4 + k, t:t + 1], x4[:, t, :] if k == 0 else preb[:, t, :],
                                                     ALU.mult, ALU.add)
                    link(ins)
                yield
                dve.wait_ge(fin_free, r + 1)
                yield from layer_norm(link, r, 1, preb, fin, d_var, d_rstd, fin_ok)
                yield

            def front(r):
                count = [0]
                link = chained(r, chain_a, count)
                yield from a_front(r, link)
                for u in range(NU + 1):
                    if u > 0:
                        a_norm(r, u - 1, link)
                    if u < NU:
                        a_got(r, u)
                    yield
                    if u < NU:
                        a_max(r, u, link)
                    yield
                yield
                yield from a_back(r, link)
                yield
                assert count[0] == CHAIN_A, count[0]

            def back(r):
                count = [0]
                link = chained(r, chain_b, count)
                yield from ffn0(r, link)
                yield from attention1(r, 0, link)
                yield from attention1(r, 1, link)
                yield from ffn1(r, link)
                assert count[0] == CHAIN_B, count[0]

            pipeline(nc.vector, front, back)


BLOCKS = first(2)
CHAIN_A, CHAIN_B = 71, 76
FRONT_STEPS = 13 + 2 * (NR // 8 - 1) + 2
A_STEPS = FRONT_STEPS + 2 * (NU + 1) + 1 + 2
FFN_STEPS = 2 + NBLK // 2 + 6
ATT_STEPS = [6 + 1 + a + len(blocks(a)) // 2 + 3 + a for a in range(2)]
B_STEPS = FFN_STEPS + sum(ATT_STEPS) + 5
A_WEIGHTS = [1.65] * FRONT_STEPS + [1.0] * (A_STEPS - FRONT_STEPS)
B_WEIGHTS = [1.05] * FFN_STEPS + [1.0] * (B_STEPS - FFN_STEPS)
SCALE0 = float((DH0 + ROPE) ** -0.5)
SCALE1 = float(HD ** -0.5)


def kernel(**inputs):
    import concourse.bacc as _bacc
    from concourse import mybir as _mybir
    from concourse.bass_utils import run_bass_kernel_spmd as _run

    g = {k: np.asarray(v) for k, v in inputs.items()}
    half = ROPE // 2
    heads = lambda a, n: a.reshape(a.shape[0], n, -1)
    swap_half = lambda a: np.concatenate([a[..., half:], a[..., :half]], -1)
    swap_pair = lambda a: a.reshape(a.shape[0], -1, 2)[:, :, ::-1].reshape(a.shape[0], -1)
    qr = heads(g["L0_attn_W_qr"], H0)
    kr = g["L0_attn_W_kr"]
    up3 = np.concatenate([qr, np.zeros((CQ, H0, LAT), np.float32)], -1)
    ffn_in = lambda e, s: np.concatenate([g[e].transpose(1, 0, 2).reshape(D, E * HE), g[s]], 1).reshape(D, NBLK, BLK)
    w3 = np.concatenate([g["L0_ffn_W3"].reshape(E * HE, D), g["L0_ffn_Ws3"]]).reshape(NBLK, BLK, D).transpose(1, 0, 2)
    kk = np.zeros((D, KV * HD), np.float32)
    glob = np.concatenate([g["L1_attn_g_wq"], kk, swap_pair(g["L1_attn_g_wq"]), kk, kk], 1)
    loc = np.concatenate([g["L1_attn_l_wq"], g["L1_attn_l_wk"], swap_pair(g["L1_attn_l_wq"]),
                          swap_pair(g["L1_attn_l_wk"]), g["L1_attn_l_wv"]], 1)
    tables, where, turns = constants()
    arrays = {
        "x": g["L0_attn_x"], "consts": tables, "turns": turns,
        "w_dqT": g["L0_attn_W_dq"].T, "w_uqT": heads(g["L0_attn_W_uq"], H0).transpose(2, 1, 0),
        "w_ukT": heads(g["L0_attn_W_uk"], H0).transpose(2, 1, 0),
        "w_uvT": heads(g["L0_attn_W_uv"], H0).transpose(2, 1, 0),
        "w_out": g["L0_attn_W_out"].reshape(H0, DH0, D).transpose(1, 0, 2), "w_up3": up3,
        "w_key": np.concatenate([kr, swap_half(kr), g["L0_attn_W_dkv"]], 1),
        "idx_wq": g["L0_attn_idx_wq"], "idx_wk": g["L0_attn_idx_wk"], "idx_w": g["L0_attn_idx_w"],
        "raw_delta": g["L0_attn_raw_delta"], "wg": g["L0_ffn_Wg"],
        "w1": ffn_in("L0_ffn_W1", "L0_ffn_Ws1"), "w2": ffn_in("L0_ffn_W2", "L0_ffn_Ws2"), "w3": w3,
        "norm_w": np.stack([g["L1_attn_norm1_w"], g["L1_attn_norm2_w"]], 1), "wpj": np.stack([glob, loc], 1),
        "kv_downT": g["L1_attn_g_kv_down"].T,
        "kv_up": np.concatenate([g["L1_attn_g_k_up"], swap_pair(g["L1_attn_g_k_up"]), g["L1_attn_g_v_up"]], 1),
        "wo": np.stack([g["L1_attn_g_wo"], g["L1_attn_l_wo"]], 1), "gate_w": g["L1_ffn_gate_w"],
        "w01": np.concatenate([g["L1_ffn_w0"].T, g["L1_ffn_w1"].T], 1),
        "b01": np.concatenate([g["L1_ffn_b0"], g["L1_ffn_b1"]])[None],
    }
    arrays = {"in_" + k: np.ascontiguousarray(v) for k, v in arrays.items()}
    nc = _bacc.Bacc("TRN2", target_bir_lowering=False, num_devices=1)
    aps = {k[3:]: nc.dram_tensor(k, v.shape, _mybir.dt.from_np(v.dtype), kind="ExternalInput").ap()
           for k, v in arrays.items()}
    out = nc.dram_tensor("out", (NB, S, D), _mybir.dt.float32, kind="ExternalOutput").ap()
    layers(nc, aps["x"], aps["consts"], aps, out, where)
    r = _run(nc, [arrays], core_ids=[0])
    return r.results[0]["out"]
```
